# Optimizing a Trainium2 kernel written in Bass

```python
import numpy as np
import jax
import jax.numpy as jnp

def _softmax(x, axis=-1):
    return jax.nn.softmax(x, axis=axis)

def _gelu(x):
    return jax.nn.gelu(x, approximate=True)

def _silu(x):
    return jax.nn.silu(x)

def _sigmoid(x):
    return jax.nn.sigmoid(x)

def _layernorm(x, axis=-1, eps=1e-05):
    m = jnp.mean(x, axis=axis, keepdims=True)
    v = jnp.var(x, axis=axis, keepdims=True)
    return (x - m) / jnp.sqrt(v + eps)

def _scatter_add(tgt, idx, src, axis=0):
    return tgt.at[idx].add(src)

def _segment_sum(src, seg, n):
    return jax.ops.segment_sum(src, seg, n)
kernel_name = 'mk_decoder_preln_d1_seqx_r4_fbe79a'

def setup_inputs(seed: int=0):
    np.random.seed(seed)
    _w = jnp.asarray

    def _rec_inputs():
        import jax
        import jax.numpy as jnp
        _rk = jax.random.key(seed)
        x = 7.22e-05 + 1 * jax.random.normal(jax.random.fold_in(_rk, 1), (8, 256, 512), jnp.float32)
        _lenS = 256 - jax.random.randint(jax.random.fold_in(_rk, 7), (8,), 0, max(1, 256 // 4) + 1, jnp.int32)
        _lenS2 = 256 - jax.random.randint(jax.random.fold_in(_rk, 8), (8,), 0, max(1, 256 // 4) + 1, jnp.int32)
        _ctx_512P = jax.random.normal(jax.random.fold_in(_rk, 11), (8, 16, 128), jnp.float32)
        _ctx_512c = jax.random.dirichlet(jax.random.fold_in(_rk, 511), 0.3 * jnp.ones((16,), jnp.float32), (8, 256))
        _ctx_512t = jnp.einsum('bsk,bkd->bsd', _ctx_512c, _ctx_512P)
        _ctx_512t = _ctx_512t * jax.lax.rsqrt(jnp.mean(jnp.square(_ctx_512t)) + 1e-12) * 0.953939
        ctx_512 = -0.000514642 + 1.00011 * (_ctx_512t + 0.3 * jax.random.normal(jax.random.fold_in(_rk, 611), (8, 256, 128), jnp.float32))
        return (x, ctx_512)
    x, ctx_512 = _rec_inputs()

    def _L0_attn_setup():
        import jax, jax.numpy as jnp
        import numpy as np
        DIM = 512
        HID = 1024
        H = 64
        P = HID // H
        N = 128
        G = 1
        K = 4
        Q = 128
        CONV_DIM = HID + 2 * G * N
        D_IN = 2 * HID + 2 * G * N + H
        EPS = 1e-05

        def _causal_conv_silu(xBC, w):
            kern = w.T[:, None, :]
            y = jax.lax.conv_general_dilated(xBC, kern, window_strides=(1,), padding=[(K - 1, 0)], dimension_numbers=('NHC', 'HIO', 'NHC'), feature_group_count=xBC.shape[-1])
            return y * jax.nn.sigmoid(y)

        def _ssm(x, W_in, conv_w, dt_bias, A_log, D, norm_w, W_out):
            Bsz, L, _ = x.shape
            zxbcdt = x @ W_in.T
            z = zxbcdt[..., :HID]
            xBC = zxbcdt[..., HID:HID + CONV_DIM]
            dt_raw = zxbcdt[..., HID + CONV_DIM:]
            xBC = _causal_conv_silu(xBC, conv_w)
            xs = xBC[..., :HID].reshape(Bsz, L, H, P)
            rep = H // G
            Bh = jnp.repeat(xBC[..., HID:HID + G * N].reshape(Bsz, L, G, N), rep, axis=2)
            Ch = jnp.repeat(xBC[..., HID + G * N:].reshape(Bsz, L, G, N), rep, axis=2)
            dt = jax.nn.softplus(dt_raw + dt_bias)
            A = -jnp.exp(A_log)
            nc = L // Q
            a = (dt * A).reshape(Bsz, nc, Q, H)
            cum = jnp.cumsum(a, axis=2)
            xs_c = xs.reshape(Bsz, nc, Q, H, P)
            dtc = dt.reshape(Bsz, nc, Q, H)
            Bc = Bh.reshape(Bsz, nc, Q, H, N)
            Cc = Ch.reshape(Bsz, nc, Q, H, N)
            diff = cum[:, :, :, None, :] - cum[:, :, None, :, :]
            tril = jnp.tril(jnp.ones((Q, Q), bool))[None, None, :, :, None]
            Lmat = jnp.exp(jnp.where(tril, diff, -jnp.inf))
            CB = jnp.einsum('bcihn,bcjhn->bcijh', Cc, Bc)
            M = CB * Lmat * dtc[:, :, None, :, :]
            Yd = jnp.einsum('bcijh,bcjhp->bcihp', M, xs_c)
            wdec = jnp.exp(cum[:, :, -1:, :] - cum) * dtc
            states = jnp.einsum('bcqh,bcqhn,bcqhp->bchpn', wdec, Bc, xs_c)
            chunk_decay = jnp.exp(cum[:, :, -1, :])

            def step(S, inp):
                dec, st = inp
                return (S * dec[..., None, None] + st, S)
            S0 = jnp.zeros((Bsz, H, P, N), x.dtype)
            _, Sprev = jax.lax.scan(step, S0, (chunk_decay.transpose(1, 0, 2), states.transpose(1, 0, 2, 3, 4)))
            Sprev = Sprev.transpose(1, 0, 2, 3, 4)
            Yoff = jnp.einsum('bcqh,bcqhn,bchpn->bcqhp', jnp.exp(cum), Cc, Sprev)
            y = (Yd + Yoff).reshape(Bsz, L, H, P) + D[None, None, :, None] * xs
            y = y.reshape(Bsz, L, HID)
            yz = y * (z * jax.nn.sigmoid(z))
            yn = yz * jax.lax.rsqrt(jnp.mean(yz * yz, axis=-1, keepdims=True) + EPS) * norm_w
            return yn @ W_out.T
        key = jax.random.key(seed)
        k = jax.random.split(key, 6)
        return {'x': jax.random.normal(k[0], (2, 1024, DIM), jnp.float32), 'W_in': jax.random.normal(k[1], (D_IN, DIM), jnp.float32) * DIM ** (-0.5), 'conv_w': jax.random.normal(k[2], (CONV_DIM, K), jnp.float32) * K ** (-0.5), 'dt_bias': jax.random.uniform(k[3], (H,), jnp.float32, minval=0.001, maxval=0.1), 'A_log': jnp.log(jax.random.uniform(k[4], (H,), jnp.float32, minval=1.0, maxval=16.0)), 'D': jnp.ones((H,), jnp.float32), 'norm_w': jnp.ones((HID,), jnp.float32), 'W_out': jax.random.normal(k[5], (DIM, HID), jnp.float32) * HID ** (-0.5)}
    _L0_attn_all = _L0_attn_setup()
    _L0_attn_in = {k: v for k, v in _L0_attn_all.items() if k in ('W_in', 'conv_w', 'dt_bias', 'A_log', 'D', 'norm_w', 'W_out')}
    del _L0_attn_all

    def _L0_xattn_setup():
        import jax, jax.numpy as jnp
        import numpy as np
        B, S, E = (2, 512, 512)
        QH, KVH = (32, 8)
        D = E // QH
        G = QH // KVH
        DROPOUT = 1.0
        key = jax.random.key(seed)
        k1, k2, k3 = jax.random.split(key, 3)
        q = jax.random.normal(k1, (B, S, E), dtype=jnp.float32)
        k = jax.random.normal(k2, (B, S, E // G), dtype=jnp.float32)
        v = jax.random.normal(k3, (B, S, E // G), dtype=jnp.float32)
        return {'q': q, 'k': k, 'v': v}
    _L0_xattn_all = _L0_xattn_setup()
    _L0_xattn_in = {k: v for k, v in _L0_xattn_all.items() if k in ()}
    del _L0_xattn_all

    def _L0_ffn_setup():
        import jax, jax.numpy as jnp
        import numpy as np
        TOP_K = 2
        key = jax.random.key(seed)
        ks = jax.random.split(key, 4)
        G, S, F, E, H = (4, 512, 512, 8, 512)
        return {'x': jax.random.normal(ks[0], (G, S, F), dtype=jnp.float32), 'router_logits': jax.random.normal(ks[1], (F, E), dtype=jnp.float32) * 0.02, 'gating_einsum': jax.random.normal(ks[2], (E, 2, H, F), dtype=jnp.float32) * 0.02, 'linear': jax.random.normal(ks[3], (E, H, F), dtype=jnp.float32) * 0.02, 'per_expert_scale': jnp.ones((E,), dtype=jnp.float32), 'router_scale': jnp.ones((F,), dtype=jnp.float32)}
    _L0_ffn_all = _L0_ffn_setup()
    _L0_ffn_in = {k: v for k, v in _L0_ffn_all.items() if k in ('router_logits', 'gating_einsum', 'linear', 'per_expert_scale', 'router_scale')}
    del _L0_ffn_all
    return {'x': x, 'ctx_512': ctx_512, 'L0_attn_W_in': _L0_attn_in['W_in'], 'L0_attn_conv_w': _L0_attn_in['conv_w'], 'L0_attn_dt_bias': _L0_attn_in['dt_bias'], 'L0_attn_A_log': _L0_attn_in['A_log'], 'L0_attn_D': _L0_attn_in['D'], 'L0_attn_norm_w': _L0_attn_in['norm_w'], 'L0_attn_W_out': _L0_attn_in['W_out'], 'L0_ffn_router_logits': _L0_ffn_in['router_logits'], 'L0_ffn_gating_einsum': _L0_ffn_in['gating_einsum'], 'L0_ffn_linear': _L0_ffn_in['linear'], 'L0_ffn_per_expert_scale': _L0_ffn_in['per_expert_scale'], 'L0_ffn_router_scale': _L0_ffn_in['router_scale']}

def reference(x, ctx_512, L0_attn_W_in, L0_attn_conv_w, L0_attn_dt_bias, L0_attn_A_log, L0_attn_D, L0_attn_norm_w, L0_attn_W_out, L0_ffn_router_logits, L0_ffn_gating_einsum, L0_ffn_linear, L0_ffn_per_expert_scale, L0_ffn_router_scale):
    import jax
    import jax.numpy as jnp

    def _L0_attn_ref(x, W_in, conv_w, dt_bias, A_log, D, norm_w, W_out):
        import jax, jax.numpy as jnp
        import numpy as np
        DIM = 512
        HID = 1024
        H = 64
        P = HID // H
        N = 128
        G = 1
        K = 4
        Q = 128
        CONV_DIM = HID + 2 * G * N
        D_IN = 2 * HID + 2 * G * N + H
        EPS = 1e-05

        def _causal_conv_silu(xBC, w):
            kern = w.T[:, None, :]
            y = jax.lax.conv_general_dilated(xBC, kern, window_strides=(1,), padding=[(K - 1, 0)], dimension_numbers=('NHC', 'HIO', 'NHC'), feature_group_count=xBC.shape[-1])
            return y * jax.nn.sigmoid(y)

        def _ssm(x, W_in, conv_w, dt_bias, A_log, D, norm_w, W_out):
            Bsz, L, _ = x.shape
            zxbcdt = x @ W_in.T
            z = zxbcdt[..., :HID]
            xBC = zxbcdt[..., HID:HID + CONV_DIM]
            dt_raw = zxbcdt[..., HID + CONV_DIM:]
            xBC = _causal_conv_silu(xBC, conv_w)
            xs = xBC[..., :HID].reshape(Bsz, L, H, P)
            rep = H // G
            Bh = jnp.repeat(xBC[..., HID:HID + G * N].reshape(Bsz, L, G, N), rep, axis=2)
            Ch = jnp.repeat(xBC[..., HID + G * N:].reshape(Bsz, L, G, N), rep, axis=2)
            dt = jax.nn.softplus(dt_raw + dt_bias)
            A = -jnp.exp(A_log)
            nc = L // Q
            a = (dt * A).reshape(Bsz, nc, Q, H)
            cum = jnp.cumsum(a, axis=2)
            xs_c = xs.reshape(Bsz, nc, Q, H, P)
            dtc = dt.reshape(Bsz, nc, Q, H)
            Bc = Bh.reshape(Bsz, nc, Q, H, N)
            Cc = Ch.reshape(Bsz, nc, Q, H, N)
            diff = cum[:, :, :, None, :] - cum[:, :, None, :, :]
            tril = jnp.tril(jnp.ones((Q, Q), bool))[None, None, :, :, None]
            Lmat = jnp.exp(jnp.where(tril, diff, -jnp.inf))
            CB = jnp.einsum('bcihn,bcjhn->bcijh', Cc, Bc)
            M = CB * Lmat * dtc[:, :, None, :, :]
            Yd = jnp.einsum('bcijh,bcjhp->bcihp', M, xs_c)
            wdec = jnp.exp(cum[:, :, -1:, :] - cum) * dtc
            states = jnp.einsum('bcqh,bcqhn,bcqhp->bchpn', wdec, Bc, xs_c)
            chunk_decay = jnp.exp(cum[:, :, -1, :])

            def step(S, inp):
                dec, st = inp
                return (S * dec[..., None, None] + st, S)
            S0 = jnp.zeros((Bsz, H, P, N), x.dtype)
            _, Sprev = jax.lax.scan(step, S0, (chunk_decay.transpose(1, 0, 2), states.transpose(1, 0, 2, 3, 4)))
            Sprev = Sprev.transpose(1, 0, 2, 3, 4)
            Yoff = jnp.einsum('bcqh,bcqhn,bchpn->bcqhp', jnp.exp(cum), Cc, Sprev)
            y = (Yd + Yoff).reshape(Bsz, L, H, P) + D[None, None, :, None] * xs
            y = y.reshape(Bsz, L, HID)
            yz = y * (z * jax.nn.sigmoid(z))
            yn = yz * jax.lax.rsqrt(jnp.mean(yz * yz, axis=-1, keepdims=True) + EPS) * norm_w
            return yn @ W_out.T
        return _ssm(x, W_in, conv_w, dt_bias, A_log, D, norm_w, W_out)

    def _L0_xattn_ref(q, k, v):
        import jax, jax.numpy as jnp
        import numpy as np
        B, S, E = (2, 512, 512)
        QH, KVH = (32, 8)
        D = E // QH
        G = QH // KVH
        DROPOUT = 1.0
        b, s, _ = q.shape
        qh = q.reshape(b, s, KVH, G, D).transpose(0, 2, 3, 1, 4)
        kh = k.reshape(b, s, KVH, D).transpose(0, 2, 1, 3)
        vh = v.reshape(b, s, KVH, D).transpose(0, 2, 1, 3)
        scale = 1.0 / jnp.sqrt(jnp.float32(D))
        scores = jnp.einsum('bkgsd,bktd->bkgst', qh, kh) * scale
        attn = jax.nn.softmax(scores, axis=-1) / DROPOUT
        out = jnp.einsum('bkgst,bktd->bkgsd', attn, vh)
        return out.transpose(0, 3, 1, 2, 4).reshape(b, s, E)

    def _L0_ffn_ref(x, router_logits, gating_einsum, linear, per_expert_scale, router_scale):
        import jax, jax.numpy as jnp
        import numpy as np
        TOP_K = 2
        G, S, F = x.shape
        E = router_logits.shape[-1]
        H = linear.shape[1]
        k = TOP_K
        dtype = x.dtype
        var = jnp.mean(jnp.square(x.astype(jnp.float32)), axis=-1, keepdims=True)
        router_input = x * jax.lax.rsqrt(var + 1e-06).astype(dtype)
        root_size = jax.lax.rsqrt(jnp.array(F, dtype=dtype))
        router_input = router_input * root_size * router_scale.astype(dtype)
        logits = jnp.einsum('gsd,de->gse', router_input, router_logits.astype(dtype))
        logits32 = logits.astype(jnp.float32)
        probs = jax.nn.softmax(logits32, axis=-1)
        _, choices = jax.lax.approx_max_k(logits32, k=k)
        indicator = jax.nn.one_hot(choices, E, dtype=probs.dtype).sum(axis=-2)
        renorm = jnp.sum(indicator * probs, axis=-1, keepdims=True)
        renorm = jnp.where(renorm > 0.0, renorm, 1.0)
        weights = probs / renorm
        x_flat = x.reshape((-1, F))
        batch_size = G * S
        choices_flat = choices.ravel()
        xs_order = choices_flat.argsort()
        xs_reverse_argsort = xs_order.argsort()
        xs_indices = jnp.repeat(jnp.arange(batch_size), k)[xs_order]
        sorted_xs = x_flat[xs_indices, :]
        choices_oh = jax.nn.one_hot(choices, num_classes=E, dtype=jnp.int32)
        tokens_per_expert = jnp.sum(choices_oh, axis=(0, 1, 2))
        combine_weights = (choices_oh.astype(jnp.float32) * jnp.expand_dims(weights, axis=2)).sum(axis=-1).astype(weights.dtype)
        w_gate = jnp.transpose(gating_einsum, (0, 3, 1, 2)).reshape(E, F, 2 * H)
        gate_out = jax.lax.ragged_dot(sorted_xs, w_gate.astype(dtype), group_sizes=tokens_per_expert)
        gate_out = gate_out.reshape(gate_out.shape[0], 2, H)
        activation = jax.nn.gelu(gate_out[:, 0, :]) * gate_out[:, 1, :]
        expert_outputs = jax.lax.ragged_dot(activation, linear.astype(dtype), group_sizes=tokens_per_expert)
        expert_indices = jnp.repeat(jnp.arange(E), tokens_per_expert, total_repeat_length=expert_outputs.shape[0])
        expert_outputs = expert_outputs * per_expert_scale.astype(expert_outputs.dtype)[expert_indices, None]
        out = expert_outputs[xs_reverse_argsort].reshape((G, S, k, -1))
        out = jnp.einsum('blkd,blk->bld', out, combine_weights, preferred_element_type=out.dtype)
        return out
    x = x + _L0_attn_ref(_layernorm(x, axis=-1), L0_attn_W_in, L0_attn_conv_w, L0_attn_dt_bias, L0_attn_A_log, L0_attn_D, L0_attn_norm_w, L0_attn_W_out)
    x = x + _L0_xattn_ref(_layernorm(x, axis=-1), ctx_512, ctx_512)
    x = x + _L0_ffn_ref(_layernorm(x, axis=-1), L0_ffn_router_logits, L0_ffn_gating_einsum, L0_ffn_linear, L0_ffn_per_expert_scale, L0_ffn_router_scale)
    return x

_drawn_inputs = setup_inputs


def setup_inputs(seed=0):
    import zlib

    import numpy as np

    out = dict(_drawn_inputs(seed))
    spreads = {'L0_attn_D': (1.0, 0.2),
     'L0_attn_norm_w': (1.0, 0.2),
     'L0_ffn_per_expert_scale': (1.0, 0.6),
     'L0_ffn_router_scale': (1.0, 0.6)}
    factors = {'L0_attn_dt_bias': 5.565, 'L0_ffn_router_logits': 2.932}
    for name, (base, spread) in spreads.items():
        noise = np.random.default_rng([zlib.crc32(name.encode()), seed]).standard_normal(out[name].shape)
        drawn = base * np.exp(spread * noise) if base else spread * noise
        out[name] = jnp.asarray(drawn.astype(out[name].dtype))
    for name, factor in factors.items():
        out[name] = (out[name] * factor).astype(out[name].dtype)
    return out
```

```python
from contextlib import ExitStack

import concourse.bass as bass
import numpy as np
from concourse import mybir

F32 = mybir.dt.float32
BF16 = mybir.dt.bfloat16
F16 = mybir.dt.float16
ALU = mybir.AluOpType
ACT = mybir.ActivationFunctionType
AX = mybir.AxisListType

P = 128
NB, L, DIM = 8, 256, 512
TPB = L // P
NT = NB * TPB
KD = DIM // P
HID, NH, HP, NS = 1024, 64, 16, 128
CONV = HID + 2 * NS
NCZ, NCX = HID // P, CONV // P
TAPS = 4
HG = 4
NG = NH // HG
DROWS = 3 * (NG + HG)
QH, KVH, DH = 32, 8, 16
SLOT = 64
NE, EH = 8, 512
LN_EPS, RMS_EPS, ROUTER_EPS = 1e-5, 1e-5, 1e-6


class Engine:

    def __init__(self, name, sem):
        self.name, self.sem, self.count, self.queue, self.seen = name, sem, 0, [], {}

    def run(self, instruction):
        self.queue.append(instruction)

    def do(self, instruction):
        self.count += 1
        self.queue.append(lambda e: instruction(e).then_inc(self.sem, 1))
        return self.sem, self.count

    def wait(self, *marks):
        for mark in marks:
            if mark is None:
                continue
            sem, value = mark
            if self.seen.get(id(sem), 0) < value:
                self.seen[id(sem)] = value
                self.queue.append(lambda e, s=sem, v=value: e.wait_ge(s, v))


class Load:

    def __init__(self, sem):
        self.sem, self.count = sem, 0

    def start(self, eng, out, in_):
        self.count += 16
        eng.queue.append(lambda e: e.dma_start(out, in_).then_inc(self.sem, 16))
        return self.sem, self.count


class Ring:

    def __init__(self, buffers):
        self.buffers, self.at = buffers, 0
        self.free = [None] * len(buffers)

    def take(self, writer):
        n = self.at % len(self.buffers)
        self.at += 1
        writer.wait(self.free[n])
        return n, self.buffers[n]

    def release(self, n, mark):
        self.free[n] = mark


def alternate(*generators):
    live = [[g, w, 0.0] for g, w in generators]
    while live:
        live.sort(key=lambda x: x[2])
        item = live[0]
        try:
            next(item[0])
            item[2] += 1.0 / item[1]
        except StopIteration:
            live.remove(item)


def layer_kernel(nc, A, out):
    x_rows = A["x"].rearrange("b s d -> (b s) d").rearrange("(t p) d -> p t d", p=P)
    out_rows = out.rearrange("b s d -> (b s) d").rearrange("(t p) d -> p t d", p=P)
    ctx_rows = A["ctx_512"].rearrange("b s d -> (b s) d").rearrange("(t p) d -> p t d", p=P)

    with ExitStack() as top:
        semaphore = lambda name: top.enter_context(nc.semaphore(name))
        T = Engine("tensor", semaphore("tensor_done"))
        V = Engine("vector", semaphore("vector_done"))
        S = Engine("scalar", semaphore("scalar_done"))
        G = Engine("gpsimd", semaphore("gpsimd_done"))
        Y = Engine("sync", semaphore("sync_done"))
        engines = [T, V, S, G, Y]

        def sb(stack, name, shape, dt=F32):
            return stack.enter_context(nc.sbuf_tensor(name, shape, dt))

        def barrier():
            for e in engines:
                e.wait(*[(o.sem, o.count) for o in engines if o.count])

        x_sb = sb(top, "x_sb", [P, NT, DIM])
        ident = sb(top, "ident", [P, P])
        ident16 = sb(top, "ident16", [P, P], F16)
        load_const = Load(semaphore("load_const"))
        load_x = Load(semaphore("load_x"))
        x_ready = [load_x.start(Y, x_sb[:, :, :], x_rows)] * NT
        const_ready = load_const.start(S, ident[:, :], A["c_ident"])

        def rsqrt(v, y, tmp, ready, mark_y=None):
            S.wait(ready, mark_y)
            m = S.do(lambda e: e.activation(tmp, v, ACT.Ln))
            S.wait(m)
            m = S.do(lambda e: e.activation(y, tmp, ACT.Exp, scale=-0.5))
            V.wait(m)
            m = V.do(lambda e: e.tensor_tensor(tmp, v, y, ALU.mult))
            V.wait(m)
            m = V.do(lambda e: e.tensor_tensor(tmp, tmp, y, ALU.mult))
            V.wait(m)
            m = V.do(lambda e: e.tensor_scalar(tmp, tmp, -0.5, 1.5, ALU.mult, ALU.add))
            V.wait(m)
            return V.do(lambda e: e.tensor_tensor(y, y, tmp, ALU.mult))

        def layer_norm(tile, ready, xn, stats, writes_after):
            src = x_sb[:, tile, :]
            V.wait(ready)
            m = V.do(lambda e: e.bn_stats(stats[:, 0:6], src))
            V.wait(m)
            m = V.do(lambda e: e.bn_aggr(stats[:, 6:8], stats[:, 0:6]))
            V.wait(m)
            m = V.do(lambda e: e.tensor_scalar(stats[:, 7:8], stats[:, 7:8], LN_EPS, None, ALU.add))
            m = rsqrt(stats[:, 7:8], stats[:, 8:9], stats[:, 9:10], m)
            V.wait(m, writes_after)
            return V.do(lambda e: e.tensor_scalar(xn, src, stats[:, 6:7], stats[:, 8:9], ALU.subtract, ALU.mult))

        def ssm_mixer(st):
            bank = lambda name, shape=[P, 512], dt=F32: st.enter_context(nc.psum_tensor(name, shape, dt))
            proj_ps = Ring([bank("proj_ps0"), bank("proj_ps1")])
            decay_ps = Ring([bank("decay_ps0"), bank("decay_ps1")])
            y_ps = Ring([bank("y_ps0"), bank("y_ps1")])
            misc_ps = Ring([bank("misc_ps")])
            out_ps = Ring([bank("out_ps")])

            w_in = sb(st, "w_in", [P, KD, 2 * HID + 2 * NS + NH])
            w_out = sb(st, "w_out", [P, NCZ, DIM])
            conv_w = sb(st, "conv_w", [P, NCX, TAPS])
            norm_w = sb(st, "norm_w", [P, NCZ])
            d_w = sb(st, "d_w", [P, NCZ])
            head_w = sb(st, "head_w", [NH, 4])
            raw_in = Ring([sb(st, f"raw{i}", [P, 2, L + TAPS - 1]) for i in range(2)])
            causal = raw_in.buffers[0][:, 0, 0:P]
            identb = sb(st, "identb", [P, P], BF16)
            future = sb(st, "future", [P, P], BF16)
            expand = sb(st, "expand", [NH, NCZ, P])
            ones = sb(st, "ones", [P, 1])

            xn = [sb(st, "xn", [P, DIM])] * TPB
            stats = sb(st, "stats", [P, 16])
            xnT = sb(st, "xnT", [P, KD, L])
            conv_out = Ring([sb(st, f"conv{i}", [P, 2, L]) for i in range(2)])
            xbc = [sb(st, f"xbc{i}", [P, NCX, L]) for i in range(2)]
            zs = [sb(st, f"zs{i}", [P, NCZ, L]) for i in range(2)]
            select_f = xbc[0][0:64, 0:NCZ, :].rearrange("p c t -> p (c t)")
            head_sign = zs[0][0:64, 0:2, :].rearrange("p c t -> p (c t)")
            dtT = sb(st, "dtT", [NH, 7, L])
            wdecT = sb(st, "wdecT", [NH, P])
            cum3 = sb(st, "cum3", [NH, 3, TPB, P], BF16)
            rest = dtT[:, 3:5, :]
            dt_tokens = [sb(st, f"dt_tok{i}", [P, TPB, NH]) for i in range(2)]
            wdec_tokens = [sb(st, f"wdec_tok{i}", [P, NH]) for i in range(2)]
            ecums = [sb(st, f"ecum{i}", [NH, P]) for i in range(2)]
            LT = [sb(st, f"LT{i}", [64, TPB, NG, P], BF16) for i in range(2)]
            RT = [sb(st, f"RT{i}", [64, TPB, HG * P], BF16) for i in range(2)]
            b_tok = sb(st, "b_tok", [P, NS])
            cbm = [sb(st, f"cbm{i}", [P, P]) for i in range(2)]
            xdt = sb(st, "xdt", [P, NH, 2 * HP])
            xw = sb(st, "xw", [P, NH, HP])
            state = sb(st, "state", [P, HID])
            decay = Ring([sb(st, f"decay{i}", [P, HG * P]) for i in range(2)])
            mix = Ring([sb(st, f"mix{i}", [P, HG * P]) for i in range(3)])
            eexp = sb(st, "eexp", [P, 512])
            yoff = sb(st, "yoff", [P, 512])
            yz = sb(st, "yz", [P, NCZ, P])
            sq = xw[:, :, :].rearrange("p h w -> p (h w)").rearrange("p (c j) -> p c j", j=P)

            load_w = Load(semaphore("load_w"))
            scratch = [nc.dram_tensor(f"cum_scratch{i}", [3, NH, TPB, P], BF16).ap() for i in range(2)]
            store_cum = Load(semaphore("store_cum"))
            load_cum = Load(semaphore("load_cum"))

            for k in range(KD):
                w_ready = load_w.start(S, w_in[:, k, :], A["c_w_inT"][k * P:(k + 1) * P, :])
            for dst, src in [
                (conv_w[:, :, :], A["L0_attn_conv_w"].rearrange("(c p) k -> p c k", p=P)),
                (norm_w[:, :], A["c_norm_w"]),
                (d_w[:, :], A["c_D_channels"]),
                (head_w[:, 0:1], A["L0_attn_dt_bias"].rearrange("(h o) -> h o", o=1)),
                (head_w[:, 1:2], A["L0_attn_A_log"].rearrange("(h o) -> h o", o=1)),
                (causal, A["c_causal"]),
                (expand[:, :, :], A["c_expand"].rearrange("h (c p) -> h c p", p=P)),
                (select_f, A["c_select"]),
                (w_out[:, :, :], A["c_w_outT"].rearrange("(c p) d -> p c d", p=P)),
            ]:
                const_ready = load_const.start(Y, dst, src)
            const_ready = load_const.start(Y, head_sign, A["c_head_sign"])

            for e in (V, S, T, G):
                e.wait(const_ready)
            init = V.do(lambda e: e.memset(ones[:, :], 1.0))
            m = V.do(lambda e: e.tensor_scalar(future[:, :], causal, 1.0, 1e30, ALU.subtract, ALU.mult))
            V.wait(m)
            for i in range(2):
                V.do(lambda e, i=i: e.memset(raw_in.buffers[i][:, :, 0:TAPS - 1], 0.0))
            V.do(lambda e: e.memset(xdt[:, :, :], 0.0))
            V.do(lambda e: e.tensor_copy(ident16[:, :], ident[:, :]))
            V.do(lambda e: e.tensor_copy(identb[:, :], ident[:, :]))
            for i in range(2):
                for c in range(TPB):
                    V.do(lambda e, i=i, c=c: e.tensor_copy(LT[i][:, c, :, :], select_f.rearrange("p (g j) -> p g j", j=P)))
                    V.do(lambda e, i=i, c=c: e.tensor_copy(RT[i][:, c, :], head_sign))
            for c in range(NCZ):
                V.do(lambda e, c=c: e.tensor_scalar(w_out[:, c, :], w_out[:, c, :], norm_w[:, c:c + 1], None, ALU.mult))
            m = S.do(lambda e: e.activation(head_w[:, 2:3], head_w[:, 1:2], ACT.Exp))
            V.wait(m)
            init = V.do(lambda e: e.tensor_scalar(head_w[:, 3:4], head_w[:, 2:3], -1.0, None, ALU.mult))
            for e in (T, S, V, G, Y):
                e.wait(init)

            xbc_free, zs_free = [[None], [None]], [[None], [None]]
            cum_free = [None, None]
            made = {}
            once = dict(xn=None, xnT=None, dt=None, stats=None)

            def project(b):
                par = b % 2
                dt_tok, wdec_tok, ecum = dt_tokens[par], wdec_tokens[par], ecums[par]
                xnT_mark = []
                for t in range(TPB):
                    tile = b * TPB + t
                    xn_mark = layer_norm(tile, x_ready[tile], xn[t][:, :], stats, once["xn"])
                    n, ps = proj_ps.take(T)
                    T.wait(xn_mark)
                    for k in range(KD):
                        f = lambda e, k=k, t=t, ps=ps: e.transpose(ps[:, k * P:(k + 1) * P], xn[t][:, k * P:(k + 1) * P], ident[:, :])
                        T.run(f) if k < KD - 1 else None
                    m = T.do(f)
                    once["xn"] = m
                    S.wait(m, once["xnT"])
                    m = S.do(lambda e, t=t, ps=ps: e.activation(xnT[:, :, t * P:(t + 1) * P], ps[:, :].rearrange("p (k j) -> p k j", k=KD), ACT.Copy))
                    proj_ps.release(n, m)
                    xnT_mark.append(m)
                    yield
                T.wait(*xnT_mark)
                T.wait(w_ready)

                def channels(ps, at, col, width):
                    for k in range(KD):
                        f = lambda e, k=k: e.matmul(ps[0:width, at:at + L], w_in[:, k, col:col + width], xnT[:, k, :], start=(k == 0), stop=(k == KD - 1))
                        T.run(f) if k < KD - 1 else None
                    return T.do(f)

                n, ps = proj_ps.take(T)
                m = channels(ps, 0, HID + CONV, NH)
                S.wait(m, once["dt"])
                m = S.do(lambda e, ps=ps: e.activation(dtT[:, 0, :], ps[0:NH, 0:L], ACT.Identity, bias=head_w[:, 0:1]))
                proj_ps.release(n, m)
                S.wait(m)
                u_mark = m
                m = S.do(lambda e: e.activation(dtT[:, 1, :], dtT[:, 0, :], ACT.Abs))
                S.wait(m)
                e_mark = S.do(lambda e: e.activation(dtT[:, 2, :], dtT[:, 1, :], ACT.Exp, scale=-1.0))
                S.wait(e_mark)
                ln_mark = S.do(lambda e: e.activation(dtT[:, 3, :], dtT[:, 2, :], ACT.Ln, bias=1.0))
                yield
                V.wait(e_mark, u_mark)
                m = V.do(lambda e: e.tensor_scalar(dtT[:, 4, :], dtT[:, 2, :], 1.0, None, ALU.add))
                V.wait(m, ln_mark)
                m = V.do(lambda e: e.scalar_tensor_tensor(dtT[:, 1, :], dtT[:, 4, :], 1.0, dtT[:, 2, :], ALU.subtract, ALU.subtract))
                V.wait(m)
                m = V.do(lambda e: e.reciprocal(dtT[:, 4, :], dtT[:, 4, :]))
                V.wait(m)
                m = V.do(lambda e: e.scalar_tensor_tensor(dtT[:, 1, :], dtT[:, 1, :], -1.0, dtT[:, 4, :], ALU.mult, ALU.mult))
                V.wait(m)
                m = V.do(lambda e: e.tensor_tensor(dtT[:, 1, :], dtT[:, 1, :], dtT[:, 3, :], ALU.add))
                V.wait(m)
                dt_mark = V.do(lambda e: e.scalar_tensor_tensor(dtT[:, 5, :], dtT[:, 0, :], 0.0, dtT[:, 1, :], ALU.max, ALU.add))
                V.wait(dt_mark)
                m = V.do(lambda e: e.tensor_scalar(dtT[:, 1, :], dtT[:, 5, :], head_w[:, 3:4], None, ALU.mult))
                V.wait(m)
                for c in range(TPB):
                    m = V.do(lambda e, c=c: e.tensor_tensor_scan(dtT[:, 6, c * P:(c + 1) * P], ones[0:NH, 0:1].to_broadcast([NH, P]), dtT[:, 1, c * P:(c + 1) * P], 0.0, ALU.mult, ALU.add))
                cumT_mark = m
                V.wait(m, cum_free[0])
                for s in range(3):
                    src = dtT[:, 6, :] if s == 0 else rest[:, s - 1, :]
                    part = cum3[:, s, :, :].rearrange("h c j -> h (c j)")
                    m = V.do(lambda e, part=part, src=src: e.tensor_copy(part, src))
                    V.wait(m)
                    if s < 2:
                        m = V.do(lambda e, s=s, part=part, src=src: e.tensor_tensor(rest[:, s, :], src, part, ALU.subtract))
                        V.wait(m)
                Y.wait(m)
                m = store_cum.start(Y, scratch[par].rearrange("s h c j -> h s c j"), cum3[:, :, :, :])
                Y.wait(m, made.get(("decay_read", b - 2)))
                cum_free[0] = m
                for c in range(TPB):
                    m = load_cum.start(Y, RT[par][0:3 * NG, c, :].rearrange("p (h i) -> p h i", h=HG),
                                       scratch[par].rearrange("s (g h) c i -> (s g) c h i", h=HG)[:, c, :, :])
                    for s in range(3):
                        m = load_cum.start(Y, LT[par][3 * NG + HG * s:3 * NG + HG * (s + 1), c, :, :],
                                           scratch[par].rearrange("s (g h) c j -> s c h g j", h=HG)[s, c, :, :, :])
                Y.wait(m)
                made["decay_operands", b] = m
                S.wait(cumT_mark, once["wdec"] if "wdec" in once else None)
                m = S.do(lambda e: e.activation(wdecT[:, :], dtT[:, 6, 0:P], ACT.Exp, bias=dtT[:, 6, P - 1:P], scale=-1.0))
                V.wait(m)
                wdec_mark = V.do(lambda e: e.tensor_tensor(wdecT[:, :], wdecT[:, :], dtT[:, 5, 0:P], ALU.mult))
                S.wait(made.get(("ecum_read", b - 2)))
                m = S.do(lambda e: e.activation(ecum[:, :], dtT[:, 6, P:2 * P], ACT.Exp))
                made["ecum", b] = m
                n, ps = proj_ps.take(T)
                T.wait(dt_mark, wdec_mark)
                for c in range(TPB):
                    T.run(lambda e, c=c, ps=ps: e.transpose(ps[:, c * NH:(c + 1) * NH], dtT[:, 5, c * P:(c + 1) * P], ident[0:NH, 0:NH]))
                once["dt"] = m = T.do(lambda e, ps=ps: e.transpose(ps[:, TPB * NH:(TPB + 1) * NH], wdecT[:, :], ident[0:NH, 0:NH]))
                once["wdec"] = m
                S.wait(m, made.get(("dt_tok_read", b - 2)))
                S.do(lambda e, ps=ps: e.activation(dt_tok[:, :, :].rearrange("p c h -> p (c h)"), ps[:, 0:TPB * NH], ACT.Copy))
                m = S.do(lambda e, ps=ps: e.activation(wdec_tok[:, :], ps[:, TPB * NH:(TPB + 1) * NH], ACT.Copy))
                proj_ps.release(n, m)
                made["dt_tok", b] = m
                yield
                conv_marks = []
                for c0 in range(0, NCX, 2):
                    n, ps = proj_ps.take(T)
                    for c in (c0, c0 + 1):
                        m = channels(ps, (c - c0) * L, HID + c * P, P)
                    rn, raw = raw_in.take(S)
                    S.wait(m)
                    m = S.do(lambda e, ps=ps, raw=raw: e.activation(raw[:, :, TAPS - 1:TAPS - 1 + L], ps[:, :].rearrange("p (c t) -> p c t", c=2), ACT.Copy))
                    proj_ps.release(n, m)
                    cn, conv = conv_out.take(V)
                    V.wait(m)
                    for k in range(TAPS):
                        V.wait(m)
                        for c in (c0, c0 + 1):
                            o, i, w = conv[:, c - c0, :], raw[:, c - c0, k:k + L], conv_w[:, c, k:k + 1]
                            if k == 0:
                                f = lambda e, o=o, i=i, w=w: e.tensor_scalar(o, i, w, None, ALU.mult)
                            else:
                                f = lambda e, o=o, i=i, w=w: e.scalar_tensor_tensor(o, i, w, o, ALU.mult, ALU.add)
                            m = V.do(f)
                    raw_in.release(rn, m)
                    S.wait(m, *(xbc_free[par] if c0 == 0 else []))
                    m2 = S.do(lambda e, c0=c0, conv=conv: e.activation(xbc[par][:, c0:c0 + 2, :], conv[:, :, :], ACT.Silu))
                    conv_out.release(cn, m2)
                    conv_marks.append(m2)
                    yield
                made["xbc", b] = m2
                for c0 in range(0, NCZ, 2):
                    n, ps = proj_ps.take(T)
                    for c in (c0, c0 + 1):
                        m = channels(ps, (c - c0) * L, c * P, P)
                    once["xnT"] = m
                    S.wait(m, *(zs_free[par] if c0 == 0 else []))
                    m = S.do(lambda e, ps=ps, c0=c0: e.activation(zs[par][:, c0:c0 + 2, :], ps[:, :].rearrange("p (c t) -> p c t", c=2), ACT.Silu))
                    proj_ps.release(n, m)
                    yield
                made["zs", b] = m

            free = dict(b_tok=None, cbm=[None, None], xdt=None, xw=None, state=None, eexp=None, yz=None, sq=None, yoff=None)

            def mixer(b):
                par = b % 2
                dt_tok, wdec_tok, ecum = dt_tokens[par], wdec_tokens[par], ecums[par]
                for c in range(TPB):
                    tile = b * TPB + c
                    tok = slice(c * P, (c + 1) * P)
                    T.wait(made["xbc", b])
                    n, ps = misc_ps.take(T)
                    if c == 0:
                        T.run(lambda e, ps=ps: e.transpose(ps[:, P:2 * P], xbc[par][:, NCZ, 0:P], ident[:, :]))
                    m = T.do(lambda e, ps=ps, tok=tok: e.matmul(ps[:, 0:P], xbc[par][:, NCZ, tok], xbc[par][:, NCZ + 1, tok], start=True, stop=True))
                    V.wait(m, free["cbm"][c])
                    m = V.do(lambda e, ps=ps, c=c: e.tensor_copy(cbm[c][:, :], ps[:, 0:P]))
                    cbm_mark = m
                    if c == 0:
                        V.wait(free["b_tok"])
                        m = V.do(lambda e, ps=ps: e.tensor_copy(b_tok[:, :], ps[:, P:2 * P]))
                        b_mark = m
                    misc_ps.release(n, m)
                    for h0 in (0, NCZ // 2):
                        n, ps = misc_ps.take(T)
                        for k in range(NCZ // 2):
                            f = lambda e, k=k, ps=ps, h0=h0, tok=tok: e.transpose(ps[:, k * P:(k + 1) * P], xbc[par][:, h0 + k, tok], ident[:, :])
                            T.run(f) if k < NCZ // 2 - 1 else None
                        m = T.do(f)
                        hs = slice(h0 * P // HP, h0 * P // HP + NH // 2)
                        V.wait(m, free["xdt"], made["dt_tok", b])
                        for par2 in range(2):
                            o = xdt[:, hs, :].rearrange("p (q two) w -> p q two w", two=2)[:, :, par2, par2 * HP:(par2 + 1) * HP]
                            i0 = ps[:, :].rearrange("p (q two w) -> p q two w", two=2, w=HP)[:, :, par2, :]
                            i1 = dt_tok[:, c, hs].rearrange("p (q two) -> p q two", two=2)[:, :, par2:par2 + 1].to_broadcast([P, NH // 4, HP])
                            m = V.do(lambda e, o=o, i0=i0, i1=i1: e.tensor_tensor(o, i0, i1, ALU.mult))
                        xdt_mark = m
                        if c == 0:
                            V.wait(free["xw"], free["sq"])
                            i1 = wdec_tok[:, hs].rearrange("p (h o) -> p h o", o=1).to_broadcast([P, NH // 2, HP])
                            m = V.do(lambda e, ps=ps, hs=hs, i1=i1: e.tensor_tensor(xw[:, hs, :], ps[:, :].rearrange("p (h w) -> p h w", w=HP), i1, ALU.mult))
                            xw_mark = m
                        misc_ps.release(n, m)
                    if c == TPB - 1:
                        made["dt_tok_read", b] = xdt_mark
                    yield
                    T.wait(made["decay_operands", b])
                    halves = []

                    def decays(g):
                        n, ps = decay_ps.take(T)
                        T.run(lambda e, ps=ps: e.matmul(ps[:, :], identb[:, :], future[:, :].rearrange("p (o i) -> p o i", o=1).to_broadcast([P, HG, P]), start=True, stop=False))
                        m = T.do(lambda e, g=g, ps=ps, c=c: e.matmul(ps[:, :], LT[par][0:DROWS, c, g, :], RT[par][0:DROWS, c, :], start=False, stop=True))
                        r, buf = decay.take(S)
                        S.wait(m)
                        m = S.do(lambda e, ps=ps, buf=buf: e.activation(buf[:, :], ps[:, :], ACT.Exp))
                        decay_ps.release(n, m)
                        q, out_buf = mix.take(V)
                        V.wait(m, cbm_mark)
                        cb = cbm[c][:, :].rearrange("p (o i) -> p o i", o=1).to_broadcast([P, HG, P])
                        m = V.do(lambda e, buf=buf, out_buf=out_buf, cb=cb: e.tensor_tensor(
                            out_buf[:, :].rearrange("p (h i) -> p h i", h=HG), buf[:, :].rearrange("p (h i) -> p h i", h=HG), cb, ALU.mult))
                        decay.release(r, m)
                        return q, out_buf, m

                    ahead = [decays(0), decays(1)]
                    for g in range(NG):
                        if g + 2 < NG:
                            ahead.append(decays(g + 2))
                        q, buf, mark = ahead.pop(0)
                        if g % (NG // 2) == 0:
                            yn, yps = y_ps.take(T)
                        T.wait(mark, xdt_mark)
                        ct = g // 2 % (NCZ // 2)
                        for k, h in enumerate((0, 2, 1, 3)):
                            quad = ((HG * g + h) // 2) % 4 * 32
                            f = lambda e, h=h, quad=quad, ct=ct, g=g, buf=buf, yps=yps: e.matmul(
                                yps[quad:quad + 32, ct * P:(ct + 1) * P], xdt[:, HG * g + h, :], buf[:, h * P:(h + 1) * P],
                                start=(h % 2 == 0), stop=(h % 2 == 1), tile_position=(0, quad))
                            T.run(f) if k < HG - 1 else None
                        m = T.do(f)
                        mix.release(q, m)
                        if g % (NG // 2) == NG // 2 - 1:
                            halves.append((yn, yps, m))
                        yield
                    free["xdt"] = m
                    free["cbm"][c] = m
                    if c == TPB - 1:
                        made["decay_read", b] = m
                    if c == 0:
                        T.wait(xw_mark, b_mark)
                        for k in range(2):
                            n, ps = misc_ps.take(T)
                            m = T.do(lambda e, k=k, ps=ps: e.matmul(ps[:, :], b_tok[:, :], xw[:, :, :].rearrange("p h w -> p (h w)")[:, k * 512:(k + 1) * 512], start=True, stop=True))
                            S.wait(m, free["state"])
                            m2 = S.do(lambda e, k=k, ps=ps: e.activation(state[:, k * 512:(k + 1) * 512], ps[:, :], ACT.Copy))
                            misc_ps.release(n, m2)
                        free["b_tok"] = free["xw"] = m
                        state_mark = m2
                    for hf, (yn, yps, ymark) in enumerate(halves):
                        cts = slice(4 * hf, 4 * hf + 4)
                        if c == 1:
                            T.wait(state_mark, made["ecum", b])
                            n, ps = misc_ps.take(T)
                            for k in range(4):
                                f = lambda e, k=k, ps=ps, hf=hf: e.matmul(ps[:, k * P:(k + 1) * P], expand[:, 4 * hf + k, :], ecum[:, :], start=True, stop=True)
                                T.run(f) if k < 3 else None
                            m = T.do(f)
                            made["ecum_read", b] = m
                            S.wait(m, free["eexp"])
                            ee = S.do(lambda e, ps=ps: e.activation(eexp[:, :], ps[:, :], ACT.Copy))
                            misc_ps.release(n, ee)
                            n, ps = misc_ps.take(T)
                            for k in range(4):
                                f = lambda e, k=k, ps=ps, hf=hf, tok=tok: e.matmul(ps[:, k * P:(k + 1) * P], state[:, (4 * hf + k) * P:(4 * hf + k + 1) * P], xbc[par][:, NCZ + 1, tok], start=True, stop=True)
                                T.run(f) if k < 3 else None
                            m = T.do(f)
                            free["state"] = m
                            V.wait(m, ee)
                            m = V.do(lambda e, ps=ps: e.tensor_tensor(yoff[:, :], ps[:, :], eexp[:, :], ALU.mult))
                            misc_ps.release(n, m)
                            free["eexp"] = m
                            V.wait(m, ymark)
                            ysum = V.do(lambda e, yps=yps: e.tensor_tensor(yoff[:, :], yoff[:, :], yps[:, :], ALU.add))
                            y_ps.release(yn, ysum)
                            src = yoff
                        else:
                            ysum, src = ymark, yps
                        V.wait(ysum, free["yz"])
                        for k in range(4):
                            ct = 4 * hf + k
                            m = V.do(lambda e, k=k, ct=ct, src=src, tok=tok: e.scalar_tensor_tensor(
                                yz[:, ct, :], xbc[par][:, ct, tok], d_w[:, ct:ct + 1], src[:, k * P:(k + 1) * P], ALU.mult, ALU.add))
                        if c == 0:
                            y_ps.release(yn, m)
                        V.wait(m, made["zs", b])
                        m = V.do(lambda e, cts=cts, tok=tok: e.tensor_tensor(yz[:, cts, :], yz[:, cts, :], zs[par][:, cts, tok], ALU.mult))
                        yz_mark = m
                        S.wait(m, free["sq"], free["xw"])
                        sq_mark = S.do(lambda e, cts=cts: e.activation(sq[:, cts, :], yz[:, cts, :], ACT.Square))
                        yield
                    if c == TPB - 1:
                        xbc_free[par] = [yz_mark, m, made["dt_tok_read", b]]
                        zs_free[par] = [yz_mark]
                    on, ops = out_ps.take(T)
                    T.wait(yz_mark)
                    for ct in range(NCZ):
                        f = lambda e, ct=ct, ops=ops: e.matmul(ops[:, :], yz[:, ct, :], w_out[:, ct, :], start=(ct == 0), stop=(ct == NCZ - 1))
                        T.run(f) if ct < NCZ - 1 else None
                    out_mark = T.do(f)
                    n, ps = misc_ps.take(T)
                    T.wait(sq_mark)
                    for ct in range(NCZ):
                        f = lambda e, ct=ct, ps=ps: e.matmul(ps[:, 0:1], sq[:, ct, :], ones[:, 0:1], start=(ct == 0), stop=(ct == NCZ - 1))
                        T.run(f) if ct < NCZ - 1 else None
                    m = T.do(f)
                    free["yz"], free["sq"] = m, m
                    V.wait(m)
                    m = V.do(lambda e, ps=ps: e.tensor_scalar(stats[:, 10:11], ps[:, 0:1], 1.0 / HID, RMS_EPS, ALU.mult, ALU.add))
                    misc_ps.release(n, m)
                    m = rsqrt(stats[:, 10:11], stats[:, 11:12], stats[:, 12:13], m)
                    V.wait(m, out_mark)
                    m = V.do(lambda e, tile=tile, ops=ops: e.scalar_tensor_tensor(x_sb[:, tile, :], ops[:, :], stats[:, 11:12], x_sb[:, tile, :], ALU.mult, ALU.add))
                    out_ps.release(on, m)
                    x_ready[tile] = m
                    yield

            alternate((project(0), 1))
            for b in range(NB):
                if b + 1 < NB:
                    alternate((mixer(b), 40), (project(b + 1), 14))
                else:
                    alternate((mixer(b), 1))
            barrier()

        with ExitStack() as st:
            ssm_mixer(st)

        def cross_attention(st):
            bank = lambda name, shape=[P, 512], dt=F32: st.enter_context(nc.psum_tensor(name, shape, dt))
            max_ps = Ring([bank("max_ps0", [P, 1024])])
            score_ps = Ring([bank("score_ps0"), bank("score_ps1")])
            pv_ps = Ring([bank("pv_ps0"), bank("pv_ps1")])
            turn_ps = Ring([bank("turn_ps0"), bank("turn_ps1")])

            NPR = QH // 2
            PARTS = 3 * DH
            xn = sb(st, "a_xn", [P, DIM])
            stats = sb(st, "a_stats", [P, 16])
            q_st = sb(st, "q_st", [P, QH, SLOT], F16)
            k_st = sb(st, "k_st", [P, KVH, 2, SLOT], F16)
            ctx = [sb(st, f"ctx{i}", [P, TPB, KVH, DH]) for i in range(2)]
            v_aug = [sb(st, f"v_aug{i}", [P, TPB, KVH, 32]) for i in range(2)]
            qT = [sb(st, f"qT{i}", [P, NPR, L], F16) for i in range(2)]
            kT = [sb(st, f"kT{i}", [P, KVH, L], F16) for i in range(2)]
            maxes = sb(st, "maxes", [P, TPB, QH])
            nmax = sb(st, "nmax", [P, TPB, QH], F16)
            nmaxT = [sb(st, f"nmaxT{i}", [QH, L], F16) for i in range(2)]
            prob = Ring([sb(st, f"prob{i}", [P, 512]) for i in range(8)])
            pv = Ring([sb(st, f"pv{i}", [P, 512]) for i in range(2)])
            recip = sb(st, "recip", [P, 4, 4])
            o_tok = [sb(st, f"o_tok{i}", [P, TPB, DIM]) for i in range(2)]

            load_ctx = Load(semaphore("load_ctx"))
            load_max = Load(semaphore("load_max"))
            for i in range(2):
                V.do(lambda e, i=i: e.memset(v_aug[i][:, :, :, :], 0.0))
            m = V.do(lambda e: e.memset(k_st[:, :, :, :], 0.0))
            m2 = V.do(lambda e: e.memset(q_st[:, :, :], 0.0))
            V.wait(m, m2)
            for i in range(2):
                V.do(lambda e, i=i: e.memset(v_aug[i][:, :, :, DH:DH + 1], 1.0))
            init = V.do(lambda e: e.memset(k_st[:, :, :, PARTS:PARTS + 1], 1.0))
            for e in (T, S, V):
                e.wait(init)
            ready = {}
            fr = dict(xn=None, q_st=None, k_st=None, ctx=[None, None], v_aug=[None, None], qT=[None, None], kT=[None, None],
                      nmax=None, nmaxT=[None, None], maxes=None, recip=None, o_tok=[None, None])

            def heads_in(b):
                par = b % 2
                Y.wait(fr["ctx"][par])
                cm = load_ctx.start(Y, ctx[par][:, :, :, :].rearrange("p t k d -> p t (k d)"), ctx_rows[:, b * TPB:(b + 1) * TPB, :])
                Y.wait(cm)
                for t in range(TPB):
                    kv = ctx[par][:, t, :, :]
                    both = kv.rearrange("p k (o d) -> p k o d", o=1).to_broadcast([P, KVH, 2, DH])
                    S.wait(cm, fr["k_st"])
                    S.do(lambda e, both=both: e.activation(k_st[:, :, :, 0:DH], both, ACT.Copy))
                    m = S.do(lambda e, both=both: e.activation(k_st[:, :, :, 2 * DH:3 * DH], both, ACT.Copy))
                    V.wait(cm, m)
                    m = V.do(lambda e, both=both: e.tensor_tensor(k_st[:, :, :, DH:2 * DH], both, k_st[:, :, :, 0:DH], ALU.subtract))
                    V.wait(fr["v_aug"][par] if t == 0 else None)
                    vm = V.do(lambda e, kv=kv, t=t: e.tensor_copy(v_aug[par][:, t, :, 0:DH], kv))
                    n, ps = turn_ps.take(T)
                    T.wait(m)
                    ps16 = ps[:, :].bitcast(F16)
                    for k in range(KVH):
                        f = lambda e, k=k, ps16=ps16: e.transpose(ps16[:, k * P:(k + 1) * P], k_st[:, k, :, :].rearrange("p a s -> p (a s)"), ident16[:, :])
                        T.run(f) if k < KVH - 1 else None
                    m = T.do(f)
                    fr["k_st"] = m
                    V.wait(m, fr["kT"][par] if t == 0 else None)
                    km = V.do(lambda e, ps16=ps16, t=t: e.tensor_copy(kT[par][:, :, t * P:(t + 1) * P], ps16.rearrange("p (k j) -> p k j", j=P)))
                    turn_ps.release(n, km)
                    yield
                fr["ctx"][par] = vm
                ready["v", b], ready["kT", b] = vm, km
                for t in range(TPB):
                    tile = b * TPB + t
                    m = layer_norm(tile, x_ready[tile], xn[:, :], stats, fr["xn"])
                    q = xn[:, :].rearrange("p (h d) -> p h d", d=DH)
                    S.wait(m, fr["q_st"])
                    S.do(lambda e, q=q: e.activation(q_st[:, :, 0:DH], q, ACT.Copy))
                    m = S.do(lambda e, q=q: e.activation(q_st[:, :, DH:2 * DH], q, ACT.Copy))
                    V.wait(m)
                    m = V.do(lambda e, q=q: e.tensor_tensor(q_st[:, :, 2 * DH:3 * DH], q, q_st[:, :, 0:DH], ALU.subtract))
                    fr["xn"] = m
                    T.wait(m)
                    for half in range(2):
                        n, ps = turn_ps.take(T)
                        ps16 = ps[:, :].bitcast(F16)
                        for k in range(NPR // 2):
                            pr = half * NPR // 2 + k
                            f = lambda e, k=k, pr=pr, ps16=ps16: e.transpose(ps16[:, k * P:(k + 1) * P], q_st[:, 2 * pr:2 * pr + 2, :].rearrange("p a s -> p (a s)"), ident16[:, :])
                            T.run(f) if k < NPR // 2 - 1 else None
                        m = T.do(f)
                        fr["q_st"] = m
                        S.wait(m, fr["qT"][par] if t == 0 else None)
                        qm = S.do(lambda e, ps16=ps16, half=half, t=t: e.activation(
                            qT[par][:, half * NPR // 2:(half + 1) * NPR // 2, t * P:(t + 1) * P], ps16.rearrange("p (k j) -> p k j", j=P), ACT.Copy))
                        turn_ps.release(n, qm)
                        yield
                T.wait(qm, km)
                for t in range(TPB):
                    for k in range(KVH):
                        n, ps = max_ps.take(T)
                        for i in range(4):
                            pr, base = 2 * k + i // 2, SLOT * (i % 2)
                            f = lambda e, i=i, pr=pr, base=base, k=k, t=t, ps=ps: e.matmul(
                                ps[:, (i % 2 * 2 + i // 2) * L:(i % 2 * 2 + i // 2 + 1) * L], qT[par][base:base + PARTS, pr, t * P:(t + 1) * P], kT[par][base:base + PARTS, k, :], start=True, stop=True)
                            T.run(f) if i < 3 else None
                        m = T.do(f)
                        V.wait(m, fr["maxes"] if k == 0 else None)
                        mm = V.do(lambda e, k=k, t=t, ps=ps: e.reduce_max(maxes[:, t, 4 * k:4 * k + 4], ps[:, :].rearrange("p (h t) -> p h t", h=4), AX.X))
                        max_ps.release(n, mm)
                        yield
                V.wait(mm, fr["nmax"])
                for t in range(TPB):
                    for odd in range(2):
                        m = V.do(lambda e, t=t, odd=odd: e.tensor_scalar(nmax[:, t, odd * NPR:(odd + 1) * NPR].rearrange("p (k hh) -> p k hh", hh=2), maxes[:, t, :].rearrange("p (k odd hh) -> p k odd hh", odd=2, hh=2)[:, :, odd, :], -1.0, None, ALU.mult))
                fr["maxes"] = m
                n, ps = turn_ps.take(T)
                ps16 = ps[:, :].bitcast(F16)
                T.wait(m)
                T.run(lambda e, ps16=ps16: e.transpose(ps16[0:QH, 0:P], nmax[:, 0, :], ident16[:, :]))
                m = T.do(lambda e, ps16=ps16: e.transpose(ps16[0:QH, P:2 * P], nmax[:, 1, :], ident16[:, :]))
                fr["nmax"] = m
                V.wait(m, fr["nmaxT"][par])
                m = V.do(lambda e, ps16=ps16: e.tensor_copy(nmaxT[par][:, :], ps16[0:QH, 0:L]))
                turn_ps.release(n, m)
                Y.wait(m)
                for odd in range(2):
                    row = SLOT * odd + PARTS
                    m = load_max.start(Y, qT[par][row:row + 1, :, :], nmaxT[par][odd * NPR:(odd + 1) * NPR, :])
                Y.wait(m)
                fr["nmaxT"][par] = m
                ready["qT", b] = m
                yield

            def attend(b):
                par = b % 2
                T.wait(ready["qT", b], ready["v", b], ready["kT", b])
                V.wait(fr["o_tok"][par])
                for kh in range(2):
                    for odd in range(2):
                        vn, vps = pv_ps.take(T)
                        base = SLOT * odd
                        probs = []

                        def scores(t, quad):
                            k = 4 * kh + quad
                            n, ps = score_ps.take(T)
                            m = T.do(lambda e, base=base: e.matmul(ps[:, :], kT[par][base:base + PARTS + 1, k, t * P:(t + 1) * P],
                                                        qT[par][base:base + PARTS + 1, 2 * k:2 * k + 2, :], start=True, stop=True))
                            r, buf = prob.take(S)
                            S.wait(m)
                            m = S.do(lambda e: e.activation(buf[:, :], ps[:, :], ACT.Exp, scale=DH ** -0.5))
                            score_ps.release(n, m)
                            probs.append((r, buf, m, t, quad))

                        todo = [(t, quad) for t in range(TPB) for quad in range(4)]
                        for t, quad in todo[:2]:
                            scores(t, quad)
                        for i in range(len(todo)):
                            if i + 2 < len(todo):
                                scores(*todo[i + 2])
                            r, buf, m, t, quad = probs[i]
                            T.wait(m)
                            m = T.do(lambda e, buf=buf, t=t, quad=quad, vps=vps, kh=kh: e.matmul(
                                vps[32 * quad:32 * quad + 32, :], v_aug[par][:, t, 4 * kh + quad, :], buf[:, :],
                                start=(t == 0), stop=(t == TPB - 1), tile_position=(0, 32 * quad)))
                            prob.release(r, m)
                            if i % 2:
                                yield
                        r, pbuf = pv.take(S)
                        S.wait(m)
                        m = S.do(lambda e, pbuf=pbuf, vps=vps: e.activation(pbuf[:, :], vps[:, :], ACT.Copy))
                        pv_ps.release(vn, m)
                        n, ps = turn_ps.take(T)
                        T.wait(m)
                        for i in range(4):
                            f = lambda e, i=i, pbuf=pbuf, ps=ps: e.transpose(ps[:, i * P:(i + 1) * P], pbuf[:, i * P:(i + 1) * P], ident[:, :])
                            T.run(f) if i < 3 else None
                        m = T.do(f)
                        pv.release(r, m)
                        V.wait(m, fr["recip"])
                        m = V.do(lambda e, ps=ps: e.reciprocal(recip[:, :, :], ps[:, :].rearrange("p (b q w) -> p b q w", b=4, q=4)[:, :, :, DH]))
                        V.wait(m)
                        for t in range(TPB):
                            cols = o_tok[par][:, t, :].rearrange("p (kh q hh odd d) -> p kh q hh odd d", kh=2, q=4, hh=2, odd=2)[:, kh, :, :, odd, :]
                            for hh in range(2):
                                i0 = ps[:, (hh * TPB + t) * P:(hh * TPB + t + 1) * P].rearrange("p (q w) -> p q w", q=4)[:, :, 0:DH]
                                i1 = recip[:, hh * TPB + t, :].rearrange("p (q o) -> p q o", o=1).to_broadcast([P, 4, DH])
                                m = V.do(lambda e, o=cols[:, :, hh, :], i0=i0, i1=i1: e.tensor_tensor(o, i0, i1, ALU.mult))
                        fr["recip"] = m
                        turn_ps.release(n, m)
                        yield
                fr["qT"][par] = fr["kT"][par] = fr["v_aug"][par] = prob.free[(prob.at - 1) % 8]
                G.wait(m)
                for t in range(TPB):
                    tile = b * TPB + t
                    gm = G.do(lambda e, t=t, tile=tile: e.tensor_tensor(x_sb[:, tile, :], x_sb[:, tile, :], o_tok[par][:, t, :], ALU.add))
                    x_ready[tile] = gm
                fr["o_tok"][par] = gm
                yield

            alternate((heads_in(0), 1))
            for b in range(NB):
                if b + 1 < NB:
                    alternate((attend(b), 21), (heads_in(b + 1), 23))
                else:
                    alternate((attend(b), 1))
            barrier()

        with ExitStack() as st:
            cross_attention(st)

        def experts(st):
            bank = lambda name, shape=[P, 512], dt=F32: st.enter_context(nc.psum_tensor(name, shape, dt))
            gate_ps = Ring([bank("gate_ps0"), bank("gate_ps1")])
            up_ps = Ring([bank("up_ps0"), bank("up_ps1")])
            turn_ps = Ring([bank("mturn_ps0"), bank("mturn_ps1")])
            down_ps = Ring([bank("down_ps0"), bank("down_ps1")])
            xn = [sb(st, f"m_xn{i}", [P, DIM]) for i in range(2)]
            stats = sb(st, "m_stats", [P, 16])
            xnT = sb(st, "m_xnT", [P, KD, NT, P])
            w_gu = [sb(st, f"w_gu{i}", [P, KD, 2 * EH]) for i in range(2)]
            w_dn = [sb(st, f"w_dn{i}", [P, KD, DIM]) for i in range(2)]
            w_router = sb(st, "w_router", [P, KD, NE])
            s_router = sb(st, "s_router", [P, KD])
            e_scale = sb(st, "e_scale", [P, NE])
            lower = sb(st, "lower", [P, NE, NE])
            r_in = sb(st, "r_in", [P, NT])
            r_tmp = sb(st, "r_tmp", [P, NT])
            junk = sb(st, "junk", [P, DIM])
            logit = sb(st, "logit", [P, NT, NE])
            chosen = sb(st, "chosen", [P, NT, NE])
            weight = sb(st, "weight", [P, NT, NE])
            col = sb(st, "col", [P, NT])
            wide = [sb(st, f"wide{i}", [P, NT, NE, NE]) for i in range(2)]
            gelu = [sb(st, f"gelu{i}", [P, EH]) for i in range(2)]
            act = [sb(st, f"act{i}", [P, EH]) for i in range(2)]
            actT = [sb(st, f"actT{i}", [P, KD, P]) for i in range(2)]
            load_e = [Load(semaphore(f"load_e{i}")) for i in range(2)]
            load_r = Load(semaphore("load_r"))
            store_o = Load(semaphore("store_o"))

            def load_expert(e, after):
                i = e % 2
                Y.wait(after)
                load_e[i].start(Y, w_gu[i][:, :, :], A["c_gatingT"][e].rearrange("(k p) n -> p k n", p=P))
                return load_e[i].start(Y, w_dn[i][:, :, :], A["L0_ffn_linear"][e].rearrange("(k p) n -> p k n", p=P))

            for dst, src in [
                (w_router[:, :, :], A["L0_ffn_router_logits"].rearrange("(k p) e -> p k e", p=P)),
                (s_router[:, :], A["c_router_scale"]),
                (lower[:, :, :], A["c_lower"].rearrange("p (a b) -> p a b", a=NE)),
                (e_scale[:, :], A["L0_ffn_per_expert_scale"].rearrange("(o e) -> o e", o=1).to_broadcast([P, NE])),
            ]:
                r_ready = load_r.start(S, dst, src)
            e_ready = [load_expert(0, None), load_expert(1, None)]
            V.wait(r_ready)
            for k in range(KD):
                wr_mark = V.do(lambda e, k=k: e.tensor_scalar(w_router[:, k, :], w_router[:, k, :], s_router[:, k:k + 1], None, ALU.mult))
            T.wait(wr_mark)
            xn_free = [None, None]
            jm = None
            for tile in range(NT):
                i = tile % 2
                m = layer_norm(tile, x_ready[tile], xn[i][:, :], stats, xn_free[i])
                S.wait(m, jm)
                jm = S.do(lambda e, i=i, tile=tile: e.activation(junk[:, :], xn[i][:, :], ACT.Square, accum_out=r_in[:, tile:tile + 1]))
                n, ps = turn_ps.take(T)
                T.wait(m)
                for k in range(KD):
                    f = lambda e, k=k, i=i, ps=ps: e.transpose(ps[:, k * P:(k + 1) * P], xn[i][:, k * P:(k + 1) * P], ident[:, :])
                    T.run(f) if k < KD - 1 else None
                m = T.do(f)
                S.wait(m)
                xnT_mark = S.do(lambda e, ps=ps, tile=tile: e.activation(xnT[:, :, tile, :], ps[:, :].rearrange("p (k j) -> p k j", k=KD), ACT.Copy))
                turn_ps.release(n, xnT_mark)
                xn_free[i] = m
                V.wait(jm)
                n, ps = down_ps.take(T)
                T.wait(xnT_mark)
                for k in range(KD):
                    f = lambda e, k=k, tile=tile, ps=ps: e.matmul(ps[:, 0:NE], xnT[:, k, tile, :], w_router[:, k, :], start=(k == 0), stop=(k == KD - 1))
                    T.run(f) if k < KD - 1 else None
                m = T.do(f)
                V.wait(m)
                lm = V.do(lambda e, tile=tile, ps=ps: e.tensor_copy(logit[:, tile, :], ps[:, 0:NE]))
                down_ps.release(n, lm)
            V.wait(lm, jm)
            m = V.do(lambda e: e.tensor_scalar(r_in[:, :], r_in[:, :], 1.0 / DIM, ROUTER_EPS, ALU.mult, ALU.add))
            m = rsqrt(r_in[:, :], col[:, :], r_tmp[:, :], m)
            V.wait(m)
            m = V.do(lambda e: e.tensor_scalar(r_in[:, :], col[:, :], float(np.float32(DIM) ** np.float32(-0.5)), None, ALU.mult))
            V.wait(m)
            per_tile = lambda a, shape: a.to_broadcast(shape)
            m = V.do(lambda e: e.tensor_tensor(logit[:, :, :], logit[:, :, :], r_in[:, :].rearrange("p (t o) -> p t o", o=1).to_broadcast([P, NT, NE]), ALU.mult))
            V.wait(m)
            la = logit[:, :, :].rearrange("p t (e o) -> p t e o", o=1).to_broadcast([P, NT, NE, NE])
            lb = logit[:, :, :].rearrange("p t (o e) -> p t o e", o=1).to_broadcast([P, NT, NE, NE])
            low = lower[:, :, :].rearrange("p (o a) b -> p o a b", o=1).to_broadcast([P, NT, NE, NE])
            V.do(lambda e: e.tensor_tensor(wide[0][:, :, :, :], lb, la, ALU.is_gt))
            m = V.do(lambda e: e.tensor_tensor(wide[1][:, :, :, :], lb, la, ALU.is_equal))
            V.wait(m)
            m = V.do(lambda e: e.tensor_tensor(wide[1][:, :, :, :], wide[1][:, :, :, :], low, ALU.mult))
            V.wait(m)
            m = V.do(lambda e: e.tensor_tensor(wide[0][:, :, :, :], wide[0][:, :, :, :], wide[1][:, :, :, :], ALU.add))
            V.wait(m)
            m = V.do(lambda e: e.reduce_sum(chosen[:, :, :], wide[0][:, :, :, :], AX.X))
            V.wait(m)
            m = V.do(lambda e: e.tensor_scalar(chosen[:, :, :], chosen[:, :, :], 2.0, None, ALU.is_lt))
            m2 = V.do(lambda e: e.reduce_max(col[:, :], logit[:, :, :], AX.X))
            V.wait(m2)
            bc = lambda a: a[:, :].rearrange("p (t o) -> p t o", o=1).to_broadcast([P, NT, NE])
            m = V.do(lambda e: e.tensor_tensor(weight[:, :, :], logit[:, :, :], bc(col), ALU.subtract))
            S.wait(m)
            m = S.do(lambda e: e.activation(weight[:, :, :], weight[:, :, :], ACT.Exp))
            V.wait(m)
            m = V.do(lambda e: e.tensor_tensor(weight[:, :, :], weight[:, :, :], chosen[:, :, :], ALU.mult))
            V.wait(m)
            m = V.do(lambda e: e.reduce_sum(col[:, :], weight[:, :, :], AX.X))
            V.wait(m)
            m = V.do(lambda e: e.reciprocal(col[:, :], col[:, :]))
            V.wait(m)
            m = V.do(lambda e: e.tensor_tensor(weight[:, :, :], weight[:, :, :], bc(col), ALU.mult))
            V.wait(m)
            m = V.do(lambda e: e.tensor_tensor(weight[:, :, :], weight[:, :, :], e_scale[:, :].rearrange("p (o e) -> p o e", o=1).to_broadcast([P, NT, NE]), ALU.mult))
            V.wait(m)

            f2 = dict(gelu=[None, None], act=[None, None], actT=[None, None])

            def up(e, tile, i):
                w = w_gu[e % 2]
                gn, gps = gate_ps.take(T)
                un, ups = up_ps.take(T)
                T.wait(e_ready[e])
                for ps, off in ((gps, 0), (ups, EH)):
                    for k in range(KD):
                        f = lambda e_, k=k, ps=ps, off=off: e_.matmul(ps[:, :], xnT[:, k, tile, :], w[:, k, off:off + EH], start=(k == 0), stop=(k == KD - 1))
                        T.run(f) if k < KD - 1 else None
                    m = T.do(f)
                    if off == 0:
                        S.wait(m, f2["gelu"][i])
                        gm = S.do(lambda e_: e_.activation(gelu[i][:, :], gps[:, :], ACT.Gelu_apprx_tanh))
                        gate_ps.release(gn, gm)
                V.wait(m, gm, f2["act"][i])
                m = V.do(lambda e_: e_.tensor_tensor(act[i][:, :], gelu[i][:, :], ups[:, :], ALU.mult))
                up_ps.release(un, m)
                f2["gelu"][i] = m
                return m

            def down(e, tile, i, am):
                w = w_dn[e % 2]
                n, ps = turn_ps.take(T)
                T.wait(am)
                for k in range(KD):
                    f = lambda e_, k=k: e_.transpose(ps[:, k * P:(k + 1) * P], act[i][:, k * P:(k + 1) * P], ident[:, :])
                    T.run(f) if k < KD - 1 else None
                m = T.do(f)
                f2["act"][i] = m
                S.wait(m, f2["actT"][i])
                m = S.do(lambda e_: e_.activation(actT[i][:, :, :], ps[:, :].rearrange("p (k j) -> p k j", k=KD), ACT.Copy))
                turn_ps.release(n, m)
                dn, dps = down_ps.take(T)
                T.wait(m)
                for k in range(KD):
                    f = lambda e_, k=k: e_.matmul(dps[:, :], actT[i][:, k, :], w[:, k, :], start=(k == 0), stop=(k == KD - 1))
                    T.run(f) if k < KD - 1 else None
                m = T.do(f)
                f2["actT"][i] = m
                V.wait(m, x_ready[tile])
                vm = V.do(lambda e_: e_.scalar_tensor_tensor(x_sb[:, tile, :], dps[:, :], weight[:, tile, e:e + 1], x_sb[:, tile, :], ALU.mult, ALU.add))
                down_ps.release(dn, vm)
                x_ready[tile] = vm
                return m

            steps = [(e, tile) for e in range(NE) for tile in range(NT)]
            prev = None
            for s, (e, tile) in enumerate(steps):
                am = up(e, tile, s % 2)
                if prev is not None:
                    m = down(*prev)
                    if prev[1] == NT - 1 and prev[0] + 2 < NE:
                        e_ready.append(load_expert(prev[0] + 2, m))
                prev = (e, tile, s % 2, am)
            down(*prev)
            for tile in range(NT):
                Y.wait(x_ready[tile])
                done = store_o.start(Y, out_rows[:, tile, :], x_sb[:, tile, :])
            Y.wait(done)

        with ExitStack() as st:
            experts(st)

        block = top_block = ExitStack()
        with block:
            b = block.enter_context(nc.Block())

            @b.tensor
            def _(e):
                for f in T.queue:
                    f(e)

            @b.vector
            def _(e):
                for f in V.queue:
                    f(e)

            @b.scalar
            def _(e):
                for f in S.queue:
                    f(e)

            @b.gpsimd
            def _(e):
                for f in G.queue:
                    f(e)

            @b.sync
            def _(e):
                for f in Y.queue:
                    f(e)


def shape_constants():
    j = np.arange(P)
    select = np.zeros((64, NG, P), np.float32)
    for part in range(3):
        for g in range(NG):
            select[part * NG + g, g, :] = 1.0
    sign = np.zeros((64, HG, P), np.float32)
    for part in range(3):
        for h in range(HG):
            sign[3 * NG + part * HG + h, h, :] = -1.0
    expand = np.zeros((NH, HID), np.float32)
    for h in range(NH):
        expand[h, h * HP:(h + 1) * HP] = 1.0
    lower = (np.arange(NE)[None, :] < np.arange(NE)[:, None]).astype(np.float32).reshape(1, NE * NE)
    return {
        "c_ident": np.eye(P, dtype=np.float32),
        "c_causal": (j[:, None] <= j[None, :]).astype(np.float32),
        "c_select": select.reshape(64, NG * P),
        "c_head_sign": sign.reshape(64, HG * P),
        "c_expand": expand,
        "c_lower": np.broadcast_to(lower, (P, NE * NE)).copy(),
    }


def kernel(**inputs):
    import concourse.bacc as bacc
    from concourse.bass_utils import run_bass_kernel_spmd

    a = {k: np.asarray(v) for k, v in inputs.items()}
    arrays = {k: np.ascontiguousarray(a[k]) for k in (
        "x", "ctx_512", "L0_attn_conv_w", "L0_attn_dt_bias", "L0_attn_A_log",
        "L0_ffn_router_logits", "L0_ffn_linear", "L0_ffn_per_expert_scale")}
    columns = lambda v: np.ascontiguousarray(v.reshape(-1, P).T)
    arrays["c_norm_w"] = columns(a["L0_attn_norm_w"])
    arrays["c_router_scale"] = columns(a["L0_ffn_router_scale"])
    arrays["c_w_inT"] = np.ascontiguousarray(a["L0_attn_W_in"].T)
    arrays["c_w_outT"] = np.ascontiguousarray(a["L0_attn_W_out"].T)
    arrays["c_gatingT"] = np.ascontiguousarray(a["L0_ffn_gating_einsum"].transpose(0, 3, 1, 2).reshape(NE, DIM, 2 * EH))
    arrays["c_D_channels"] = columns(np.repeat(a["L0_attn_D"], HP))
    arrays.update(shape_constants())

    nc = bacc.Bacc("TRN2", target_bir_lowering=False, num_devices=1)
    feeds, aps = {}, {}
    for name, value in arrays.items():
        feeds[name + "_dram"] = value
        aps[name] = nc.dram_tensor(name + "_dram", value.shape, mybir.dt.from_np(value.dtype), kind="ExternalInput").ap()
    out = nc.dram_tensor("out_dram", (NB, L, DIM), F32, kind="ExternalOutput").ap()
    layer_kernel(nc, aps, out)
    result = run_bass_kernel_spmd(nc, [feeds], core_ids=[0])
    return result.results[0]["out_dram"]
```

```python
from contextlib import ExitStack

import concourse.bass as bass
import numpy as np
from concourse import mybir

F32 = mybir.dt.float32
BF16 = mybir.dt.bfloat16
F16 = mybir.dt.float16
ALU = mybir.AluOpType
ACT = mybir.ActivationFunctionType
AX = mybir.AxisListType

P = 128
NB, L, DIM = 8, 256, 512
TPB = L // P
NT = NB * TPB
KD = DIM // P
HID, NH, HP, NS = 1024, 64, 16, 128
CONV = HID + 2 * NS
NCZ, NCX = HID // P, CONV // P
TAPS = 4
HG = 4
NG = NH // HG
DROWS = 3 * (NG + HG)
QH, KVH, DH = 32, 8, 16
SLOT = 64
NE, EH = 8, 512
MT = (2 * NT * P + NE * P) // P
WR = 3
LN_EPS, RMS_EPS, ROUTER_EPS = 1e-5, 1e-5, 1e-6


class Engine:

    def __init__(self, name, sem):
        self.name, self.sem, self.count, self.queue, self.seen = name, sem, 0, [], {}

    def run(self, instruction):
        self.queue.append(instruction)

    def do(self, instruction):
        self.count += 1
        self.queue.append(lambda e: instruction(e).then_inc(self.sem, 1))
        return self.sem, self.count

    def wait(self, *marks):
        for mark in marks:
            if mark is None:
                continue
            sem, value = mark
            if self.seen.get(id(sem), 0) < value:
                self.seen[id(sem)] = value
                self.queue.append(lambda e, s=sem, v=value: e.wait_ge(s, v))


class Load:

    def __init__(self, sem):
        self.sem, self.count = sem, 0

    def start(self, eng, out, in_):
        self.count += 16
        eng.queue.append(lambda e: e.dma_start(out, in_).then_inc(self.sem, 16))
        return self.sem, self.count


class Ring:

    def __init__(self, buffers):
        self.buffers, self.at = buffers, 0
        self.free = [None] * len(buffers)
        self.in_use = [False] * len(buffers)

    def busy(self):
        return self.in_use[self.at % len(self.buffers)]

    def take(self, writer):
        n = self.at % len(self.buffers)
        assert not self.in_use[n], "taken before its last reader is queued"
        self.at, self.in_use[n] = self.at + 1, True
        writer.wait(self.free[n])
        return n, self.buffers[n]

    def release(self, n, mark):
        self.free[n], self.in_use[n] = mark, False


BLOCKED = "blocked"


def alternate(*generators):
    live = [[g, w, 0.0] for g, w in generators]
    blocked = 0
    while live:
        item = min(live, key=lambda x: x[2])
        r = next(item[0], "end")
        if r == "end":
            live.remove(item)
            blocked = 0
        elif r == BLOCKED:
            blocked += 1
            assert len(live) > 1 and blocked < 8, "every stage is blocked"
            item[2] = max(x[2] for x in live if x is not item) + 1e-9
        else:
            blocked = 0
            item[2] += 1.0 / item[1]


def together(*generators):
    live = list(generators)
    while live:
        live = [g for g in live if next(g, "end") != "end"]
        yield


def pipeline(items, stages, lag=1):
    at = [{} for _ in items]
    for s in range(len(items) + lag * (len(stages) - 1)):
        for d, stage in reversed(list(enumerate(stages))):
            i = s - d * lag
            if 0 <= i < len(items):
                stage(items[i], at[i])
        yield


def layer_kernel(nc, A, out):
    x_rows = A["x"].rearrange("b s d -> (b s) d").rearrange("(t p) d -> p t d", p=P)
    ctx_rows = A["ctx_512"].rearrange("b s d -> (b s) d").rearrange("(t p) d -> p t d", p=P)

    with ExitStack() as top:
        semaphore = lambda name: top.enter_context(nc.semaphore(name))
        T = Engine("tensor", semaphore("tensor_done"))
        V = Engine("vector", semaphore("vector_done"))
        S = Engine("scalar", semaphore("scalar_done"))
        G = Engine("gpsimd", semaphore("gpsimd_done"))
        Y = Engine("sync", semaphore("sync_done"))
        engines = [T, V, S, G, Y]

        def sb(stack, name, shape, dt=F32):
            return stack.enter_context(nc.sbuf_tensor(name, shape, dt))

        def barrier():
            for e in engines:
                e.wait(*[(o.sem, o.count) for o in engines if o.count])

        x_sb = sb(top, "x_sb", [P, NT, DIM])
        ident = sb(top, "ident", [P, P])
        ident16 = sb(top, "ident16", [P, P], F16)
        tokens = nc.dram_tensor("normed_tokens", [(NT + 1) * P, DIM], F32).ap()
        slots = nc.dram_tensor("slots", [MT * P, 2], F32).ap()
        load_const = Load(semaphore("load_const"))
        load_x = Load(semaphore("load_x"))
        load_r = Load(semaphore("load_r"))
        store_tokens = [Load(semaphore(f"store_tokens{i}")) for i in range(2)]
        x_ready = [load_x.start(Y, x_sb[:, :, :], x_rows)] * NT
        const_ready = load_const.start(S, ident[:, :], A["c_ident"])

        def rsqrt(v, y, tmp, ready):
            I32 = mybir.dt.int32
            V.wait(ready)
            m = V.do(lambda e: e.tensor_scalar(tmp.bitcast(I32), v.bitcast(I32), 1, None, ALU.arith_shift_right))
            V.wait(m)
            m = V.do(lambda e: e.tensor_scalar(y.bitcast(I32), tmp.bitcast(I32), -1.0, float(0x5F3759DF), ALU.mult, ALU.add))
            yield m
            for _ in range(4):
                G.wait(m)
                m = G.do(lambda e: e.tensor_tensor(tmp, y, y, ALU.mult))
                G.wait(m)
                m = G.do(lambda e: e.tensor_tensor(tmp, tmp, v, ALU.mult))
                G.wait(m)
                m = G.do(lambda e: e.tensor_scalar(tmp, tmp, -0.5, 1.5, ALU.mult, ALU.add))
                G.wait(m)
                m = G.do(lambda e: e.tensor_tensor(y, y, tmp, ALU.mult))
            yield m

        def norm_factors(b, s):
            for t in range(TPB):
                V.wait(x_ready[b * TPB + t])
                m = V.do(lambda e, t=t: e.bn_stats(s[:, 6 * t:6 * t + 6], x_sb[:, b * TPB + t, :]))
            V.wait(m)
            for t in range(TPB):
                m = V.do(lambda e, t=t: e.bn_aggr(s[:, 12 + 2 * t:14 + 2 * t], s[:, 6 * t:6 * t + 6]))
            V.wait(m)
            m = V.do(lambda e: e.tensor_scalar(s[:, 16:18], s[:, 12:16].rearrange("p (t c) -> p t c", c=2)[:, :, 1], LN_EPS, None, ALU.add))
            yield from rsqrt(s[:, 16:18], s[:, 18:20], s[:, 20:22], m)

        def layer_norm(tile, xn_, s, after):
            b, t = divmod(tile, TPB)
            for m in norm_factors(b, s):
                pass
            V.wait(m, after)
            return V.do(lambda e: normalise(e, xn_, tile, s, t))

        def normalise(e, out_, tile, s, t):
            return e.tensor_scalar(out_, x_sb[:, tile, :], s[:, 12 + 2 * t:13 + 2 * t], s[:, 18 + t:19 + t], ALU.subtract, ALU.mult)

        def ssm_mixer(st):
            bank = lambda name, shape=[P, 512], dt=F32: st.enter_context(nc.psum_tensor(name, shape, dt))
            proj_ps = Ring([bank("proj_ps0"), bank("proj_ps1")])
            decay_ps = Ring([bank("decay_ps0"), bank("decay_ps1")])
            y_ps = Ring([bank("y_ps0"), bank("y_ps1")])
            misc_ps = Ring([bank("misc_ps")])
            out_ps = Ring([bank("out_ps")])

            w_in = sb(st, "w_in", [P, KD, 2 * HID + 2 * NS + NH])
            w_out = sb(st, "w_out", [P, NCZ, DIM])
            conv_w = sb(st, "conv_w", [P, NCX, TAPS])
            norm_w = sb(st, "norm_w", [P, NCZ])
            d_w = sb(st, "d_w", [P, NCZ])
            head_w = sb(st, "head_w", [NH, 4])
            raw_in = Ring([sb(st, f"raw{i}", [P, 2, L + TAPS - 1]) for i in range(2)])
            causal = raw_in.buffers[0][:, 0, 0:P]
            identb = sb(st, "identb", [P, P], BF16)
            future = sb(st, "future", [P, P], BF16)
            expand = sb(st, "expand", [NH, NCZ, P])
            ones = sb(st, "ones", [P, 1])

            xn = sb(st, "xn", [P, DIM])
            stats = sb(st, "stats", [P, 24])
            rstats = sb(st, "rstats", [P, 4])
            xnT = sb(st, "xnT", [P, KD, L])
            conv_out = Ring([sb(st, f"conv{i}", [P, 2, L]) for i in range(2)])
            xbc = [sb(st, f"xbc{i}", [P, NCX, L]) for i in range(2)]
            zs = [sb(st, f"zs{i}", [P, NCZ, L]) for i in range(2)]
            select_f = xbc[0][0:64, 0:NCZ, :].rearrange("p c t -> p (c t)")
            head_sign = zs[0][0:64, 0:2, :].rearrange("p c t -> p (c t)")
            dtT = sb(st, "dtT", [NH, 7, L])
            wdecT = sb(st, "wdecT", [NH, P])
            cum3 = sb(st, "cum3", [NH, 3, TPB, P], BF16)
            rest = dtT[:, 3:5, :]
            dt_tokens = [sb(st, f"dt_tok{i}", [P, TPB, NH]) for i in range(2)]
            wdec_tokens = [sb(st, f"wdec_tok{i}", [P, NH]) for i in range(2)]
            ecums = [sb(st, f"ecum{i}", [NH, P]) for i in range(2)]
            LT = [sb(st, f"LT{i}", [64, TPB, NG, P], BF16) for i in range(2)]
            RT = [sb(st, f"RT{i}", [64, TPB, HG * P], BF16) for i in range(2)]
            b_tok = sb(st, "b_tok", [P, NS])
            cbm = [sb(st, f"cbm{i}", [P, P]) for i in range(2)]
            xdt = [sb(st, f"xdt{i}", [P, NH // 2, 2 * HP]) for i in range(2)]
            xw = sb(st, "xw", [P, NH, HP])
            state = sb(st, "state", [P, HID])
            decay = Ring([sb(st, f"decay{i}", [P, HG * P]) for i in range(2)])
            mix = Ring([sb(st, f"mix{i}", [P, HG * P]) for i in range(4)])
            eexp = sb(st, "eexp", [P, 512])
            yz = sb(st, "yz", [P, NCZ, P])

            load_w = Load(semaphore("load_w"))
            scratch = [nc.dram_tensor(f"cum_scratch{i}", [3, NH, TPB, P], BF16).ap() for i in range(2)]
            store_cum = Load(semaphore("store_cum"))
            load_cum = Load(semaphore("load_cum"))

            for k in range(KD):
                w_ready = load_w.start(S, w_in[:, k, :], A["c_w_inT"][k * P:(k + 1) * P, :])
            for dst, src in [
                (conv_w[:, :, :], A["L0_attn_conv_w"].rearrange("(c p) k -> p c k", p=P)),
                (norm_w[:, :], A["c_norm_w"]),
                (d_w[:, :], A["c_D_channels"]),
                (head_w[:, 0:1], A["L0_attn_dt_bias"].rearrange("(h o) -> h o", o=1)),
                (head_w[:, 1:2], A["L0_attn_A_log"].rearrange("(h o) -> h o", o=1)),
                (causal, A["c_causal"]),
                (expand[:, :, :], A["c_expand"].rearrange("h (c p) -> h c p", p=P)),
                (select_f, A["c_select"]),
                (w_out[:, :, :], A["c_w_outT"].rearrange("(c p) d -> p c d", p=P)),
            ]:
                const_ready = load_const.start(Y, dst, src)
            const_ready = load_const.start(Y, head_sign, A["c_head_sign"])

            for e in (V, S, T, G):
                e.wait(const_ready)
            V.do(lambda e: e.memset(ones[:, :], 1.0))
            m = V.do(lambda e: e.tensor_scalar(future[:, :], causal, 1.0, 1e30, ALU.subtract, ALU.mult))
            V.wait(m)
            for i in range(2):
                V.do(lambda e, i=i: e.memset(raw_in.buffers[i][:, :, 0:TAPS - 1], 0.0))
                V.do(lambda e, i=i: e.memset(xdt[i][:, :, :], 0.0))
            V.do(lambda e: e.tensor_copy(ident16[:, :], ident[:, :]))
            V.do(lambda e: e.tensor_copy(identb[:, :], ident[:, :]))
            for i in range(2):
                for c in range(TPB):
                    V.do(lambda e, i=i, c=c: e.tensor_copy(LT[i][:, c, :, :], select_f.rearrange("p (g j) -> p g j", j=P)))
                    V.do(lambda e, i=i, c=c: e.tensor_copy(RT[i][:, c, :], head_sign))
            V.do(lambda e: e.tensor_scalar(conv_w[:, :, :], conv_w[:, :, :], 0.5, None, ALU.mult))
            G.wait(w_ready)
            for k in range(KD):
                half_z = G.do(lambda e, k=k: e.tensor_scalar(w_in[:, k, 0:HID], w_in[:, k, 0:HID], 0.5, None, ALU.mult))
            for c in range(NCZ):
                normed_out = G.do(lambda e, c=c: e.tensor_scalar(w_out[:, c, :], w_out[:, c, :], norm_w[:, c:c + 1], None, ALU.mult))
            m = S.do(lambda e: e.activation(head_w[:, 2:3], head_w[:, 1:2], ACT.Exp))
            V.wait(m)
            init = V.do(lambda e: e.tensor_scalar(head_w[:, 3:4], head_w[:, 2:3], -1.0, None, ALU.mult))
            for e in (T, S, V, G, Y):
                e.wait(init)

            made = {}
            last = {}
            NHALF = NG // 2
            UNITS = [(b, c, hf) for b in range(NB) for c in range(TPB) for hf in range(2)]

            def project(b):
                par = b % 2
                dt_tok, wdec_tok, ecum = dt_tokens[par], wdec_tokens[par], ecums[par]
                norm = None
                for norm in norm_factors(b, stats):
                    yield
                for t in range(TPB):
                    tile = b * TPB + t
                    V.wait(norm, last.get("xn"))
                    xm = V.do(lambda e, t=t, tile=tile: normalise(e, xn[:, :], tile, stats, t))
                    yield
                    n, ps = proj_ps.take(T)
                    T.wait(xm)
                    for k in range(KD):
                        f = lambda e, k=k, ps=ps: e.transpose(ps[:, k * P:(k + 1) * P], xn[:, k * P:(k + 1) * P], ident[:, :])
                        T.run(f) if k < KD - 1 else None
                    last["xn"] = m = T.do(f)
                    yield
                    S.wait(m, last.get("xnT"))
                    xnT_mark = S.do(lambda e, t=t, ps=ps: e.activation(xnT[:, :, t * P:(t + 1) * P], ps[:, :].rearrange("p (k j) -> p k j", k=KD), ACT.Copy))
                    proj_ps.release(n, xnT_mark)
                yield
                T.wait(xnT_mark, w_ready)
                while b >= 2 and ("finished", b - 2) not in made:
                    yield BLOCKED

                def channels(ps, at, col, width):
                    for k in range(KD):
                        f = lambda e, k=k: e.matmul(ps[0:width, at:at + L], w_in[:, k, col:col + width], xnT[:, k, :], start=(k == 0), stop=(k == KD - 1))
                        T.run(f) if k < KD - 1 else None
                    return T.do(f)

                def step_sizes():
                    n, ps = proj_ps.take(T)
                    m = channels(ps, 0, HID + CONV, NH)
                    yield
                    S.wait(m, last.get("dtT"))
                    u_mark = m = S.do(lambda e, ps=ps: e.activation(dtT[:, 0, :], ps[0:NH, 0:L], ACT.Identity, bias=head_w[:, 0:1]))
                    proj_ps.release(n, m)
                    S.wait(m)
                    m = S.do(lambda e: e.activation(dtT[:, 1, :], dtT[:, 0, :], ACT.Abs))
                    yield
                    S.wait(m)
                    e_mark = S.do(lambda e: e.activation(dtT[:, 2, :], dtT[:, 1, :], ACT.Exp, scale=-1.0))
                    S.wait(e_mark)
                    ln_mark = S.do(lambda e: e.activation(dtT[:, 3, :], dtT[:, 2, :], ACT.Ln, bias=1.0))
                    yield
                    V.wait(e_mark, u_mark)
                    m = V.do(lambda e: e.tensor_scalar(dtT[:, 4, :], dtT[:, 2, :], 1.0, None, ALU.add))
                    V.wait(m, ln_mark)
                    m = V.do(lambda e: e.scalar_tensor_tensor(dtT[:, 1, :], dtT[:, 4, :], 1.0, dtT[:, 2, :], ALU.subtract, ALU.subtract))
                    V.wait(m)
                    m = V.do(lambda e: e.reciprocal(dtT[:, 4, :], dtT[:, 4, :]))
                    yield
                    V.wait(m)
                    m = V.do(lambda e: e.scalar_tensor_tensor(dtT[:, 1, :], dtT[:, 1, :], -1.0, dtT[:, 4, :], ALU.mult, ALU.mult))
                    V.wait(m)
                    m = V.do(lambda e: e.tensor_tensor(dtT[:, 1, :], dtT[:, 1, :], dtT[:, 3, :], ALU.add))
                    V.wait(m)
                    dt_mark = m = V.do(lambda e: e.scalar_tensor_tensor(dtT[:, 5, :], dtT[:, 0, :], 0.0, dtT[:, 1, :], ALU.max, ALU.add))
                    yield
                    V.wait(m)
                    m = V.do(lambda e: e.tensor_scalar(dtT[:, 1, :], dtT[:, 5, :], head_w[:, 3:4], None, ALU.mult))
                    V.wait(m)
                    for c in range(TPB):
                        m = V.do(lambda e, c=c: e.tensor_tensor_scan(dtT[:, 6, c * P:(c + 1) * P], ones[0:NH, 0:1].to_broadcast([NH, P]), dtT[:, 1, c * P:(c + 1) * P], 0.0, ALU.mult, ALU.add))
                    cumT_mark = m
                    yield
                    V.wait(m, last.get("cum3"))
                    for s in range(3):
                        src = dtT[:, 6, :] if s == 0 else rest[:, s - 1, :]
                        part = cum3[:, s, :, :].rearrange("h c j -> h (c j)")
                        m = V.do(lambda e, part=part, src=src: e.tensor_copy(part, src))
                        V.wait(m)
                        if s < 2:
                            m = V.do(lambda e, s=s, part=part, src=src: e.tensor_tensor(rest[:, s, :], src, part, ALU.subtract))
                            V.wait(m)
                            yield
                    Y.wait(m)
                    m = store_cum.start(Y, scratch[par].rearrange("s h c j -> h s c j"), cum3[:, :, :, :])
                    Y.wait(m, last.get(("decay operands", par)))
                    last["cum3"] = m
                    for c in range(TPB):
                        m = load_cum.start(Y, RT[par][0:3 * NG, c, :].rearrange("p (h i) -> p h i", h=HG),
                                           scratch[par].rearrange("s (g h) c i -> (s g) c h i", h=HG)[:, c, :, :])
                        for s in range(3):
                            m = load_cum.start(Y, LT[par][3 * NG + HG * s:3 * NG + HG * (s + 1), c, :, :],
                                               scratch[par].rearrange("s (g h) c j -> s c h g j", h=HG)[s, c, :, :, :])
                    Y.wait(m)
                    made["decay operands", b] = m
                    S.wait(cumT_mark, last.get("wdecT"), last.get(("ecum", par)))
                    m = S.do(lambda e: e.activation(wdecT[:, :], dtT[:, 6, 0:P], ACT.Exp, bias=dtT[:, 6, P - 1:P], scale=-1.0))
                    made["ecum", b] = S.do(lambda e: e.activation(ecum[:, :], dtT[:, 6, P:2 * P], ACT.Exp))
                    yield
                    V.wait(m, dt_mark)
                    wdec_mark = V.do(lambda e: e.tensor_tensor(wdecT[:, :], wdecT[:, :], dtT[:, 5, 0:P], ALU.mult))
                    yield
                    n, ps = proj_ps.take(T)
                    T.wait(dt_mark, wdec_mark)
                    for c in range(TPB):
                        T.run(lambda e, c=c, ps=ps: e.transpose(ps[:, c * NH:(c + 1) * NH], dtT[:, 5, c * P:(c + 1) * P], ident[0:NH, 0:NH]))
                    m = T.do(lambda e, ps=ps: e.transpose(ps[:, TPB * NH:(TPB + 1) * NH], wdecT[:, :], ident[0:NH, 0:NH]))
                    last["wdecT"] = last["dtT"] = m
                    yield
                    S.wait(m, last.get(("dt_tok", par)))
                    S.do(lambda e, ps=ps: e.activation(dt_tok[:, :, :].rearrange("p c h -> p (c h)"), ps[:, 0:TPB * NH], ACT.Copy))
                    m = S.do(lambda e, ps=ps: e.activation(wdec_tok[:, :], ps[:, TPB * NH:(TPB + 1) * NH], ACT.Copy))
                    proj_ps.release(n, m)
                    made["dt_tok", b] = m
                    yield

                def conv_project(c0, at):
                    at["n"], at["ps"] = n, ps = proj_ps.take(T)
                    for c in (c0, c0 + 1):
                        at["m"] = channels(ps, (c - c0) * L, HID + c * P, P)

                def conv_copy(c0, at):
                    at["rn"], raw = at["rn"], at["raw"] = raw_in.take(S)
                    raw, ps = at["raw"], at["ps"]
                    S.wait(at["m"])
                    at["m"] = S.do(lambda e: e.activation(raw[:, :, TAPS - 1:TAPS - 1 + L], ps[:, :].rearrange("p (c t) -> p c t", c=2), ACT.Copy))
                    proj_ps.release(at["n"], at["m"])

                def conv_taps(c0, at):
                    at["cn"], at["conv"] = conv_out.take(V)
                    raw, conv, m = at["raw"], at["conv"], at["m"]
                    for k in range(TAPS):
                        V.wait(m)
                        for c in (c0, c0 + 1):
                            o, i, w = conv[:, c - c0, :], raw[:, c - c0, k:k + L], conv_w[:, c, k:k + 1]
                            if k == 0:
                                f = lambda e, o=o, i=i, w=w: e.tensor_scalar(o, i, w, None, ALU.mult)
                            else:
                                f = lambda e, o=o, i=i, w=w: e.scalar_tensor_tensor(o, i, w, o, ALU.mult, ALU.add)
                            m = V.do(f)
                    at["m"] = m
                    raw_in.release(at["rn"], m)

                def conv_tanh(c0, at):
                    conv = at["conv"]
                    S.wait(at["m"], *last.get(("x|B|C", par), ()))
                    at["m"] = S.do(lambda e: e.activation(xbc[par][:, c0:c0 + 2, :], conv[:, :, :], ACT.Tanh))

                def conv_gate(c0, at):
                    conv = at["conv"]
                    V.wait(at["m"])
                    m = V.do(lambda e: e.scalar_tensor_tensor(xbc[par][:, c0:c0 + 2, :], xbc[par][:, c0:c0 + 2, :], 1.0, conv[:, :, :], ALU.add, ALU.mult))
                    conv_out.release(at["cn"], m)
                    made["x|B|C", b] = m

                for _ in together(step_sizes(), pipeline(list(range(0, NCX, 2)), [conv_project, conv_copy, conv_taps, conv_tanh, conv_gate])):
                    yield
                made["x|B|C all", b] = made["x|B|C", b]

                T.wait(half_z)
                def z_project(c0, at):
                    at["n"], at["ps"] = n, ps = proj_ps.take(T)
                    for c in (c0, c0 + 1):
                        at["m"] = channels(ps, (c - c0) * L, c * P, P)

                def z_tanh(c0, at):
                    ps = at["ps"]
                    S.wait(at["m"], last.get(("z", par)))
                    at["m"] = S.do(lambda e: e.activation(zs[par][:, c0:c0 + 2, :], ps[:, :].rearrange("p (c t) -> p c t", c=2), ACT.Tanh))

                def z_gate(c0, at):
                    ps = at["ps"]
                    V.wait(at["m"])
                    m = V.do(lambda e: e.scalar_tensor_tensor(zs[par][:, c0:c0 + 2, :], zs[par][:, c0:c0 + 2, :], 1.0, ps[:, :].rearrange("p (c t) -> p c t", c=2), ALU.add, ALU.mult))
                    proj_ps.release(at["n"], m)
                    made["z", b] = m

                for _ in pipeline(list(range(0, NCZ, 2)), [z_project, z_tanh, z_gate]):
                    yield
                last["xnT"] = made["z", b]
                made["z all", b] = made["z", b]

            def prepare(b, c, hf):
                par, tok = b % 2, slice(c * P, (c + 1) * P)
                dt_tok, wdec_tok = dt_tokens[par], wdec_tokens[par]
                while ("x|B|C all", b) not in made or ("dt_tok", b) not in made:
                    yield BLOCKED
                T.wait(made["x|B|C", b])
                if hf == 0:
                    while misc_ps.busy():
                        yield
                    n, ps = misc_ps.take(T)
                    if c == 0:
                        T.run(lambda e: e.transpose(ps[:, P:2 * P], xbc[par][:, NCZ, 0:P], ident[:, :]))
                    m = T.do(lambda e: e.matmul(ps[:, 0:P], xbc[par][:, NCZ, tok], xbc[par][:, NCZ + 1, tok], start=True, stop=True))
                    yield
                    V.wait(m, last.get(("cbm", c)))
                    m = V.do(lambda e: e.tensor_copy(cbm[c][:, :], ps[:, 0:P]))
                    made["cbm", b, c] = m
                    if c == 0:
                        V.wait(last.get("b_tok"))
                        made["b_tok", b] = m = V.do(lambda e: e.tensor_copy(b_tok[:, :], ps[:, P:2 * P]))
                    misc_ps.release(n, m)
                    yield
                while misc_ps.busy():
                    yield
                n, ps = misc_ps.take(T)
                for k in range(4):
                    f = lambda e, k=k, ps=ps: e.transpose(ps[:, k * P:(k + 1) * P], xbc[par][:, 4 * hf + k, tok], ident[:, :])
                    T.run(f) if k < 3 else None
                m = T.do(f)
                last["x|B|C read", b] = m
                yield
                hs = slice(hf * NH // 2, (hf + 1) * NH // 2)
                V.wait(m, last.get(("xdt", hf)), made["dt_tok", b])
                for odd in range(2):
                    o = xdt[hf][:, :, :].rearrange("p (q two) w -> p q two w", two=2)[:, :, odd, odd * HP:(odd + 1) * HP]
                    i0 = ps[:, :].rearrange("p (q two w) -> p q two w", two=2, w=HP)[:, :, odd, :]
                    i1 = dt_tok[:, c, hs].rearrange("p (q two) -> p q two", two=2)[:, :, odd:odd + 1].to_broadcast([P, NH // 4, HP])
                    m = V.do(lambda e, o=o, i0=i0, i1=i1: e.tensor_tensor(o, i0, i1, ALU.mult))
                made["xdt", b, c, hf] = m
                if c == 0:
                    V.wait(last.get("xw"))
                    i1 = wdec_tok[:, hs].rearrange("p (h o) -> p h o", o=1).to_broadcast([P, NH // 2, HP])
                    made["xw", b, hf] = m = V.do(lambda e: e.tensor_tensor(xw[:, hs, :], ps[:, :].rearrange("p (h w) -> p h w", w=HP), i1, ALU.mult))
                misc_ps.release(n, m)
                last["dt_tok", par] = m
                yield

            def finish(b, c, hf):
                par, tok, tile = b % 2, slice(c * P, (c + 1) * P), b * TPB + c
                yn, yps, ymark = made["y", b, c, hf]
                cts = slice(4 * hf, 4 * hf + 4)
                if c == 0:
                    T.wait(made["xw", b, hf], made["b_tok", b])
                    while misc_ps.busy():
                        yield
                    n, ps = misc_ps.take(T)
                    m = T.do(lambda e: e.matmul(ps[:, :], b_tok[:, :], xw[:, hf * NH // 2:(hf + 1) * NH // 2, :].rearrange("p h w -> p (h w)"), start=True, stop=True))
                    last["b_tok"] = last["xw"] = m
                    yield
                    S.wait(m, last.get(("state", hf)))
                    made["state", b, hf] = m = S.do(lambda e: e.activation(state[:, hf * 512:(hf + 1) * 512], ps[:, :], ACT.Copy))
                    misc_ps.release(n, m)
                    ysum, src = ymark, yps
                else:
                    T.wait(made["state", b, hf], made["ecum", b])
                    while misc_ps.busy():
                        yield
                    n, ps = misc_ps.take(T)
                    for k in range(4):
                        f = lambda e, k=k, ps=ps: e.matmul(ps[:, k * P:(k + 1) * P], expand[:, 4 * hf + k, :], ecums[par][:, :], start=True, stop=True)
                        T.run(f) if k < 3 else None
                    last["ecum", par] = m = T.do(f)
                    yield
                    S.wait(m, last.get("eexp"))
                    ee = S.do(lambda e, ps=ps: e.activation(eexp[:, :], ps[:, :], ACT.Copy))
                    misc_ps.release(n, ee)
                    yield
                    while misc_ps.busy():
                        yield
                    n, ps = misc_ps.take(T)
                    for k in range(4):
                        f = lambda e, k=k, ps=ps: e.matmul(ps[:, k * P:(k + 1) * P], state[:, (4 * hf + k) * P:(4 * hf + k + 1) * P], xbc[par][:, NCZ + 1, tok], start=True, stop=True)
                        T.run(f) if k < 3 else None
                    last["state", hf] = m = T.do(f)
                    last["C", b] = m
                    yield
                    V.wait(m, ee)
                    m = V.do(lambda e, ps=ps: e.tensor_tensor(eexp[:, :], ps[:, :], eexp[:, :], ALU.mult))
                    misc_ps.release(n, m)
                    V.wait(m, ymark)
                    ysum = V.do(lambda e: e.tensor_tensor(eexp[:, :], eexp[:, :], yps[:, :], ALU.add))
                    y_ps.release(yn, ysum)
                    src = eexp
                yield
                V.wait(ysum, last.get("yz"), last.get("eexp"))
                for k in range(4):
                    ct = 4 * hf + k
                    m = V.do(lambda e, k=k, ct=ct: e.scalar_tensor_tensor(
                        yz[:, ct, :], xbc[par][:, ct, tok], d_w[:, ct:ct + 1], src[:, k * P:(k + 1) * P], ALU.mult, ALU.add))
                if c == 0:
                    y_ps.release(yn, m)
                V.wait(m, made["z", b])
                yz_mark = V.do(lambda e: e.tensor_tensor(yz[:, cts, :], yz[:, cts, :], zs[par][:, cts, tok], ALU.mult))
                yield
                S.wait(yz_mark)
                m = S.do(lambda e: e.activation(eexp[:, :].rearrange("p (c j) -> p c j", j=P), yz[:, cts, :], ACT.Square))
                yield
                G.wait(m)
                m = G.do(lambda e: e.tensor_tensor(eexp[:, 0:2 * P], eexp[:, 0:2 * P], eexp[:, 2 * P:4 * P], ALU.add))
                G.wait(m)
                m = G.do(lambda e: e.tensor_tensor(eexp[:, 0:P], eexp[:, 0:P], eexp[:, P:2 * P], ALU.add))
                yield
                yield
                while misc_ps.busy():
                    yield
                n, ps = misc_ps.take(T)
                T.wait(m)
                f = lambda e, ps=ps: e.matmul(ps[:, 0:1], eexp[:, 0:P], ones[:, 0:1], start=True, stop=True)
                last["eexp"] = m = T.do(f)
                yield
                V.wait(m)
                if hf == 0:
                    m = V.do(lambda e, ps=ps: e.tensor_copy(rstats[:, 3:4], ps[:, 0:1]))
                else:
                    m = V.do(lambda e, ps=ps: e.tensor_tensor(rstats[:, 0:1], ps[:, 0:1], rstats[:, 3:4], ALU.add))
                    V.wait(m)
                misc_ps.release(n, m)
                if c == TPB - 1 and hf == 1:
                    last["x|B|C", par] = (yz_mark, last["C", b], last["x|B|C read", b])
                    last["z", par] = yz_mark
                    made["finished", b] = yz_mark
                if hf == 0:
                    return
                on, ops = out_ps.take(T)
                for ct in range(NCZ):
                    if ct % 2 == 0:
                        yield
                    if ct == 0:
                        T.wait(yz_mark, normed_out)
                    f = lambda e, ct=ct: e.matmul(ops[:, :], yz[:, ct, :], w_out[:, ct, :], start=(ct == 0), stop=(ct == NCZ - 1))
                    T.run(f) if ct < NCZ - 1 else None
                out_mark = T.do(f)
                last["yz"] = out_mark
                yield
                m = V.do(lambda e: e.tensor_scalar(rstats[:, 0:1], rstats[:, 0:1], 1.0 / HID, RMS_EPS, ALU.mult, ALU.add))
                for m in rsqrt(rstats[:, 0:1], rstats[:, 1:2], rstats[:, 2:3], m):
                    yield
                V.wait(m, out_mark)
                m = V.do(lambda e: e.scalar_tensor_tensor(x_sb[:, tile, :], ops[:, :], rstats[:, 1:2], x_sb[:, tile, :], ALU.mult, ALU.add))
                out_ps.release(on, m)
                x_ready[tile] = m
                yield

            def group_decay(s, at):
                b, c, hf = UNITS[s // NHALF]
                par, g = b % 2, hf * NHALF + s % NHALF
                at["n"], at["ps"] = n, ps = decay_ps.take(T)
                T.wait(made["decay operands", b])
                T.run(lambda e: e.matmul(ps[:, :], identb[:, :], future[:, :].rearrange("p (o i) -> p o i", o=1).to_broadcast([P, HG, P]), start=True, stop=False))
                at["m"] = T.do(lambda e: e.matmul(ps[:, :], LT[par][0:DROWS, c, g, :], RT[par][0:DROWS, c, :], start=False, stop=True))
                last["decay operands", par] = at["m"]

            def group_exp(s, at):
                at["r"], at["buf"] = decay.take(S)
                ps, buf = at["ps"], at["buf"]
                S.wait(at["m"])
                at["m"] = S.do(lambda e: e.activation(buf[:, :], ps[:, :], ACT.Exp))
                decay_ps.release(at["n"], at["m"])

            def group_mix(s, at):
                b, c, hf = UNITS[s // NHALF]
                at["q"], at["mix"] = mix.take(V)
                buf, out_buf = at["buf"], at["mix"]
                V.wait(at["m"], made["cbm", b, c])
                cb = cbm[c][:, :].rearrange("p (o i) -> p o i", o=1).to_broadcast([P, HG, P])
                at["m"] = V.do(lambda e: e.tensor_tensor(out_buf[:, :].rearrange("p (h i) -> p h i", h=HG), buf[:, :].rearrange("p (h i) -> p h i", h=HG), cb, ALU.mult))
                last["cbm", c] = at["m"]
                decay.release(at["r"], at["m"])
                held.append(at)

            held, ybank = [], {}

            def group_heads(s, at):
                if s % 2 == 0:
                    return
                b, c, hf = u = UNITS[s // NHALF]
                if s % NHALF == 1:
                    ybank["now"] = y_ps.take(T)
                yn, yps = ybank["now"]
                two = [held.pop(0), held.pop(0)]
                T.wait(two[1]["m"], made["xdt", b, c, hf])
                ct = s % NHALF // 2
                for odd in range(2):
                    for quad in range(4):
                        h = 2 * quad + odd
                        buf = two[h // HG]["mix"]
                        f = lambda e, h=h, odd=odd, quad=quad, buf=buf: e.matmul(
                            yps[32 * quad:32 * quad + 32, ct * P:(ct + 1) * P], xdt[hf][:, 2 * HG * ct + h, :], buf[:, h % HG * P:(h % HG + 1) * P],
                            start=(odd == 0), stop=(odd == 1), tile_position=(0, 32 * quad))
                        T.run(f) if (odd, quad) != (1, 3) else None
                m = T.do(f)
                for x in two:
                    mix.release(x["q"], m)
                last["xdt", hf] = m
                made[("y",) + u] = (yn, yps, m)

            def advance(sides):
                for g in list(sides):
                    if next(g, "end") == "end":
                        sides.remove(g)

            def mixer():
                n = len(UNITS) * NHALF
                main = pipeline(list(range(n)), [group_decay, group_exp, group_mix, group_heads])
                sides = [prepare(*UNITS[0])]
                for s in range(n + 3):
                    u, k = divmod(s, NHALF)
                    if k == 3:
                        if u >= 1:
                            sides.append(finish(*UNITS[u - 1]))
                        if u + 1 < len(UNITS):
                            sides.append(prepare(*UNITS[u + 1]))
                    if k == 1 and u < len(UNITS):
                        while ("xdt",) + UNITS[u] not in made:
                            for g in list(sides):
                                r = next(g, "end")
                                if r == "end":
                                    sides.remove(g)
                                elif r == BLOCKED:
                                    yield BLOCKED
                    if u < len(UNITS):
                        while ("decay operands", UNITS[u][0]) not in made:
                            yield BLOCKED
                    advance(sides)
                    next(main)
                    advance(sides)
                    yield
                sides.append(finish(*UNITS[-1]))
                for g in sides:
                    for _ in g:
                        yield

            def projects():
                for b in range(NB):
                    yield from project(b)

            alternate((mixer(), 260), (projects(), 8 * 30))
            barrier()

        with ExitStack() as st:
            ssm_mixer(st)

        logit = sb(top, "logit", [P, NT, NE])
        r_in = sb(top, "r_in", [P, NT])
        w_router = sb(top, "w_router", [P, KD, NE])
        s_router = sb(top, "s_router", [P, KD])

        def cross_attention(st):
            bank = lambda name, shape=[P, 512], dt=F32: st.enter_context(nc.psum_tensor(name, shape, dt))
            max_ps = Ring([bank("max_ps0", [P, 1024]), bank("max_ps1", [P, 1024])])
            score_ps = Ring([bank("score_ps0"), bank("score_ps1")])
            pv_ps = Ring([bank("pv_ps0")])
            turn_ps = Ring([bank("turn_ps0")])

            NPR = QH // 2
            PARTS = 3 * DH
            xn = sb(st, "a_xn", [P, DIM])
            stats = sb(st, "a_stats", [P, 24])
            q_st = sb(st, "q_st", [P, QH, SLOT], F16)
            k_st = sb(st, "k_st", [P, KVH, 2, SLOT], F16)
            ctx = [sb(st, f"ctx{i}", [P, TPB, KVH, DH]) for i in range(2)]
            v_aug = [sb(st, f"v_aug{i}", [P, TPB, KVH, 32]) for i in range(2)]
            qT = [sb(st, f"qT{i}", [P, NPR, L], F16) for i in range(2)]
            kT = [sb(st, f"kT{i}", [P, KVH, L], F16) for i in range(2)]
            maxes = sb(st, "maxes", [P, TPB, QH])
            nmax = sb(st, "nmax", [P, TPB, QH], F16)
            nmaxT = [sb(st, f"nmaxT{i}", [QH, L], F16) for i in range(2)]
            prob = Ring([sb(st, f"prob{i}", [P, 512]) for i in range(8)])
            pv = Ring([sb(st, f"pv{i}", [P, 512]) for i in range(2)])
            recip = sb(st, "recip", [P, 4, 4])
            o_tok = [sb(st, f"o_tok{i}", [P, TPB, DIM]) for i in range(2)]

            load_ctx = Load(semaphore("load_ctx"))
            load_max = Load(semaphore("load_max"))
            for i in range(2):
                V.do(lambda e, i=i: e.memset(v_aug[i][:, :, :, :], 0.0))
            m = V.do(lambda e: e.memset(k_st[:, :, :, :], 0.0))
            m2 = V.do(lambda e: e.memset(q_st[:, :, :], 0.0))
            V.wait(m, m2)
            for i in range(2):
                V.do(lambda e, i=i: e.memset(v_aug[i][:, :, :, DH:DH + 1], 1.0))
            init = V.do(lambda e: e.memset(k_st[:, :, :, PARTS:PARTS + 1], 1.0))
            for e in (T, S, V, G):
                e.wait(init)
            made = {}
            last = {}

            def heads_in(b):
                par = b % 2
                Y.wait(last.get(("ctx", par)))
                cm = load_ctx.start(Y, ctx[par][:, :, :, :].rearrange("p t k d -> p t (k d)"), ctx_rows[:, b * TPB:(b + 1) * TPB, :])
                Y.wait(cm)
                for nm in norm_factors(b, stats):
                    yield
                if b >= 2:
                    while ("attended", b - 2) not in made:
                        yield BLOCKED
                for t in range(TPB):
                    kv = ctx[par][:, t, :, :]
                    both = kv.rearrange("p k (o d) -> p k o d", o=1).to_broadcast([P, KVH, 2, DH])
                    S.wait(cm, last.get("k_st"))
                    S.do(lambda e, both=both: e.activation(k_st[:, :, :, 0:DH], both, ACT.Copy))
                    m = S.do(lambda e, both=both: e.activation(k_st[:, :, :, 2 * DH:3 * DH], both, ACT.Copy))
                    yield
                    V.wait(cm, m)
                    m = V.do(lambda e, both=both: e.tensor_tensor(k_st[:, :, :, DH:2 * DH], both, k_st[:, :, :, 0:DH], ALU.subtract))
                    G.wait(cm, last.get(("v", par)) if t == 0 else None)
                    vm = G.do(lambda e, kv=kv, t=t: e.tensor_copy(v_aug[par][:, t, :, 0:DH], kv))
                    yield
                    while turn_ps.busy():
                        yield
                    n, ps = turn_ps.take(T)
                    T.wait(m)
                    ps16 = ps[:, :].bitcast(F16)
                    for k in range(KVH):
                        f = lambda e, k=k, ps16=ps16: e.transpose(ps16[:, k * P:(k + 1) * P], k_st[:, k, :, :].rearrange("p a s -> p (a s)"), ident16[:, :])
                        T.run(f) if k < KVH - 1 else None
                    last["k_st"] = m = T.do(f)
                    yield
                    V.wait(m, last.get(("kT", par)) if t == 0 else None)
                    km = V.do(lambda e, ps16=ps16, t=t: e.tensor_copy(kT[par][:, :, t * P:(t + 1) * P], ps16.rearrange("p (k j) -> p k j", j=P)))
                    turn_ps.release(n, km)
                    yield
                last["ctx", par] = vm
                made["v", b], made["kT", b] = vm, km
                q_marks = [None, None]
                for t in range(TPB):
                    tile = b * TPB + t
                    V.wait(nm, last.get("xn"))
                    m = V.do(lambda e, t=t, tile=tile: normalise(e, xn[:, :], tile, stats, t))
                    q = xn[:, :].rearrange("p (h d) -> p h d", d=DH)
                    yield
                    S.wait(m, last.get("q_st"))
                    m = S.do(lambda e, q=q: e.activation(q_st[:, :, 0:DH], q, ACT.Copy))
                    yield
                    V.wait(m)
                    last["xn"] = m = V.do(lambda e, q=q: e.tensor_tensor(q_st[:, :, 2 * DH:3 * DH], q, q_st[:, :, 0:DH], ALU.subtract))
                    G.wait(m, last.get("q_st"))
                    gm = G.do(lambda e: e.tensor_copy(q_st[:, :, DH:2 * DH], q_st[:, :, 0:DH]))
                    yield
                    yield
                    T.wait(m, gm)
                    for half in range(2):
                        while turn_ps.busy():
                            yield
                        n, ps = turn_ps.take(T)
                        ps16 = ps[:, :].bitcast(F16)
                        for k in range(NPR // 2):
                            pr = half * NPR // 2 + k
                            f = lambda e, k=k, pr=pr, ps16=ps16: e.transpose(ps16[:, k * P:(k + 1) * P], q_st[:, 2 * pr:2 * pr + 2, :].rearrange("p a s -> p (a s)"), ident16[:, :])
                            T.run(f) if k < NPR // 2 - 1 else None
                        last["q_st"] = m = T.do(f)
                        yield
                        E_ = S if half else V
                        out_ = qT[par][:, half * NPR // 2:(half + 1) * NPR // 2, t * P:(t + 1) * P]
                        in_ = ps16.rearrange("p (k j) -> p k j", j=P)
                        E_.wait(m, last.get(("qT", par)) if t == 0 else None)
                        qm = E_.do((lambda e, o=out_, i=in_: e.activation(o, i, ACT.Copy)) if half else (lambda e, o=out_, i=in_: e.tensor_copy(o, i)))
                        turn_ps.release(n, qm)
                        q_marks[half] = qm
                        yield
                T.wait(km, *q_marks)

                def max_scores(tk, at):
                    t, k = tk
                    at["n"], at["ps"] = n, ps = max_ps.take(T)
                    for i in range(4):
                        pr, base, col = 2 * k + i // 2, SLOT * (i % 2), (i % 2 * 2 + i // 2) * L
                        f = lambda e, pr=pr, base=base, col=col: e.matmul(
                            ps[:, col:col + L], qT[par][base:base + PARTS, pr, t * P:(t + 1) * P], kT[par][base:base + PARTS, k, :], start=True, stop=True)
                        T.run(f) if i < 3 else None
                    at["m"] = T.do(f)

                def max_reduce(tk, at):
                    t, k = tk
                    ps = at["ps"]
                    V.wait(at["m"])
                    m = V.do(lambda e: e.reduce_max(maxes[:, t, 4 * k:4 * k + 4], ps[:, :].rearrange("p (h t) -> p h t", h=4), AX.X))
                    max_ps.release(at["n"], m)
                    made["maxes"] = m

                for _ in pipeline([(t, k) for t in range(TPB) for k in range(KVH)], [max_scores, max_reduce]):
                    yield
                V.wait(made["maxes"], last.get("nmax"))
                for t in range(TPB):
                    for odd in range(2):
                        m = V.do(lambda e, t=t, odd=odd: e.tensor_scalar(nmax[:, t, odd * NPR:(odd + 1) * NPR].rearrange("p (k hh) -> p k hh", hh=2), maxes[:, t, :].rearrange("p (k odd hh) -> p k odd hh", odd=2, hh=2)[:, :, odd, :], -1.0, None, ALU.mult))
                yield
                while turn_ps.busy():
                    yield
                n, ps = turn_ps.take(T)
                ps16 = ps[:, :].bitcast(F16)
                T.wait(m)
                T.run(lambda e, ps16=ps16: e.transpose(ps16[0:QH, 0:P], nmax[:, 0, :], ident16[:, :]))
                last["nmax"] = m = T.do(lambda e, ps16=ps16: e.transpose(ps16[0:QH, P:2 * P], nmax[:, 1, :], ident16[:, :]))
                yield
                V.wait(m, last.get(("nmaxT", par)))
                m = V.do(lambda e, ps16=ps16: e.tensor_copy(nmaxT[par][:, :], ps16[0:QH, 0:L]))
                turn_ps.release(n, m)
                Y.wait(m)
                for odd in range(2):
                    row = SLOT * odd + PARTS
                    m = load_max.start(Y, qT[par][row:row + 1, :, :], nmaxT[par][odd * NPR:(odd + 1) * NPR, :])
                Y.wait(m)
                last["nmaxT", par] = m
                made["qT", b] = m
                yield

            ITEMS = [(b, kh, odd, t, quad) for b in range(NB) for kh in range(2) for odd in range(2) for t in range(TPB) for quad in range(4)]
            held = []

            def score(item, at):
                b, kh, odd, t, quad = item
                par, base, k = b % 2, SLOT * odd, 4 * kh + quad
                at["n"], at["ps"] = n, ps = score_ps.take(T)
                T.wait(made["qT", b], made["v", b], made["kT", b])
                at["m"] = T.do(lambda e: e.matmul(ps[:, :], kT[par][base:base + PARTS + 1, k, t * P:(t + 1) * P],
                                                  qT[par][base:base + PARTS + 1, 2 * k:2 * k + 2, :], start=True, stop=True))
                last["kT", par] = last["qT", par] = at["m"]

            def exponent(item, at):
                ps = at["ps"]
                at["r"], at["buf"] = r, buf = prob.take(S)
                S.wait(at["m"])
                at["m"] = S.do(lambda e: e.activation(buf[:, :], ps[:, :], ACT.Exp, scale=DH ** -0.5))
                score_ps.release(at["n"], at["m"])
                held.append((item, at))

            pv_bank = {}

            def product(item, at):
                b, kh, odd, t, quad = item
                if quad != 3:
                    return
                par = b % 2
                if t == 0:
                    pv_bank["now"] = pv_ps.take(T)
                vn, vps = pv_bank["now"]
                four = [held.pop(0)[1] for _ in range(4)]
                T.wait(four[3]["m"])
                for q, x in enumerate(four):
                    f = lambda e, q=q, buf=x["buf"]: e.matmul(
                        vps[32 * q:32 * q + 32, :], v_aug[par][:, t, 4 * kh + q, :], buf[:, :],
                        start=(t == 0), stop=(t == TPB - 1), tile_position=(0, 32 * q))
                    T.run(f) if q < 3 else None
                m = T.do(f)
                for x in four:
                    prob.release(x["r"], m)
                last["v", par] = m
                if t == TPB - 1:
                    sides.append(weighted(b, kh, odd, vn, vps, m))

            def weighted(b, kh, odd, vn, vps, m):
                par = b % 2
                r, pbuf = pv.take(S)
                S.wait(m)
                m = S.do(lambda e: e.activation(pbuf[:, :], vps[:, :], ACT.Copy))
                pv_ps.release(vn, m)
                yield
                yield
                while turn_ps.busy():
                    yield
                n, ps = turn_ps.take(T)
                T.wait(m)
                for i in range(4):
                    f = lambda e, i=i: e.transpose(ps[:, i * P:(i + 1) * P], pbuf[:, i * P:(i + 1) * P], ident[:, :])
                    T.run(f) if i < 3 else None
                m = T.do(f)
                pv.release(r, m)
                yield
                V.wait(m, last.get("recip"))
                m = V.do(lambda e: e.reciprocal(recip[:, :, :], ps[:, :].rearrange("p (b q w) -> p b q w", b=4, q=4)[:, :, :, DH]))
                V.wait(m, last.get(("o_tok", par)))
                for t in range(TPB):
                    cols = o_tok[par][:, t, :].rearrange("p (kh q hh odd d) -> p kh q hh odd d", kh=2, q=4, hh=2, odd=2)[:, kh, :, :, odd, :]
                    for hh in range(2):
                        i0 = ps[:, (hh * TPB + t) * P:(hh * TPB + t + 1) * P].rearrange("p (q w) -> p q w", q=4)[:, :, 0:DH]
                        i1 = recip[:, hh * TPB + t, :].rearrange("p (q o) -> p q o", o=1).to_broadcast([P, 4, DH])
                        m = V.do(lambda e, o=cols[:, :, hh, :], i0=i0, i1=i1: e.tensor_tensor(o, i0, i1, ALU.mult))
                last["recip"] = m
                turn_ps.release(n, m)
                yield
                if kh == 1 and odd == 1:
                    G.wait(m)
                    for t in range(TPB):
                        tile = b * TPB + t
                        gm = G.do(lambda e, t=t, tile=tile: e.tensor_tensor(x_sb[:, tile, :], x_sb[:, tile, :], o_tok[par][:, t, :], ALU.add))
                        x_ready[tile] = gm
                    last["o_tok", par] = gm
                    made["attended", b] = gm
                yield

            sides = []

            def attention():
                main = pipeline(ITEMS, [score, exponent, product], lag=2)
                for s in range(len(ITEMS) + 4):
                    if s < len(ITEMS):
                        while ("qT", ITEMS[s][0]) not in made:
                            for g in list(sides):
                                if next(g, "end") == "end":
                                    sides.remove(g)
                            yield BLOCKED
                    next(main)
                    for g in list(sides):
                        if next(g, "end") == "end":
                            sides.remove(g)
                    yield
                while sides:
                    for g in list(sides):
                        if next(g, "end") == "end":
                            sides.remove(g)
                    yield

            def heads():
                for b in range(NB):
                    yield from heads_in(b)

            def routes():
                for b in range(NB):
                    while ("attended", b) not in made:
                        yield BLOCKED
                    yield from route_in(b)

            r_xn = [sb(st, f"r_xn{i}", [P, DIM]) for i in range(2)]
            r_xnT = sb(st, "r_xnT", [P, KD, P])
            r_stats = sb(st, "r_stats", [P, 24])
            junk = sb(st, "junk", [P, DIM])
            r_free = dict(xn=[(), ()], xnT=None, junk=None)
            for dst, src in [
                (w_router[:, :, :], A["L0_ffn_router_logits"].rearrange("(k p) e -> p k e", p=P)),
                (s_router[:, :], A["c_router_scale"]),
            ]:
                r_ready = load_r.start(Y, dst, src)
            V.wait(r_ready)
            for k in range(KD):
                wr_mark = V.do(lambda e, k=k: e.tensor_scalar(w_router[:, k, :], w_router[:, k, :], s_router[:, k:k + 1], None, ALU.mult))

            def route_in(b):
                for nm in norm_factors(b, r_stats):
                    yield
                for t in range(TPB):
                    tile = b * TPB + t
                    i = tile % 2
                    V.wait(nm, *r_free["xn"][i])
                    m = V.do(lambda e, i=i, t=t, tile=tile: normalise(e, r_xn[i][:, :], tile, r_stats, t))
                    Y.wait(m)
                    kept = store_tokens[i].start(Y, tokens[tile * P:(tile + 1) * P, :], r_xn[i][:, :])
                    if tile == NT - 1:
                        kept = store_tokens[i].start(Y, tokens[NT * P:(NT + 1) * P, :], r_xn[i][:, :])
                    yield
                    S.wait(m, r_free["junk"])
                    jm = S.do(lambda e, i=i, tile=tile: e.activation(junk[:, :], r_xn[i][:, :], ACT.Square, accum_out=r_in[:, tile:tile + 1]))
                    r_free["junk"] = jm
                    while turn_ps.busy():
                        yield
                    n, ps = turn_ps.take(T)
                    T.wait(m)
                    for k in range(KD):
                        f = lambda e, k=k, i=i, ps=ps: e.transpose(ps[:, k * P:(k + 1) * P], r_xn[i][:, k * P:(k + 1) * P], ident[:, :])
                        T.run(f) if k < KD - 1 else None
                    m = T.do(f)
                    r_free["xn"][i] = (m, jm, kept)
                    yield
                    S.wait(m, r_free["xnT"])
                    xm = S.do(lambda e, ps=ps: e.activation(r_xnT[:, :, :], ps[:, :].rearrange("p (k j) -> p k j", k=KD), ACT.Copy))
                    turn_ps.release(n, xm)
                    yield
                    while turn_ps.busy():
                        yield
                    n, ps = turn_ps.take(T)
                    T.wait(xm, wr_mark)
                    for k in range(KD):
                        f = lambda e, k=k, ps=ps: e.matmul(ps[:, 0:NE], r_xnT[:, k, :], w_router[:, k, :], start=(k == 0), stop=(k == KD - 1))
                        T.run(f) if k < KD - 1 else None
                    m = T.do(f)
                    r_free["xnT"] = m
                    yield
                    V.wait(m)
                    m = V.do(lambda e, tile=tile, ps=ps: e.tensor_copy(logit[:, tile, :], ps[:, 0:NE]))
                    turn_ps.release(n, m)
                    yield

            alternate((attention(), 32 * NB), (heads(), 44 * NB), (routes(), 12 * NB))
            barrier()

        with ExitStack() as st:
            cross_attention(st)

        def experts(st):
            bank = lambda name, shape=[P, 512], dt=F32: st.enter_context(nc.psum_tensor(name, shape, dt))
            gate_ps = Ring([bank("gate_ps0"), bank("gate_ps1")])
            up_ps = Ring([bank("up_ps0"), bank("up_ps1")])
            turn_ps = Ring([bank("mturn_ps0"), bank("mturn_ps1")])
            down_ps = Ring([bank("down_ps0"), bank("down_ps1")])
            w_gu = sb(st, "w_gu", [P, WR, KD, 2 * EH])
            w_dn = sb(st, "w_dn", [P, WR, KD, DIM])
            e_scale = sb(st, "e_scale", [P, NE])
            lower = sb(st, "lower", [P, NE, NE])
            before = sb(st, "before", [P, P])
            token_id = sb(st, "token_id", [P, NT])
            tile_id = sb(st, "tile_id", [P, MT])
            ones = sb(st, "m_ones", [P, P])
            r_tmp = sb(st, "r_tmp", [P, NT])
            col = sb(st, "col", [P, NT])
            rank = sb(st, "rank", [P, NT, NE])
            sel = [sb(st, f"sel{i}", [P, NT, NE]) for i in range(3)]
            weight = sb(st, "weight", [P, NT, NE])
            wide = [sb(st, f"wide{i}", [P, NT, NE, NE]) for i in range(2)]
            total = sb(st, "total", [P, NT, NE])
            upto = sb(st, "upto", [P, NT, NE])
            counts = sb(st, "counts", [P, 4, NE])
            counts_i = sb(st, "counts_i", [P, 2, NE], mybir.dt.int32)
            slot_f = sb(st, "slot_f", [P, 2, NT])
            slot_i = sb(st, "slot_i", [P, 2, NT], mybir.dt.uint32)
            rows = sb(st, "rows", [P, 2, NT, 2])
            owner_f = sb(st, "owner_f", [P, 3, MT])
            owner = sb(st, "owner", [P, 3, MT], mybir.dt.int32)
            owned = sb(st, "owned", [P, MT, NE])
            back = sb(st, "back", [MT, P, 2])
            ids = sb(st, "ids", [P, MT], mybir.dt.uint32)
            row_w = sb(st, "row_w", [P, MT])
            xg = Ring([sb(st, f"xg{i}", [P, DIM]) for i in range(3)])
            xgT = [sb(st, f"xgT{i}", [P, KD, P]) for i in range(2)]
            gelu = [sb(st, f"gelu{i}", [P, EH]) for i in range(2)]
            act = [sb(st, f"act{i}", [P, EH]) for i in range(2)]
            actT = [sb(st, f"actT{i}", [P, KD, P]) for i in range(2)]
            y_out = Ring([sb(st, f"y_out{i}", [P, DIM]) for i in range(3)])
            load_m = Load(semaphore("load_m"))
            load_e = [Load(semaphore(f"load_e{i}")) for i in range(4)]
            slots_clear = Load(semaphore("slots_clear"))
            slots_put = Load(semaphore("slots_put"))
            slots_get = Load(semaphore("slots_get"))
            out_init = Load(semaphore("out_init"))
            gather = [Load(semaphore(f"gather{i}")) for i in range(3)]
            scatter = Load(semaphore("scatter"))

            gu_dram = A["c_gatingT"].rearrange("e (k p) n -> p e k n", p=P)
            dn_dram = A["L0_ffn_linear"].rearrange("e (k p) n -> p e k n", p=P)
            cleared = slots_clear.start(Y, slots.rearrange("(i p) c -> i (p c)", p=P), A["c_slots"])
            for dst, src in [
                (lower[:, :, :], A["c_lower"].rearrange("p (a b) -> p a b", a=NE)),
                (before[:, :], A["c_before"]),
                (token_id[:, :], A["c_token_id"]),
                (tile_id[:, :], A["c_tile_id"]),
                (e_scale[:, :], A["L0_ffn_per_expert_scale"].rearrange("(o e) -> o e", o=1).to_broadcast([P, NE])),
            ]:
                m_ready = load_m.start(S, dst, src)
            load_e[0].start(Y, w_gu[:, 0, :, :], gu_dram[:, 0, :, :])
            weights_ready = [load_e[0].start(Y, w_dn[:, 0, :, :], dn_dram[:, 0, :, :])]
            for t in range(NT):
                Y.wait(x_ready[t])
                out_init.start(Y, out[t * P:(t + 1) * P, :], x_sb[:, t, :])
            residual_out = out_init.start(Y, out[NT * P:(NT + 1) * P, :], x_sb[:, 0, :])

            V.wait(m_ready)
            V.do(lambda e: e.memset(ones[:, :], 1.0))
            m = V.do(lambda e: e.tensor_scalar(r_in[:, :], r_in[:, :], 1.0 / DIM, ROUTER_EPS, ALU.mult, ALU.add))
            for m in rsqrt(r_in[:, :], col[:, :], r_tmp[:, :], m):
                pass
            V.wait(m)
            m = V.do(lambda e: e.tensor_scalar(r_in[:, :], col[:, :], float(np.float32(DIM) ** np.float32(-0.5)), None, ALU.mult))
            V.wait(m)
            over_e = lambda a: a.rearrange("p (t o) -> p t o", o=1).to_broadcast([P, NT, NE])
            over_t = lambda a: a.rearrange("p (o e) -> p o e", o=1).to_broadcast([P, NT, NE])
            step = lambda f: V.wait(V.do(f))
            step(lambda e: e.tensor_tensor(logit[:, :, :], logit[:, :, :], over_e(r_in[:, :]), ALU.mult))
            la = logit[:, :, :].rearrange("p t (e o) -> p t e o", o=1).to_broadcast([P, NT, NE, NE])
            lb = logit[:, :, :].rearrange("p t (o e) -> p t o e", o=1).to_broadcast([P, NT, NE, NE])
            low = lower[:, :, :].rearrange("p (o a) b -> p o a b", o=1).to_broadcast([P, NT, NE, NE])
            V.do(lambda e: e.tensor_tensor(wide[0][:, :, :, :], lb, la, ALU.is_gt))
            step(lambda e: e.tensor_tensor(wide[1][:, :, :, :], lb, la, ALU.is_equal))
            step(lambda e: e.tensor_tensor(wide[1][:, :, :, :], wide[1][:, :, :, :], low, ALU.mult))
            step(lambda e: e.tensor_tensor(wide[0][:, :, :, :], wide[0][:, :, :, :], wide[1][:, :, :, :], ALU.add))
            step(lambda e: e.reduce_sum(rank[:, :, :], wide[0][:, :, :, :], AX.X))
            V.do(lambda e: e.tensor_scalar(sel[0][:, :, :], rank[:, :, :], 0.0, None, ALU.is_equal))
            V.do(lambda e: e.tensor_scalar(sel[1][:, :, :], rank[:, :, :], 1.0, None, ALU.is_equal))
            m = V.do(lambda e: e.tensor_scalar(sel[2][:, :, :], rank[:, :, :], 2.0, None, ALU.is_lt))
            n1, ps1 = gate_ps.take(T)
            n2, ps2 = up_ps.take(T)
            T.wait(m, m_ready)
            both = sel[2][:, :, :].rearrange("p t e -> p (t e)")
            T.run(lambda e: e.matmul(ps2[:, 0:NT * NE], ones[:, :], both, start=True, stop=True))
            pm = T.do(lambda e: e.matmul(ps1[:, 0:NT * NE], before[:, :], both, start=True, stop=True))
            step(lambda e: e.reduce_max(col[:, :], logit[:, :, :], AX.X))
            m = V.do(lambda e: e.tensor_tensor(weight[:, :, :], logit[:, :, :], over_e(col[:, :]), ALU.subtract))
            S.wait(m)
            em = S.do(lambda e: e.activation(weight[:, :, :], weight[:, :, :], ACT.Exp))
            V.wait(pm)
            step(lambda e: e.tensor_copy(total[:, :, :].rearrange("p t e -> p (t e)"), ps2[:, 0:NT * NE]))
            for x in range(NE):
                m = V.do(lambda e, x=x: e.tensor_tensor_scan(upto[:, :, x], ones[:, 0:NT], total[:, :, x], 0.0, ALU.mult, ALU.add))
            V.wait(m)
            step(lambda e: e.tensor_scalar(counts[:, 3, :], upto[:, NT - 1, :], float(P - 1), None, ALU.add))
            step(lambda e: e.tensor_copy(counts_i[:, 0, :], counts[:, 3, :]))
            step(lambda e: e.tensor_scalar(counts_i[:, 1, :], counts_i[:, 0, :], P.bit_length() - 1, None, ALU.arith_shift_right))
            step(lambda e: e.tensor_copy(counts[:, 3, :], counts_i[:, 1, :]))
            step(lambda e: e.tensor_scalar(counts[:, 0, :], counts[:, 3, :], 1.0, None, ALU.max))
            step(lambda e: e.tensor_tensor_scan(counts[:, 1, :], ones[:, 0:NE], counts[:, 0, :], 0.0, ALU.mult, ALU.add))
            step(lambda e: e.tensor_tensor(counts[:, 2, :], counts[:, 1, :], counts[:, 0, :], ALU.subtract))
            bases = counts[:, 2, :].rearrange("p (o e) -> p o e", o=1).to_broadcast([P, MT, NE])
            tiles = tile_id[:, :].rearrange("p (i o) -> p i o", o=1).to_broadcast([P, MT, NE])
            step(lambda e: e.tensor_tensor(owned[:, :, :], bases, tiles, ALU.is_le))
            step(lambda e: e.reduce_sum(owner_f[:, 2, :], owned[:, :, :], AX.X))
            step(lambda e: e.tensor_scalar(owner_f[:, 0, :], owner_f[:, 2, :], 1.0, None, ALU.subtract))
            step(lambda e: e.tensor_scalar(owner_f[:, 1, :], owner_f[:, 0, :], float(WR), float(-WR), ALU.is_ge, ALU.mult))
            step(lambda e: e.tensor_tensor(owner_f[:, 1, :], owner_f[:, 1, :], owner_f[:, 0, :], ALU.add))
            step(lambda e: e.tensor_scalar(owner_f[:, 2, :], owner_f[:, 0, :], float(2 * WR), float(-WR), ALU.is_ge, ALU.mult))
            step(lambda e: e.tensor_tensor(owner_f[:, 1, :], owner_f[:, 1, :], owner_f[:, 2, :], ALU.add))
            step(lambda e: e.tensor_tensor(owner_f[:, 2, 1:MT], owner_f[:, 0, 1:MT], owner_f[:, 0, 0:MT - 1], ALU.subtract))
            owner_mark = V.do(lambda e: e.tensor_copy(owner[:, :, :], owner_f[:, :, :]))
            step(lambda e: e.tensor_tensor(upto[:, :, :], upto[:, :, :], total[:, :, :], ALU.subtract))
            step(lambda e: e.tensor_tensor(upto[:, :, :].rearrange("p t e -> p (t e)"), upto[:, :, :].rearrange("p t e -> p (t e)"), ps1[:, 0:NT * NE], ALU.add))
            step(lambda e: e.tensor_scalar(counts[:, 3, :], counts[:, 2, :], float(P), None, ALU.mult))
            step(lambda e: e.tensor_tensor(upto[:, :, :], upto[:, :, :], over_t(counts[:, 3, :]), ALU.add))
            for c in range(2):
                step(lambda e, c=c: e.tensor_tensor(total[:, :, :], sel[c][:, :, :], upto[:, :, :], ALU.mult))
                step(lambda e, c=c: e.reduce_sum(slot_f[:, c, :], total[:, :, :], AX.X))
            step(lambda e: e.tensor_copy(slot_i[:, :, :], slot_f[:, :, :]))
            V.wait(em)
            step(lambda e: e.tensor_tensor(weight[:, :, :], weight[:, :, :], sel[2][:, :, :], ALU.mult))
            step(lambda e: e.reduce_sum(col[:, :], weight[:, :, :], AX.X))
            step(lambda e: e.reciprocal(col[:, :], col[:, :]))
            step(lambda e: e.tensor_tensor(weight[:, :, :], weight[:, :, :], over_e(col[:, :]), ALU.mult))
            step(lambda e: e.tensor_tensor(weight[:, :, :], weight[:, :, :], over_t(e_scale[:, :]), ALU.mult))
            for c in range(2):
                V.do(lambda e, c=c: e.tensor_copy(rows[:, c, :, 0], token_id[:, :]))
                step(lambda e, c=c: e.tensor_tensor(total[:, :, :], sel[c][:, :, :], weight[:, :, :], ALU.mult))
                m = V.do(lambda e, c=c: e.reduce_sum(rows[:, c, :, 1], total[:, :, :], AX.X))
                V.wait(m)
            G.wait(m, cleared)
            for c in range(2):
                for t in range(NT):
                    slots_put.count += 16
                    G.run(lambda e, c=c, t=t: e.indirect_dma_start(
                        out=slots, out_offset=bass.IndirectOffsetOnAxis(ap=slot_i[:, c, t:t + 1], axis=0),
                        in_=rows[:, c, t, :], in_offset=None).then_inc(slots_put.sem, 16))
            Y.wait((slots_put.sem, slots_put.count))
            got = slots_get.start(Y, back[:, :, :].rearrange("i p c -> i (p c)"), slots.rearrange("(i p) c -> i (p c)", p=P))
            n3, ps3 = turn_ps.take(T)
            T.wait(got)
            T.run(lambda e: e.transpose(ps3[:, 0:MT], back[:, :, 0], ident[0:MT, 0:MT]))
            m = T.do(lambda e: e.transpose(ps3[:, MT:2 * MT], back[:, :, 1], ident[0:MT, 0:MT]))
            V.wait(m)
            ids_mark = V.do(lambda e: e.tensor_copy(ids[:, :], ps3[:, 0:MT]))
            row_w_mark = V.do(lambda e: e.tensor_copy(row_w[:, :], ps3[:, MT:2 * MT]))
            V.wait(row_w_mark)
            turn_ps.release(n3, row_w_mark)
            gate_ps.release(n1, row_w_mark)
            up_ps.release(n2, row_w_mark)

            fr = dict(xgT=[None, None], gelu=[None, None], act=[None, None], actT=[None, None])
            gathered, place, done_tile = [], {}, []

            def fetch(i):
                n, buf = xg.take(G)
                G.wait(ids_mark)
                s = gather[n]
                s.count += 16
                G.run(lambda e: e.indirect_dma_start(out=buf[:, :], out_offset=None, in_=tokens,
                                                     in_offset=bass.IndirectOffsetOnAxis(ap=ids[:, i:i + 1], axis=0)).then_inc(s.sem, 16))
                gathered.append((n, buf, (s.sem, s.count)))

            def load_weights(i):
                s = load_e[i % 4]
                Y.wait(owner_mark, done_tile[i - WR] if i >= WR else None)

                def go(e):
                    expert = e.value_load(owner[0:1, 0, i:i + 1], min_val=0, max_val=NE - 1)
                    at = e.value_load(owner[0:1, 1, i:i + 1], min_val=0, max_val=WR - 1)
                    new = e.value_load(owner[0:1, 2, i:i + 1], min_val=0, max_val=1)
                    e.dma_start(w_gu[:, bass.ds(at, 1), :, :], gu_dram[:, bass.ds(expert, 1), :, :], cond=new).then_inc(s.sem, 16)
                    e.dma_start(w_dn[:, bass.ds(at, 1), :, :], dn_dram[:, bass.ds(expert, 1), :, :], cond=new).then_inc(s.sem, 16)
                Y.run(go)
                s.count += 32
                weights_ready.append((s.sem, s.count))

            def up(i):
                j = i % 2
                gn, buf, mark = gathered[i]
                n, ps = turn_ps.take(T)
                T.wait(mark)
                for k in range(KD):
                    f = lambda e, k=k: e.transpose(ps[:, k * P:(k + 1) * P], buf[:, k * P:(k + 1) * P], ident[:, :])
                    T.run(f) if k < KD - 1 else None
                m = T.do(f)
                xg.release(gn, m)
                S.wait(m, fr["xgT"][j])
                m = S.do(lambda e: e.activation(xgT[j][:, :, :], ps[:, :].rearrange("p (k j) -> p k j", k=KD), ACT.Copy))
                turn_ps.release(n, m)
                n1, gps = gate_ps.take(T)
                n2, ups = up_ps.take(T)
                T.wait(m, weights_ready[i], owner_mark)
                T.run(lambda e: place.__setitem__(i, e.value_load(owner[0:1, 1, i:i + 1], min_val=0, max_val=WR - 1)))
                for ps_, off in ((gps, 0), (ups, EH)):
                    for k in range(KD):
                        f = lambda e, k=k, ps_=ps_, off=off: e.matmul(ps_[:, :], xgT[j][:, k, :], w_gu[:, bass.ds(place[i], 1), k, off:off + EH].rearrange("p o n -> p (o n)"), start=(k == 0), stop=(k == KD - 1))
                        T.run(f) if k < KD - 1 else None
                    m = T.do(f)
                    if off == 0:
                        S.wait(m, fr["gelu"][j])
                        gm = S.do(lambda e: e.activation(gelu[j][:, :], gps[:, :], ACT.Gelu_apprx_tanh))
                        gate_ps.release(n1, gm)
                fr["xgT"][j] = m
                V.wait(m, gm, fr["act"][j])
                m = V.do(lambda e: e.tensor_tensor(act[j][:, :], gelu[j][:, :], ups[:, :], ALU.mult))
                up_ps.release(n2, m)
                fr["gelu"][j] = m
                return m

            def down(i, am):
                j = i % 2
                n, ps = turn_ps.take(T)
                T.wait(am)
                for k in range(KD):
                    f = lambda e, k=k: e.transpose(ps[:, k * P:(k + 1) * P], act[j][:, k * P:(k + 1) * P], ident[:, :])
                    T.run(f) if k < KD - 1 else None
                m = T.do(f)
                fr["act"][j] = m
                S.wait(m, fr["actT"][j])
                m = S.do(lambda e: e.activation(actT[j][:, :, :], ps[:, :].rearrange("p (k j) -> p k j", k=KD), ACT.Copy))
                turn_ps.release(n, m)
                dn, dps = down_ps.take(T)
                T.wait(m)
                for k in range(KD):
                    f = lambda e, k=k: e.matmul(dps[:, :], actT[j][:, k, :], w_dn[:, bass.ds(place[i], 1), k, :].rearrange("p o n -> p (o n)"), start=(k == 0), stop=(k == KD - 1))
                    T.run(f) if k < KD - 1 else None
                m = T.do(f)
                fr["actT"][j] = m
                done_tile.append(m)
                yn, ybuf = y_out.take(V)
                V.wait(m)
                vm = V.do(lambda e: e.tensor_scalar(ybuf[:, :], dps[:, :], row_w[:, i:i + 1], None, ALU.mult))
                down_ps.release(dn, vm)
                G.wait(vm, residual_out, (scatter.sem, scatter.count) if scatter.count else None)
                scatter.count += 16
                G.run(lambda e: e.indirect_dma_start(
                    out=out, out_offset=bass.IndirectOffsetOnAxis(ap=ids[:, i:i + 1], axis=0),
                    in_=ybuf[:, :], in_offset=None, compute_op=ALU.add).then_inc(scatter.sem, 16))
                y_out.release(yn, (scatter.sem, scatter.count))

            fetch(0)
            fetch(1)
            for i in range(1, WR):
                load_weights(i)
            am = up(0)
            for i in range(1, MT):
                if i + 1 < MT:
                    fetch(i + 1)
                nxt = up(i)
                down(i - 1, am)
                am = nxt
                if i - 1 + WR < MT:
                    load_weights(i - 1 + WR)
            down(MT - 1, am)
            Y.wait((scatter.sem, scatter.count))

        with ExitStack() as st:
            experts(st)

        block = ExitStack()
        with block:
            b = block.enter_context(nc.Block())

            @b.tensor
            def _(e):
                for f in T.queue:
                    f(e)

            @b.vector
            def _(e):
                for f in V.queue:
                    f(e)

            @b.scalar
            def _(e):
                for f in S.queue:
                    f(e)

            @b.gpsimd
            def _(e):
                for f in G.queue:
                    f(e)

            @b.sync
            def _(e):
                for f in Y.queue:
                    f(e)


def shape_constants():
    j = np.arange(P)
    select = np.zeros((64, NG, P), np.float32)
    for part in range(3):
        for g in range(NG):
            select[part * NG + g, g, :] = 1.0
    sign = np.zeros((64, HG, P), np.float32)
    for part in range(3):
        for h in range(HG):
            sign[3 * NG + part * HG + h, h, :] = -1.0
    expand = np.zeros((NH, HID), np.float32)
    for h in range(NH):
        expand[h, h * HP:(h + 1) * HP] = 1.0
    lower = (np.arange(NE)[None, :] < np.arange(NE)[:, None]).astype(np.float32).reshape(1, NE * NE)
    return {
        "c_ident": np.eye(P, dtype=np.float32),
        "c_causal": (j[:, None] <= j[None, :]).astype(np.float32),
        "c_select": select.reshape(64, NG * P),
        "c_head_sign": sign.reshape(64, HG * P),
        "c_expand": expand,
        "c_before": (j[:, None] < j[None, :]).astype(np.float32),
        "c_token_id": (np.arange(NT)[None, :] * P + j[:, None]).astype(np.float32),
        "c_tile_id": np.broadcast_to(np.arange(MT, dtype=np.float32), (P, MT)).copy(),
        "c_slots": np.broadcast_to(np.stack([NT * P + j, 0 * j], axis=1).astype(np.float32).reshape(1, 2 * P), (MT, 2 * P)).copy(),
        "c_lower": np.broadcast_to(lower, (P, NE * NE)).copy(),
    }


def kernel(**inputs):
    import concourse.bacc as bacc
    from concourse.bass_utils import run_bass_kernel_spmd

    a = {k: np.asarray(v) for k, v in inputs.items()}
    arrays = {k: np.ascontiguousarray(a[k]) for k in (
        "x", "ctx_512", "L0_attn_conv_w", "L0_attn_dt_bias", "L0_attn_A_log",
        "L0_ffn_router_logits", "L0_ffn_linear", "L0_ffn_per_expert_scale")}
    columns = lambda v: np.ascontiguousarray(v.reshape(-1, P).T)
    arrays["c_norm_w"] = columns(a["L0_attn_norm_w"])
    arrays["c_router_scale"] = columns(a["L0_ffn_router_scale"])
    arrays["c_w_inT"] = np.ascontiguousarray(a["L0_attn_W_in"].T)
    arrays["c_w_outT"] = np.ascontiguousarray(a["L0_attn_W_out"].T)
    arrays["c_gatingT"] = np.ascontiguousarray(a["L0_ffn_gating_einsum"].transpose(0, 3, 1, 2).reshape(NE, DIM, 2 * EH))
    arrays["c_D_channels"] = columns(np.repeat(a["L0_attn_D"], HP))
    arrays.update(shape_constants())

    nc = bacc.Bacc("TRN2", target_bir_lowering=False, num_devices=1)
    feeds, aps = {}, {}
    for name, value in arrays.items():
        feeds[name + "_dram"] = value
        aps[name] = nc.dram_tensor(name + "_dram", value.shape, mybir.dt.from_np(value.dtype), kind="ExternalInput").ap()
    out = nc.dram_tensor("out_dram", ((NT + 1) * P, DIM), F32, kind="ExternalOutput").ap()
    layer_kernel(nc, aps, out)
    result = run_bass_kernel_spmd(nc, [feeds], core_ids=[0])
    return result.results[0]["out_dram"][:NT * P].reshape(NB, L, DIM)
```

```python
from contextlib import ExitStack

import concourse.bass as bass
import numpy as np
from concourse import mybir

F32 = mybir.dt.float32
BF16 = mybir.dt.bfloat16
F16 = mybir.dt.float16
ALU = mybir.AluOpType
ACT = mybir.ActivationFunctionType
AX = mybir.AxisListType

P = 128
NB, L, DIM = 8, 256, 512
TPB = L // P
NT = NB * TPB
KD = DIM // P
HID, NH, HP, NS = 1024, 64, 16, 128
CONV = HID + 2 * NS
NCZ, NCX = HID // P, CONV // P
TAPS = 4
HG = 4
NG = NH // HG
DROWS = 3 * (NG + HG)
QH, KVH, DH = 32, 8, 16
SLOT = 64
NE, EH = 8, 512
MT = (2 * NT * P + NE * P) // P
WR = 3
LN_EPS, RMS_EPS, ROUTER_EPS = 1e-5, 1e-5, 1e-6


class Engine:

    def __init__(self, name, sem):
        self.name, self.sem, self.count, self.queue, self.seen = name, sem, 0, [], {}

    def run(self, instruction):
        self.queue.append(instruction)

    def do(self, instruction):
        self.count += 1
        self.queue.append(lambda e: instruction(e).then_inc(self.sem, 1))
        return self.sem, self.count

    def wait(self, *marks):
        for mark in marks:
            if mark is None:
                continue
            sem, value = mark
            if self.seen.get(id(sem), 0) < value:
                self.seen[id(sem)] = value
                self.queue.append(lambda e, s=sem, v=value: e.wait_ge(s, v))


class Load:

    def __init__(self, sem):
        self.sem, self.count = sem, 0

    def start(self, eng, out, in_):
        self.count += 16
        eng.queue.append(lambda e: e.dma_start(out, in_).then_inc(self.sem, 16))
        return self.sem, self.count


class Ring:

    def __init__(self, buffers):
        self.buffers, self.at = buffers, 0
        self.free = [()] * len(buffers)
        self.in_use = [False] * len(buffers)

    def busy(self):
        return self.in_use[self.at % len(self.buffers)]

    def take(self, writer):
        n = self.at % len(self.buffers)
        assert not self.in_use[n], "taken before its last reader is queued"
        self.at, self.in_use[n] = self.at + 1, True
        writer.wait(*self.free[n])
        return n, self.buffers[n]

    def release(self, n, *marks):
        self.free[n], self.in_use[n] = marks, False


BLOCKED = "blocked"


def alternate(*generators):
    live = [[g, w, 0.0] for g, w in generators]
    blocked = 0
    while live:
        item = min(live, key=lambda x: x[2])
        r = next(item[0], "end")
        if r == "end":
            live.remove(item)
            blocked = 0
        elif r == BLOCKED:
            blocked += 1
            assert len(live) > 1 and blocked < 8, "every stage is blocked"
            item[2] = max(x[2] for x in live if x is not item) + 1e-9
        else:
            blocked = 0
            item[2] += 1.0 / item[1]


def together(*generators):
    live = list(generators)
    while live:
        live = [g for g in live if next(g, "end") != "end"]
        yield


def advance(sides):
    steps = [(g, next(g, "end")) for g in sides]
    sides[:] = [g for g, r in steps if r != "end"]
    return any(r == BLOCKED for _, r in steps)


def pipeline(items, stages):
    at = [{} for _ in items]
    for s in range(len(items) + len(stages) - 1):
        for d, stage in reversed(list(enumerate(stages))):
            i = s - d
            if stage and 0 <= i < len(items):
                stage(items[i], at[i])
        yield


def layer_kernel(nc, A, out):
    x_rows = A["x"].rearrange("b s d -> (b s) d").rearrange("(t p) d -> p t d", p=P)
    ctx_rows = A["ctx_512"].rearrange("b s d -> (b s) d").rearrange("(t p) d -> p t d", p=P)

    with ExitStack() as top:
        semaphore = lambda name: top.enter_context(nc.semaphore(name))
        T = Engine("tensor", semaphore("tensor_done"))
        V = Engine("vector", semaphore("vector_done"))
        S = Engine("scalar", semaphore("scalar_done"))
        G = Engine("gpsimd", semaphore("gpsimd_done"))
        Y = Engine("sync", semaphore("sync_done"))
        engines = [T, V, S, G, Y]

        def sb(stack, name, shape, dt=F32):
            return stack.enter_context(nc.sbuf_tensor(name, shape, dt))

        def barrier():
            for e in engines:
                e.wait(*[(o.sem, o.count) for o in engines if o.count])

        x_sb = sb(top, "x_sb", [P, NT, DIM])
        ident = sb(top, "ident", [P, P])
        ident16 = sb(top, "ident16", [P, P], F16)
        tokens = nc.dram_tensor("normed_tokens", [(NT + 1) * P, DIM], F32).ap()
        load_ident = Load(semaphore("load_ident"))
        load_const = Load(semaphore("load_const"))
        load_x = [Load(semaphore(f"load_x{i}")) for i in range(2)]
        load_r = Load(semaphore("load_r"))
        store_tokens = [Load(semaphore(f"store_tokens{i}")) for i in range(2)]
        x_ready = [load_x[0].start(Y, x_sb[:, 0:TPB, :], x_rows[:, 0:TPB, :])] * TPB
        ident_ready = load_ident.start(S, ident[:, :], A["c_ident"])

        def rsqrt(v, y, tmp, ready):
            I32 = mybir.dt.int32
            V.wait(ready)
            m = V.do(lambda e: e.tensor_scalar(tmp.bitcast(I32), v.bitcast(I32), 1, None, ALU.arith_shift_right))
            V.wait(m)
            m = V.do(lambda e: e.tensor_scalar(y.bitcast(I32), tmp.bitcast(I32), -1.0, float(0x5F3759DF), ALU.mult, ALU.add))
            yield m
            for _ in range(3):
                G.wait(m)
                m = G.do(lambda e: e.tensor_tensor(tmp, y, y, ALU.mult))
                G.wait(m)
                m = G.do(lambda e: e.tensor_tensor(tmp, tmp, v, ALU.mult))
                G.wait(m)
                m = G.do(lambda e: e.tensor_scalar(tmp, tmp, -0.5, 1.5, ALU.mult, ALU.add))
                G.wait(m)
                m = G.do(lambda e: e.tensor_tensor(y, y, tmp, ALU.mult))
            yield m

        def norm_factors(b, s):
            for t in range(TPB):
                V.wait(x_ready[b * TPB + t])
                m = V.do(lambda e, t=t: e.bn_stats(s[:, 6 * t:6 * t + 6], x_sb[:, b * TPB + t, :]))
            V.wait(m)
            for t in range(TPB):
                m = V.do(lambda e, t=t: e.bn_aggr(s[:, 12 + 2 * t:14 + 2 * t], s[:, 6 * t:6 * t + 6]))
            V.wait(m)
            m = V.do(lambda e: e.tensor_scalar(s[:, 16:18], s[:, 12:16].rearrange("p (t c) -> p t c", c=2)[:, :, 1], LN_EPS, None, ALU.add))
            yield from rsqrt(s[:, 16:18], s[:, 18:20], s[:, 20:22], m)

        def normalise(e, out_, tile, s, t):
            return e.tensor_scalar(out_, x_sb[:, tile, :], s[:, 12 + 2 * t:13 + 2 * t], s[:, 18 + t:19 + t], ALU.subtract, ALU.mult)

        def ssm_mixer(st):
            bank = lambda name, shape=[P, 512], dt=F32: st.enter_context(nc.psum_tensor(name, shape, dt))
            proj_ps = Ring([bank("proj_ps0"), bank("proj_ps1")])
            decay_ps = Ring([bank("decay_ps0"), bank("decay_ps1")])
            y_ps = Ring([bank("y_ps0"), bank("y_ps1")])
            misc_ps = Ring([bank("misc_ps")])
            out_ps = Ring([bank("out_ps")])

            w_in = sb(st, "w_in", [P, KD, 2 * HID + 2 * NS + NH])
            w_out = sb(st, "w_out", [P, NCZ, DIM])
            conv_w = sb(st, "conv_w", [P, NCX, TAPS])
            norm_w = sb(st, "norm_w", [P, NCZ])
            d_w = sb(st, "d_w", [P, NCZ])
            head_w = sb(st, "head_w", [NH, 4])
            raw_in = Ring([sb(st, f"raw{i}", [P, 2, L + TAPS - 1]) for i in range(2)])
            causal = sb(st, "causal", [P, P])
            expand = sb(st, "expand", [NH, NCZ // 2, P])
            ones = sb(st, "ones", [P, 1])

            xn = sb(st, "xn", [P, DIM])
            stats = sb(st, "stats", [P, 24])
            rstats = sb(st, "rstats", [P, 4])
            xnT = sb(st, "xnT", [P, KD, L])
            conv_out = Ring([sb(st, f"conv{i}", [P, 2, L]) for i in range(2)])
            xbc = [sb(st, f"xbc{i}", [P, NCX, L]) for i in range(2)]
            zs = [sb(st, f"zs{i}", [P, NCZ, L]) for i in range(2)]
            select_f = xbc[0][0:64, 0:NCZ, :].rearrange("p c t -> p (c t)")
            head_sign = zs[0][0:64, 0:2, :].rearrange("p c t -> p (c t)")
            dtT = sb(st, "dtT", [NH, 6, L])
            wdecT = sb(st, "wdecT", [NH, P])
            cum3 = sb(st, "cum3", [NH, 3, TPB, P], BF16)
            rest = dtT[:, 3:5, :]
            dt_tokens = [sb(st, f"dt_tok{i}", [P, TPB, NH]) for i in range(2)]
            wdec_tokens = [sb(st, f"wdec_tok{i}", [P, NH]) for i in range(2)]
            ecums = [sb(st, f"ecum{i}", [NH, P]) for i in range(2)]
            LT = [sb(st, f"LT{i}", [64, TPB, NG, P], BF16) for i in range(2)]
            RT = [sb(st, f"RT{i}", [64, TPB, HG * P], BF16) for i in range(2)]
            b_tok = sb(st, "b_tok", [P, NS])
            cbm = [sb(st, f"cbm{i}", [P, P]) for i in range(2)]
            xdt = [sb(st, f"xdt{i}", [P, NH // 2, 2 * HP]) for i in range(2)]
            xw = sb(st, "xw", [P, NH, HP])
            state = sb(st, "state", [P, HID])
            decay = Ring([sb(st, f"decay{i}", [P, HG * P]) for i in range(3)])
            mix = Ring([sb(st, f"mix{i}", [P, HG * P]) for i in range(4)])
            eexp = sb(st, "eexp", [P, 512])
            yz = sb(st, "yz", [P, NCZ, P])

            load_w_in = {kind: Load(semaphore(f"load_w_{kind}")) for kind in ("dt", "xbc", "z")}
            load_w_out = Load(semaphore("load_w_out"))
            scratch = [nc.dram_tensor(f"cum_scratch{i}", [3, NH, TPB, P], BF16).ap() for i in range(2)]
            store_cum = Load(semaphore("store_cum"))
            load_cum = Load(semaphore("load_cum"))

            columns = {"dt": (HID + CONV, NH), "xbc": (HID, CONV), "z": (0, HID)}
            w_rows = A["c_w_inT"].rearrange("(k p) n -> p k n", p=P)
            w_ready = {}
            load_w = lambda eng, kind, at, n: w_ready.__setitem__(kind, load_w_in[kind].start(eng, w_in[:, :, at:at + n], w_rows[:, :, at:at + n]))
            load_w(S, "dt", *columns["dt"])
            load_w(S, "xbc", *columns["xbc"])
            for dst, src in [
                (conv_w[:, :, :], A["L0_attn_conv_w"].rearrange("(c p) k -> p c k", p=P)),
                (norm_w[:, :], A["c_norm_w"]),
                (d_w[:, :], A["c_D_channels"]),
                (head_w[:, 0:1], A["L0_attn_dt_bias"].rearrange("(h o) -> h o", o=1)),
                (head_w[:, 1:2], A["L0_attn_A_log"].rearrange("(h o) -> h o", o=1)),
                (causal[:, :], A["c_causal"]),
                (expand[:, :, :], A["c_expand"].rearrange("h (c p) -> h c p", p=P)),
                (select_f, A["c_select"]),
                (head_sign, A["c_head_sign"]),
            ]:
                const_ready = load_const.start(Y, dst, src)
            Y.wait(w_ready["xbc"])
            load_w(Y, "z", *columns["z"])
            w_out_ready = load_w_out.start(Y, w_out[:, :, :], A["c_w_outT"].rearrange("(c p) d -> p c d", p=P))
            x_ready.extend([load_x[1].start(Y, x_sb[:, TPB:NT, :], x_rows[:, TPB:NT, :])] * (NT - TPB))

            made = {}
            last = {}
            NHALF = NG // 2
            PROJECT_FIRST, PROJECT_EVERY = 4, 1.35
            UNITS = [(b, c, hf) for b in range(NB) for c in range(TPB) for hf in range(2)]

            def constants():
                for e in (V, S, G):
                    e.wait(const_ready)
                V.do(lambda e: e.memset(ones[:, :], 1.0))
                for i in range(2):
                    V.do(lambda e, i=i: e.memset(raw_in.buffers[i][:, :, 0:TAPS - 1], 0.0))
                    V.do(lambda e, i=i: e.memset(xdt[i][:, :, :], 0.0))
                V.wait(ident_ready)
                V.do(lambda e: e.tensor_copy(ident16[:, :], ident[:, :]))
                for i in range(2):
                    for c in range(TPB):
                        V.do(lambda e, i=i, c=c: e.tensor_copy(LT[i][:, c, :, :], select_f.rearrange("p (g j) -> p g j", j=P)))
                        V.do(lambda e, i=i, c=c: e.tensor_copy(RT[i][:, c, :], head_sign))
                V.do(lambda e: e.tensor_scalar(conv_w[:, :, :], conv_w[:, :, :], 0.5, None, ALU.mult))
                m = S.do(lambda e: e.activation(head_w[:, 2:3], head_w[:, 1:2], ACT.Exp))
                V.wait(m)
                init = made["constants"] = V.do(lambda e: e.tensor_scalar(head_w[:, 3:4], head_w[:, 2:3], -1.0, None, ALU.mult))
                for e in (S, V, G, Y):
                    e.wait(init)

            def scale_weights():
                G.wait(w_out_ready)
                for c in range(NCZ):
                    made["normed out"] = G.do(lambda e, c=c: e.tensor_scalar(w_out[:, c, :], w_out[:, c, :], norm_w[:, c:c + 1], 0.5, ALU.mult, ALU.mult))

            def project(b):
                par = b % 2
                dt_tok, wdec_tok, ecum = dt_tokens[par], wdec_tokens[par], ecums[par]
                norm = None
                for norm in norm_factors(b, stats):
                    yield
                for t in range(TPB):
                    tile = b * TPB + t
                    V.wait(norm, last.get("xn"))
                    xm = V.do(lambda e, t=t, tile=tile: normalise(e, xn[:, :], tile, stats, t))
                    yield
                    n, ps = proj_ps.take(T)
                    T.wait(xm, ident_ready)
                    for k in range(KD):
                        f = lambda e, k=k, ps=ps: e.transpose(ps[:, k * P:(k + 1) * P], xn[:, k * P:(k + 1) * P], ident[:, :])
                        T.run(f) if k < KD - 1 else None
                    last["xn"] = m = T.do(f)
                    yield
                    S.wait(m, last.get("xnT"))
                    xnT_mark = S.do(lambda e, t=t, ps=ps: e.activation(xnT[:, :, t * P:(t + 1) * P], ps[:, :].rearrange("p (k j) -> p k j", k=KD), ACT.Copy))
                    proj_ps.release(n, xnT_mark)
                if b == 0:
                    constants()
                    scale_weights()
                yield
                T.wait(xnT_mark, w_ready["dt"])
                while b >= 2 and ("finished", b - 2) not in made:
                    yield BLOCKED

                def channels(ps, at, col, width):
                    for k in range(KD):
                        f = lambda e, k=k: e.matmul(ps[0:width, at:at + L], w_in[:, k, col:col + width], xnT[:, k, :], start=(k == 0), stop=(k == KD - 1))
                        T.run(f) if k < KD - 1 else None
                    return T.do(f)

                def step_sizes():
                    n, ps = proj_ps.take(T)
                    m = channels(ps, 0, HID + CONV, NH)
                    yield
                    S.wait(m, last.get("dtT"))
                    u_mark = m = S.do(lambda e, ps=ps: e.activation(dtT[:, 0, :], ps[0:NH, 0:L], ACT.Identity, bias=head_w[:, 0:1]))
                    proj_ps.release(n, m)
                    S.wait(m)
                    m = S.do(lambda e: e.activation(dtT[:, 1, :], dtT[:, 0, :], ACT.Abs))
                    yield
                    S.wait(m)
                    e_mark = S.do(lambda e: e.activation(dtT[:, 2, :], dtT[:, 1, :], ACT.Exp, scale=-1.0))
                    S.wait(e_mark)
                    ln_mark = S.do(lambda e: e.activation(dtT[:, 3, :], dtT[:, 2, :], ACT.Ln, bias=1.0))
                    yield
                    V.wait(e_mark, u_mark)
                    m = V.do(lambda e: e.tensor_scalar(dtT[:, 4, :], dtT[:, 2, :], 1.0, None, ALU.add))
                    V.wait(m, ln_mark)
                    m = V.do(lambda e: e.scalar_tensor_tensor(dtT[:, 1, :], dtT[:, 4, :], 1.0, dtT[:, 2, :], ALU.subtract, ALU.subtract))
                    V.wait(m)
                    m = V.do(lambda e: e.reciprocal(dtT[:, 4, :], dtT[:, 4, :]))
                    yield
                    V.wait(m)
                    m = V.do(lambda e: e.scalar_tensor_tensor(dtT[:, 1, :], dtT[:, 1, :], -1.0, dtT[:, 4, :], ALU.mult, ALU.mult))
                    V.wait(m)
                    m = V.do(lambda e: e.tensor_tensor(dtT[:, 1, :], dtT[:, 1, :], dtT[:, 3, :], ALU.add))
                    V.wait(m)
                    dt_mark = m = V.do(lambda e: e.scalar_tensor_tensor(dtT[:, 5, :], dtT[:, 0, :], 0.0, dtT[:, 1, :], ALU.max, ALU.add))
                    yield
                    V.wait(m)
                    m = V.do(lambda e: e.tensor_scalar(dtT[:, 1, :], dtT[:, 5, :], head_w[:, 3:4], None, ALU.mult))
                    V.wait(m)
                    for c in range(TPB):
                        m = V.do(lambda e, c=c: e.tensor_tensor_scan(dtT[:, 0, c * P:(c + 1) * P], ones[0:NH, 0:1].to_broadcast([NH, P]), dtT[:, 1, c * P:(c + 1) * P], 0.0, ALU.mult, ALU.add))
                    cumT_mark = m
                    yield
                    V.wait(m, last.get("cum3"))
                    for s in range(3):
                        src = dtT[:, 0, :] if s == 0 else rest[:, s - 1, :]
                        part = cum3[:, s, :, :].rearrange("h c j -> h (c j)")
                        m = V.do(lambda e, part=part, src=src: e.tensor_copy(part, src))
                        V.wait(m)
                        if s < 2:
                            m = V.do(lambda e, s=s, part=part, src=src: e.tensor_tensor(rest[:, s, :], src, part, ALU.subtract))
                            V.wait(m)
                            yield
                    Y.wait(m)
                    m = store_cum.start(Y, scratch[par].rearrange("s h c j -> h s c j"), cum3[:, :, :, :])
                    Y.wait(m, last.get(("decay operands", par)))
                    last["cum3"] = m
                    for c in range(TPB):
                        m = load_cum.start(Y, RT[par][0:3 * NG, c, :].rearrange("p (h i) -> p h i", h=HG),
                                           scratch[par].rearrange("s (g h) c i -> (s g) c h i", h=HG)[:, c, :, :])
                        for s in range(3):
                            m = load_cum.start(Y, LT[par][3 * NG + HG * s:3 * NG + HG * (s + 1), c, :, :],
                                               scratch[par].rearrange("s (g h) c j -> s c h g j", h=HG)[s, c, :, :, :])
                    Y.wait(m)
                    made["decay operands", b] = m
                    S.wait(cumT_mark, last.get("wdecT"), last.get(("ecum", par)))
                    m = S.do(lambda e: e.activation(wdecT[:, :], dtT[:, 0, 0:P], ACT.Exp, bias=dtT[:, 0, P - 1:P], scale=-1.0))
                    made["ecum", b] = S.do(lambda e: e.activation(ecum[:, :], dtT[:, 0, P:2 * P], ACT.Exp))
                    yield
                    V.wait(m, dt_mark)
                    wdec_mark = V.do(lambda e: e.tensor_tensor(wdecT[:, :], wdecT[:, :], dtT[:, 5, 0:P], ALU.mult))
                    yield
                    n, ps = proj_ps.take(T)
                    T.wait(dt_mark, wdec_mark)
                    for c in range(TPB):
                        T.run(lambda e, c=c, ps=ps: e.transpose(ps[:, c * NH:(c + 1) * NH], dtT[:, 5, c * P:(c + 1) * P], ident[0:NH, 0:NH]))
                    m = T.do(lambda e, ps=ps: e.transpose(ps[:, TPB * NH:(TPB + 1) * NH], wdecT[:, :], ident[0:NH, 0:NH]))
                    last["wdecT"] = last["dtT"] = m
                    yield
                    S.wait(m, last.get(("dt_tok", par)))
                    S.do(lambda e, ps=ps: e.activation(dt_tok[:, :, :].rearrange("p c h -> p (c h)"), ps[:, 0:TPB * NH], ACT.Copy))
                    m = S.do(lambda e, ps=ps: e.activation(wdec_tok[:, :], ps[:, TPB * NH:(TPB + 1) * NH], ACT.Copy))
                    proj_ps.release(n, m)
                    made["dt_tok", b] = m
                    yield

                def conv_project(c0, at):
                    T.wait(w_ready["xbc"])
                    at["n"], at["ps"] = n, ps = proj_ps.take(T)
                    for c in (c0, c0 + 1):
                        at["m"] = channels(ps, (c - c0) * L, HID + c * P, P)

                def conv_copy(c0, at):
                    at["rn"], at["raw"] = raw_in.take(S)
                    raw, ps = at["raw"], at["ps"]
                    S.wait(at["m"])
                    S.do(lambda e: e.activation(raw[:, :, TAPS - 1:TAPS - 1 + L], ps[:, :].rearrange("p (c t) -> p c t", c=2), ACT.Copy))
                    at["cn"], at["conv"] = conv_out.take(S)
                    conv = at["conv"]
                    for j in range(2):
                        at["m"] = S.do(lambda e, j=j: e.activation(conv[:, j, :], ps[:, j * L:(j + 1) * L], ACT.Copy, scale=conv_w[:, c0 + j, TAPS - 1:TAPS]))
                    proj_ps.release(at["n"], at["m"])

                def conv_taps(c0, at):
                    raw, conv, m = at["raw"], at["conv"], at["m"]
                    for k in range(TAPS - 1):
                        V.wait(m)
                        for c in (c0, c0 + 1):
                            o, i, w = conv[:, c - c0, :], raw[:, c - c0, k:k + L], conv_w[:, c, k:k + 1]
                            m = V.do(lambda e, o=o, i=i, w=w: e.scalar_tensor_tensor(o, i, w, o, ALU.mult, ALU.add))
                    at["m"] = m
                    raw_in.release(at["rn"], m)

                def conv_tanh(c0, at):
                    conv = at["conv"]
                    S.wait(at["m"], *last.get(("x|B|C", par), ()))
                    at["m"] = S.do(lambda e: e.activation(xbc[par][:, c0:c0 + 2, :], conv[:, :, :], ACT.Tanh))

                def conv_gate(c0, at):
                    conv = at["conv"]
                    V.wait(at["m"])
                    m = V.do(lambda e: e.scalar_tensor_tensor(xbc[par][:, c0:c0 + 2, :], xbc[par][:, c0:c0 + 2, :], 1.0, conv[:, :, :], ALU.add, ALU.mult))
                    conv_out.release(at["cn"], m)
                    made["x|B|C", b] = m

                def z_project(c0, at):
                    T.wait(w_ready["z"])
                    at["n"], at["ps"] = n, ps = proj_ps.take(T)
                    for c in (c0, c0 + 1):
                        at["m"] = channels(ps, (c - c0) * L, c * P, P)

                def z_tanh(c0, at):
                    ps = at["ps"]
                    S.wait(at["m"], last.get(("z", par)))
                    at["m"] = S.do(lambda e: e.activation(zs[par][:, c0:c0 + 2, :], ps[:, :].rearrange("p (c t) -> p c t", c=2), ACT.Tanh, scale=0.5))

                def z_gate(c0, at):
                    ps = at["ps"]
                    V.wait(at["m"])
                    m = V.do(lambda e: e.scalar_tensor_tensor(zs[par][:, c0:c0 + 2, :], zs[par][:, c0:c0 + 2, :], 1.0, ps[:, :].rearrange("p (c t) -> p c t", c=2), ALU.add, ALU.mult))
                    proj_ps.release(at["n"], m)
                    made["z", b] = m

                stages = {"x|B|C": [conv_project, conv_copy, conv_taps, conv_tanh, conv_gate],
                          "z": [z_project, z_tanh, z_gate]}
                items = [(kind, c0) for c0 in range(0, NCX, 2) for kind in stages if kind == "x|B|C" or c0 < NCZ]

                def stage(d):
                    return lambda item, at: stages[item[0]][d](item[1], at) if d < len(stages[item[0]]) else None

                for _ in together(step_sizes(), pipeline(items, [stage(d) for d in range(5)])):
                    yield
                made["x|B|C whole", b] = made["x|B|C", b]
                last["xnT"] = made["x|B|C", b]

            def prepare(b, c, hf):
                par, tok = b % 2, slice(c * P, (c + 1) * P)
                dt_tok, wdec_tok = dt_tokens[par], wdec_tokens[par]
                while ("x|B|C whole", b) not in made or ("dt_tok", b) not in made:
                    yield BLOCKED
                T.wait(made["x|B|C", b], made["constants"])
                if hf == 0:
                    while misc_ps.busy():
                        yield
                    n, ps = misc_ps.take(T)
                    if c == 0:
                        T.run(lambda e: e.transpose(ps[:, P:2 * P], xbc[par][:, NCZ, 0:P], ident[:, :]))
                    m = T.do(lambda e: e.matmul(ps[:, 0:P], xbc[par][:, NCZ, tok], xbc[par][:, NCZ + 1, tok], start=True, stop=True))
                    yield
                    V.wait(m, last.get(("cbm", c, "vector")), last.get(("cbm", c, "gpsimd")))
                    m = V.do(lambda e: e.tensor_tensor(cbm[c][:, :], ps[:, 0:P], causal[:, :], ALU.mult))
                    made["cbm", b, c] = m
                    if c == 0:
                        V.wait(last.get("b_tok"))
                        made["b_tok", b] = m = V.do(lambda e: e.tensor_copy(b_tok[:, :], ps[:, P:2 * P]))
                    misc_ps.release(n, m)
                    yield
                while misc_ps.busy():
                    yield
                n, ps = misc_ps.take(T)
                for k in range(4):
                    f = lambda e, k=k, ps=ps: e.transpose(ps[:, k * P:(k + 1) * P], xbc[par][:, 4 * hf + k, tok], ident[:, :])
                    T.run(f) if k < 3 else None
                m = T.do(f)
                last["x|B|C read", b] = m
                yield
                hs = slice(hf * NH // 2, (hf + 1) * NH // 2)
                V.wait(m, last.get(("xdt", hf)), made["dt_tok", b])
                for odd in range(2):
                    o = xdt[hf][:, :, :].rearrange("p (q two) w -> p q two w", two=2)[:, :, odd, odd * HP:(odd + 1) * HP]
                    i0 = ps[:, :].rearrange("p (q two w) -> p q two w", two=2, w=HP)[:, :, odd, :]
                    i1 = dt_tok[:, c, hs].rearrange("p (q two) -> p q two", two=2)[:, :, odd:odd + 1].to_broadcast([P, NH // 4, HP])
                    m = V.do(lambda e, o=o, i0=i0, i1=i1: e.tensor_tensor(o, i0, i1, ALU.mult))
                made["xdt", b, c, hf] = m
                if c == 0:
                    V.wait(last.get("xw"))
                    i1 = wdec_tok[:, hs].rearrange("p (h o) -> p h o", o=1).to_broadcast([P, NH // 2, HP])
                    made["xw", b, hf] = m = V.do(lambda e: e.tensor_tensor(xw[:, hs, :], ps[:, :].rearrange("p (h w) -> p h w", w=HP), i1, ALU.mult))
                misc_ps.release(n, m)
                last["dt_tok", par] = m
                yield

            def finish(b, c, hf):
                par, tok, tile = b % 2, slice(c * P, (c + 1) * P), b * TPB + c
                yn, yps, ymark = made["y", b, c, hf]
                cts = slice(4 * hf, 4 * hf + 4)
                if c == 0:
                    T.wait(made["xw", b, hf], made["b_tok", b])
                    while misc_ps.busy():
                        yield
                    n, ps = misc_ps.take(T)
                    m = T.do(lambda e: e.matmul(ps[:, :], b_tok[:, :], xw[:, hf * NH // 2:(hf + 1) * NH // 2, :].rearrange("p h w -> p (h w)"), start=True, stop=True))
                    last["b_tok"] = last["xw"] = m
                    yield
                    S.wait(m, last.get(("state", hf)))
                    made["state", b, hf] = m = S.do(lambda e: e.activation(state[:, hf * 512:(hf + 1) * 512], ps[:, :], ACT.Copy))
                    misc_ps.release(n, m)
                    ysum, src = ymark, yps
                else:
                    T.wait(made["state", b, hf], made["ecum", b])
                    while misc_ps.busy():
                        yield
                    n, ps = misc_ps.take(T)
                    for k in range(4):
                        heads = slice(hf * NH // 2, (hf + 1) * NH // 2)
                        f = lambda e, k=k, ps=ps, heads=heads: e.matmul(ps[:, k * P:(k + 1) * P], expand[heads, k, :], ecums[par][heads, :], start=True, stop=True)
                        T.run(f) if k < 3 else None
                    last["ecum", par] = m = T.do(f)
                    yield
                    S.wait(m, last.get("eexp"))
                    ee = S.do(lambda e, ps=ps: e.activation(eexp[:, :], ps[:, :], ACT.Copy))
                    misc_ps.release(n, ee)
                    yield
                    while misc_ps.busy():
                        yield
                    n, ps = misc_ps.take(T)
                    for k in range(4):
                        f = lambda e, k=k, ps=ps: e.matmul(ps[:, k * P:(k + 1) * P], state[:, (4 * hf + k) * P:(4 * hf + k + 1) * P], xbc[par][:, NCZ + 1, tok], start=True, stop=True)
                        T.run(f) if k < 3 else None
                    last["state", hf] = m = T.do(f)
                    last["C", b] = m
                    yield
                    V.wait(m, ee)
                    m = V.do(lambda e, ps=ps: e.tensor_tensor(eexp[:, :], ps[:, :], eexp[:, :], ALU.mult))
                    misc_ps.release(n, m)
                    V.wait(m, ymark)
                    ysum = V.do(lambda e: e.tensor_tensor(eexp[:, :], eexp[:, :], yps[:, :], ALU.add))
                    y_ps.release(yn, ysum)
                    src = eexp
                yield
                V.wait(ysum, last.get("yz"), last.get("eexp"))
                for k in range(4):
                    ct = 4 * hf + k
                    m = V.do(lambda e, k=k, ct=ct: e.scalar_tensor_tensor(
                        yz[:, ct, :], xbc[par][:, ct, tok], d_w[:, ct:ct + 1], src[:, k * P:(k + 1) * P], ALU.mult, ALU.add))
                if c == 0:
                    y_ps.release(yn, m)
                V.wait(m, made["z", b])
                yz_mark = V.do(lambda e: e.tensor_tensor(yz[:, cts, :], yz[:, cts, :], zs[par][:, cts, tok], ALU.mult))
                yield
                S.wait(yz_mark)
                m = S.do(lambda e: e.activation(eexp[:, :].rearrange("p (c j) -> p c j", j=P), yz[:, cts, :], ACT.Square))
                yield
                G.wait(m)
                m = G.do(lambda e: e.tensor_tensor(eexp[:, 0:2 * P], eexp[:, 0:2 * P], eexp[:, 2 * P:4 * P], ALU.add))
                G.wait(m)
                m = G.do(lambda e: e.tensor_tensor(eexp[:, 0:P], eexp[:, 0:P], eexp[:, P:2 * P], ALU.add))
                for _ in range(5):
                    yield
                while misc_ps.busy():
                    yield
                n, ps = misc_ps.take(T)
                T.wait(m)
                f = lambda e, ps=ps: e.matmul(ps[:, 0:1], eexp[:, 0:P], ones[:, 0:1], start=True, stop=True)
                last["eexp"] = m = T.do(f)
                yield
                V.wait(m)
                if hf == 0:
                    m = V.do(lambda e, ps=ps: e.tensor_copy(rstats[:, 3:4], ps[:, 0:1]))
                else:
                    m = V.do(lambda e, ps=ps: e.tensor_tensor(rstats[:, 0:1], ps[:, 0:1], rstats[:, 3:4], ALU.add))
                    V.wait(m)
                misc_ps.release(n, m)
                if c == TPB - 1 and hf == 1:
                    last["x|B|C", par] = (yz_mark, last["C", b], last["x|B|C read", b])
                    last["z", par] = yz_mark
                    made["finished", b] = yz_mark
                if hf == 0:
                    return
                on, ops = out_ps.take(T)
                for ct in range(NCZ):
                    if ct % 2 == 0:
                        yield
                    if ct == 0:
                        T.wait(yz_mark, made["normed out"])
                    f = lambda e, ct=ct: e.matmul(ops[:, :], yz[:, ct, :], w_out[:, ct, :], start=(ct == 0), stop=(ct == NCZ - 1))
                    T.run(f) if ct < NCZ - 1 else None
                out_mark = T.do(f)
                last["yz"] = out_mark
                yield
                m = V.do(lambda e: e.tensor_scalar(rstats[:, 0:1], rstats[:, 0:1], 0.25 / HID, RMS_EPS, ALU.mult, ALU.add))
                for m in rsqrt(rstats[:, 0:1], rstats[:, 1:2], rstats[:, 2:3], m):
                    yield
                V.wait(m, out_mark)
                m = V.do(lambda e: e.scalar_tensor_tensor(x_sb[:, tile, :], ops[:, :], rstats[:, 1:2], x_sb[:, tile, :], ALU.mult, ALU.add))
                out_ps.release(on, m)
                x_ready[tile] = m
                yield

            def group_decay(s, at):
                b, c, hf = UNITS[s // NHALF]
                par, g = b % 2, hf * NHALF + s % NHALF
                at["n"], at["ps"] = n, ps = decay_ps.take(T)
                T.wait(made["decay operands", b])
                at["m"] = T.do(lambda e: e.matmul(ps[:, :], LT[par][0:DROWS, c, g, :], RT[par][0:DROWS, c, :], start=True, stop=True))
                last["decay operands", par] = at["m"]

            def group_bound(s, at):
                at["r"], at["buf"] = decay.take(S)
                ps, buf = at["ps"], at["buf"]
                S.wait(at["m"])
                at["m"] = S.do(lambda e: e.activation(buf[:, :], ps[:, :], ACT.Relu, scale=-1.0))
                decay_ps.release(at["n"], at["m"])

            def group_exp(s, at):
                buf = at["buf"]
                S.wait(at["m"])
                at["m"] = S.do(lambda e: e.activation(buf[:, :], buf[:, :], ACT.Exp, scale=-1.0))

            def group_mix(s, at):
                b, c, hf = UNITS[s // NHALF]
                E_ = V if s % 2 else G
                at["q"], at["mix"] = mix.take(E_)
                buf, out_buf = at["buf"], at["mix"]
                E_.wait(at["m"], made["cbm", b, c])
                cb = cbm[c][:, :].rearrange("p (o i) -> p o i", o=1).to_broadcast([P, HG, P])
                at["m"] = E_.do(lambda e: e.tensor_tensor(out_buf[:, :].rearrange("p (h i) -> p h i", h=HG), buf[:, :].rearrange("p (h i) -> p h i", h=HG), cb, ALU.mult))
                last["cbm", c, E_.name] = at["m"]
                decay.release(at["r"], at["m"])
                held.append(at)

            held, ybank = [], {}

            def group_heads(s, at):
                if s % 2 == 0:
                    return
                b, c, hf = u = UNITS[s // NHALF]
                if s % NHALF == 1:
                    ybank["now"] = y_ps.take(T)
                yn, yps = ybank["now"]
                two = [held.pop(0), held.pop(0)]
                T.wait(two[0]["m"], two[1]["m"], made["xdt", b, c, hf])
                ct = s % NHALF // 2
                for odd in range(2):
                    for quad in range(4):
                        h = 2 * quad + odd
                        buf = two[h // HG]["mix"]
                        f = lambda e, h=h, odd=odd, quad=quad, buf=buf: e.matmul(
                            yps[32 * quad:32 * quad + 32, ct * P:(ct + 1) * P], xdt[hf][:, 2 * HG * ct + h, :], buf[:, h % HG * P:(h % HG + 1) * P],
                            start=(odd == 0), stop=(odd == 1), tile_position=(0, 32 * quad))
                        T.run(f) if (odd, quad) != (1, 3) else None
                m = T.do(f)
                for x in two:
                    mix.release(x["q"], m)
                last["xdt", hf] = m
                made[("y",) + u] = (yn, yps, m)

            mixing = {"step": 0, "blocked": False}

            def mixer():
                n = len(UNITS) * NHALF
                main = pipeline(list(range(n)), [group_decay, group_bound, group_exp, group_mix, None, group_heads])
                sides = [prepare(*UNITS[0])]
                for s in range(n + 5):
                    u, k = divmod(s, NHALF)
                    mixing["step"] = s
                    if k == 5:
                        if u >= 1:
                            sides.append(finish(*UNITS[u - 1]))
                        if u + 1 < len(UNITS):
                            sides.append(prepare(*UNITS[u + 1]))
                    if k == 2 and u < len(UNITS):
                        while ("xdt",) + UNITS[u] not in made:
                            if advance(sides):
                                mixing["blocked"] = True
                                yield BLOCKED
                    if u < len(UNITS):
                        while ("decay operands", UNITS[u][0]) not in made:
                            mixing["blocked"] = True
                            yield BLOCKED
                    mixing["blocked"] = False
                    advance(sides)
                    next(main)
                    advance(sides)
                    yield
                sides.append(finish(*UNITS[-1]))
                for g in sides:
                    for _ in g:
                        yield

            def projects():
                for b in range(NB):
                    for j, step in enumerate(project(b)):
                        yield step
                        due = (b - 1) * TPB * NG + PROJECT_FIRST + PROJECT_EVERY * j
                        while b and mixing["step"] < due and not mixing["blocked"]:
                            yield BLOCKED

            alternate((mixer(), 1), (projects(), 2))
            barrier()

        with ExitStack() as st:
            ssm_mixer(st)

        logit = sb(top, "logit", [P, NT, NE])
        sel = [sb(top, f"sel{i}", [P, NT, NE]) for i in range(3)]
        weight = sb(top, "weight", [P, NT, NE])
        value = sb(top, "value", [P, 2, 2, NT])

        w_gu = sb(top, "w_gu", [P, WR, KD, 2 * EH])
        w_dn = sb(top, "w_dn", [P, WR, KD, DIM])
        before = sb(top, "before", [P, P])
        token_id = sb(top, "token_id", [P, NT])
        tile_id = sb(top, "tile_id", [P, MT])
        ones = sb(top, "m_ones", [P, P])
        row_id = sb(top, "row_id", [P, P])
        load_m = Load(semaphore("load_m"))
        load_e = [Load(semaphore(f"load_e{i}")) for i in range(4)]
        gu_dram = A["c_gatingT"].rearrange("e (k p) n -> p e k n", p=P)
        dn_dram = A["L0_ffn_linear"].rearrange("e (k p) n -> p e k n", p=P)
        expert_loads = {}

        def load_first_expert():
            for dst, src in [
                (row_id[:, :], A["c_row_id"]),
                (before[:, :], A["c_before"]),
                (token_id[:, :], A["c_token_id"]),
                (tile_id[:, :], A["c_tile_id"]),
            ]:
                expert_loads["constants"] = load_m.start(Y, dst, src)
            load_e[0].start(Y, w_gu[:, 0, :, :], gu_dram[:, 0, :, :])
            expert_loads["weights 0"] = load_e[0].start(Y, w_dn[:, 0, :, :], dn_dram[:, 0, :, :])

        def cross_attention(st):
            bank = lambda name, shape=[P, 512], dt=F32: st.enter_context(nc.psum_tensor(name, shape, dt))
            max_ps = Ring([bank(f"max_ps{i}") for i in range(3)])
            score_ps = Ring([bank(f"score_ps{i}") for i in range(3)])
            pv_ps = Ring([bank(f"pv_ps{i}") for i in range(1)])
            turn_ps = Ring([bank(f"turn_ps{i}") for i in range(1)])

            NPR = QH // 2
            PARTS = 3 * DH
            xn = sb(st, "a_xn", [P, DIM])
            stats = sb(st, "a_stats", [P, 24])
            q_st = sb(st, "q_st", [P, QH, SLOT], F16)
            k_st = sb(st, "k_st", [P, KVH, 2, SLOT], F16)
            ctx = [sb(st, f"ctx{i}", [P, TPB, KVH, DH]) for i in range(2)]
            v_aug = [sb(st, f"v_aug{i}", [P, TPB, KVH, 32]) for i in range(2)]
            qT = [sb(st, f"qT{i}", [P, NPR, L], F16) for i in range(2)]
            kT = [sb(st, f"kT{i}", [P, KVH, L], F16) for i in range(2)]
            maxes = sb(st, "maxes", [P, TPB, QH])
            nmax = sb(st, "nmax", [P, TPB, QH], F16)
            nmaxT = [sb(st, f"nmaxT{i}", [QH, L], F16) for i in range(2)]
            prob = Ring([sb(st, f"prob{i}", [P, 512]) for i in range(8)])
            pv = Ring([sb(st, f"pv{i}", [P, 512]) for i in range(2)])
            recip = sb(st, "recip", [P, 4, 4])
            o_tok = [sb(st, f"o_tok{i}", [P, TPB, DIM]) for i in range(2)]

            load_ctx = Load(semaphore("load_ctx"))
            load_max = Load(semaphore("load_max"))
            for i in range(2):
                V.do(lambda e, i=i: e.memset(v_aug[i][:, :, :, :], 0.0))
            m = V.do(lambda e: e.memset(k_st[:, :, :, :], 0.0))
            m2 = V.do(lambda e: e.memset(q_st[:, :, :], 0.0))
            V.wait(m, m2)
            for i in range(2):
                V.do(lambda e, i=i: e.memset(v_aug[i][:, :, :, DH:DH + 1], 1.0))
            init = V.do(lambda e: e.memset(k_st[:, :, :, PARTS:PARTS + 1], 1.0))
            for e in (T, S, V, G):
                e.wait(init)
            made = {}
            last = {}

            def heads_in(b):
                par = b % 2
                Y.wait(last.get(("ctx", par)))
                cm = load_ctx.start(Y, ctx[par][:, :, :, :].rearrange("p t k d -> p t (k d)"), ctx_rows[:, b * TPB:(b + 1) * TPB, :])
                Y.wait(cm)
                if b == 1:
                    load_first_expert()
                for nm in norm_factors(b, stats):
                    yield
                if b >= 2:
                    while ("attended", b - 2) not in made:
                        yield BLOCKED
                for t in range(TPB):
                    kv = ctx[par][:, t, :, :]
                    both = kv.rearrange("p k (o d) -> p k o d", o=1).to_broadcast([P, KVH, 2, DH])
                    S.wait(cm, last.get("k_st"))
                    S.do(lambda e, both=both: e.activation(k_st[:, :, :, 0:DH], both, ACT.Copy))
                    m = S.do(lambda e, both=both: e.activation(k_st[:, :, :, 2 * DH:3 * DH], both, ACT.Copy))
                    yield
                    V.wait(cm, m)
                    m = V.do(lambda e, both=both: e.tensor_tensor(k_st[:, :, :, DH:2 * DH], both, k_st[:, :, :, 0:DH], ALU.subtract))
                    G.wait(cm, last.get(("v", par)) if t == 0 else None)
                    vm = G.do(lambda e, kv=kv, t=t: e.tensor_copy(v_aug[par][:, t, :, 0:DH], kv))
                    yield
                    while turn_ps.busy():
                        yield
                    n, ps = turn_ps.take(T)
                    T.wait(m)
                    ps16 = ps[:, :].bitcast(F16)
                    for k in range(KVH):
                        f = lambda e, k=k, ps16=ps16: e.transpose(ps16[:, k * P:(k + 1) * P], k_st[:, k, :, :].rearrange("p a s -> p (a s)"), ident16[:, :])
                        T.run(f) if k < KVH - 1 else None
                    last["k_st"] = m = T.do(f)
                    yield
                    V.wait(m, last.get(("kT", par)) if t == 0 else None)
                    km = V.do(lambda e, ps16=ps16, t=t: e.tensor_copy(kT[par][:, :, t * P:(t + 1) * P], ps16.rearrange("p (k j) -> p k j", j=P)))
                    turn_ps.release(n, km)
                    yield
                last["ctx", par] = vm
                made["v", b], made["kT", b] = vm, km
                q_marks = [None, None]
                for t in range(TPB):
                    tile = b * TPB + t
                    V.wait(nm, last.get("xn"))
                    m = V.do(lambda e, t=t, tile=tile: normalise(e, xn[:, :], tile, stats, t))
                    q = xn[:, :].rearrange("p (h d) -> p h d", d=DH)
                    yield
                    S.wait(m, last.get("q_st"))
                    m = S.do(lambda e, q=q: e.activation(q_st[:, :, 0:DH], q, ACT.Copy))
                    yield
                    V.wait(m)
                    last["xn"] = m = V.do(lambda e, q=q: e.tensor_tensor(q_st[:, :, 2 * DH:3 * DH], q, q_st[:, :, 0:DH], ALU.subtract))
                    G.wait(m, last.get("q_st"))
                    gm = G.do(lambda e: e.tensor_copy(q_st[:, :, DH:2 * DH], q_st[:, :, 0:DH]))
                    yield
                    yield
                    T.wait(m, gm)
                    for half in range(2):
                        while turn_ps.busy():
                            yield
                        n, ps = turn_ps.take(T)
                        ps16 = ps[:, :].bitcast(F16)
                        for k in range(NPR // 2):
                            pr = half * NPR // 2 + k
                            f = lambda e, k=k, pr=pr, ps16=ps16: e.transpose(ps16[:, k * P:(k + 1) * P], q_st[:, 2 * pr:2 * pr + 2, :].rearrange("p a s -> p (a s)"), ident16[:, :])
                            T.run(f) if k < NPR // 2 - 1 else None
                        last["q_st"] = m = T.do(f)
                        yield
                        E_ = S if half else V
                        out_ = qT[par][:, half * NPR // 2:(half + 1) * NPR // 2, t * P:(t + 1) * P]
                        in_ = ps16.rearrange("p (k j) -> p k j", j=P)
                        E_.wait(m, last.get(("qT", par)) if t == 0 else None)
                        qm = E_.do((lambda e, o=out_, i=in_: e.activation(o, i, ACT.Copy)) if half else (lambda e, o=out_, i=in_: e.tensor_copy(o, i)))
                        turn_ps.release(n, qm)
                        q_marks[half] = qm
                        yield
                T.wait(km, *q_marks)

                def max_scores(tk, at):
                    t, k, odd = tk
                    base = SLOT * odd
                    at["n"], at["ps"] = n, ps = max_ps.take(T)
                    for hh in range(2):
                        f = lambda e, hh=hh: e.matmul(
                            ps[:, hh * L:(hh + 1) * L], qT[par][base:base + PARTS, 2 * k + hh, t * P:(t + 1) * P], kT[par][base:base + PARTS, k, :], start=True, stop=True)
                        T.run(f) if hh < 1 else None
                    at["m"] = T.do(f)

                def max_reduce(tk, at):
                    t, k, odd = tk
                    ps, first = at["ps"], 4 * k + 2 * odd
                    V.wait(at["m"])
                    m = V.do(lambda e: e.reduce_max(maxes[:, t, first:first + 2], ps[:, :].rearrange("p (h t) -> p h t", h=2), AX.X))
                    max_ps.release(at["n"], m)
                    made["maxes"] = m

                pairs = [(t, k, odd) for t in range(TPB) for k in range(KVH) for odd in range(2)]
                for step, _ in enumerate(pipeline(pairs, [max_scores, max_reduce])):
                    if step % 2 == 0:
                        yield
                V.wait(made["maxes"], last.get("nmax"))
                for t in range(TPB):
                    for odd in range(2):
                        m = V.do(lambda e, t=t, odd=odd: e.tensor_scalar(nmax[:, t, odd * NPR:(odd + 1) * NPR].rearrange("p (k hh) -> p k hh", hh=2), maxes[:, t, :].rearrange("p (k odd hh) -> p k odd hh", odd=2, hh=2)[:, :, odd, :], -1.0, None, ALU.mult))
                yield
                while turn_ps.busy():
                    yield
                n, ps = turn_ps.take(T)
                ps16 = ps[:, :].bitcast(F16)
                T.wait(m)
                T.run(lambda e, ps16=ps16: e.transpose(ps16[0:QH, 0:P], nmax[:, 0, :], ident16[:, :]))
                last["nmax"] = m = T.do(lambda e, ps16=ps16: e.transpose(ps16[0:QH, P:2 * P], nmax[:, 1, :], ident16[:, :]))
                yield
                V.wait(m, last.get(("nmaxT", par)))
                m = V.do(lambda e, ps16=ps16: e.tensor_copy(nmaxT[par][:, :], ps16[0:QH, 0:L]))
                turn_ps.release(n, m)
                Y.wait(m)
                for odd in range(2):
                    row = SLOT * odd + PARTS
                    m = load_max.start(Y, qT[par][row:row + 1, :, :], nmaxT[par][odd * NPR:(odd + 1) * NPR, :])
                Y.wait(m)
                last["nmaxT", par] = m
                made["qT", b] = m
                yield

            ITEMS = [(b, kh, odd, t, quad) for b in range(NB) for kh in range(2) for odd in range(2) for t in range(TPB) for quad in range(4)]
            held = []

            def score(item, at):
                b, kh, odd, t, quad = item
                par, base, k = b % 2, SLOT * odd, 4 * kh + quad
                at["n"], at["ps"] = n, ps = score_ps.take(T)
                T.wait(made["qT", b], made["v", b], made["kT", b])
                at["m"] = T.do(lambda e: e.matmul(ps[:, :], kT[par][base:base + PARTS + 1, k, t * P:(t + 1) * P],
                                                  qT[par][base:base + PARTS + 1, 2 * k:2 * k + 2, :], start=True, stop=True))
                last["kT", par] = last["qT", par] = at["m"]

            def exponent(item, at):
                ps = at["ps"]
                at["r"], at["buf"] = r, buf = prob.take(S)
                S.wait(at["m"])
                at["m"] = S.do(lambda e: e.activation(buf[:, :], ps[:, :], ACT.Exp, scale=DH ** -0.5))
                score_ps.release(at["n"], at["m"])
                held.append((item, at))

            pv_bank = {}

            def product(item, at):
                b, kh, odd, t, quad = item
                if quad != 3:
                    return
                par = b % 2
                if t == 0:
                    pv_bank["now"] = pv_ps.take(T)
                vn, vps = pv_bank["now"]
                four = [held.pop(0)[1] for _ in range(4)]
                T.wait(four[3]["m"])
                for q, x in enumerate(four):
                    f = lambda e, q=q, buf=x["buf"]: e.matmul(
                        vps[32 * q:32 * q + 32, :], v_aug[par][:, t, 4 * kh + q, :], buf[:, :],
                        start=(t == 0), stop=(t == TPB - 1), tile_position=(0, 32 * q))
                    T.run(f) if q < 3 else None
                m = T.do(f)
                for x in four:
                    prob.release(x["r"], m)
                last["v", par] = m
                if t == TPB - 1:
                    sides.append(weighted(b, kh, odd, vn, vps, m))

            def weighted(b, kh, odd, vn, vps, m):
                par = b % 2
                r, pbuf = pv.take(S)
                S.wait(m)
                m = S.do(lambda e: e.activation(pbuf[:, :], vps[:, :], ACT.Copy))
                pv_ps.release(vn, m)
                yield
                yield
                while turn_ps.busy():
                    yield
                n, ps = turn_ps.take(T)
                T.wait(m)
                for i in range(4):
                    f = lambda e, i=i: e.transpose(ps[:, i * P:(i + 1) * P], pbuf[:, i * P:(i + 1) * P], ident[:, :])
                    T.run(f) if i < 3 else None
                m = T.do(f)
                pv.release(r, m)
                yield
                V.wait(m, last.get("recip"))
                m = V.do(lambda e: e.reciprocal(recip[:, :, :], ps[:, :].rearrange("p (b q w) -> p b q w", b=4, q=4)[:, :, :, DH]))
                V.wait(m, last.get(("o_tok", par)))
                for t in range(TPB):
                    cols = o_tok[par][:, t, :].rearrange("p (kh q hh odd d) -> p kh q hh odd d", kh=2, q=4, hh=2, odd=2)[:, kh, :, :, odd, :]
                    for hh in range(2):
                        i0 = ps[:, (hh * TPB + t) * P:(hh * TPB + t + 1) * P].rearrange("p (q w) -> p q w", q=4)[:, :, 0:DH]
                        i1 = recip[:, hh * TPB + t, :].rearrange("p (q o) -> p q o", o=1).to_broadcast([P, 4, DH])
                        m = V.do(lambda e, o=cols[:, :, hh, :], i0=i0, i1=i1: e.tensor_tensor(o, i0, i1, ALU.mult))
                last["recip"] = m
                turn_ps.release(n, m)
                yield
                if kh == 1 and odd == 1:
                    G.wait(m)
                    for t in range(TPB):
                        tile = b * TPB + t
                        gm = G.do(lambda e, t=t, tile=tile: e.tensor_tensor(x_sb[:, tile, :], x_sb[:, tile, :], o_tok[par][:, t, :], ALU.add))
                        x_ready[tile] = gm
                    last["o_tok", par] = gm
                    made["attended", b] = gm
                yield

            sides = []

            def attention():
                main = pipeline(ITEMS, [score, None, exponent, None, None, product])
                for s in range(len(ITEMS) + 5):
                    if s < len(ITEMS):
                        while ("qT", ITEMS[s][0]) not in made:
                            advance(sides)
                            yield BLOCKED
                    next(main)
                    advance(sides)
                    yield
                while sides:
                    advance(sides)
                    yield

            def heads():
                for b in range(NB):
                    yield from heads_in(b)

            def routes():
                for b in range(NB):
                    while ("attended", b) not in made:
                        yield BLOCKED
                    yield from together(*[route_in(b)] + ([choose(b - 1)] if b else []))
                yield from choose(NB - 1)

            r_xn = [sb(st, f"r_xn{i}", [P, DIM]) for i in range(2)]
            r_xnT = sb(st, "r_xnT", [P, KD, P])
            r_stats = sb(st, "r_stats", [P, 24])
            w_router = sb(st, "w_router", [P, KD, NE])
            s_router = sb(st, "s_router", [P, KD])
            lower = sb(st, "lower", [P, NE, NE])
            e_scale = sb(st, "e_scale", [P, NE])
            mean_sqs = [sb(st, f"mean_sq{i}", [P, 4, TPB]) for i in range(2)]
            larger = sb(st, "larger", [P, TPB, NE, NE])
            equal = sb(st, "equal", [P, TPB, NE, NE])
            rank = sb(st, "rank", [P, TPB, NE])
            junk = sb(st, "junk", [P, DIM])
            r_free = dict(xn=[(), ()], xnT=None, junk=None)
            for dst, src in [
                (w_router[:, :, :], A["L0_ffn_router_logits"].rearrange("(k p) e -> p k e", p=P)),
                (s_router[:, :], A["c_router_scale"]),
                (lower[:, :, :], A["c_lower"].rearrange("p (a b) -> p a b", a=NE)),
                (e_scale[:, :], A["L0_ffn_per_expert_scale"].rearrange("(o e) -> o e", o=1).to_broadcast([P, NE])),
            ]:
                r_ready = load_r.start(Y, dst, src)
            V.wait(r_ready)
            for k in range(KD):
                wr_mark = V.do(lambda e, k=k: e.tensor_scalar(w_router[:, k, :], w_router[:, k, :], s_router[:, k:k + 1], None, ALU.mult))

            def route_in(b):
                for nm in norm_factors(b, r_stats):
                    yield
                for t in range(TPB):
                    tile = b * TPB + t
                    i = tile % 2
                    V.wait(nm, *r_free["xn"][i])
                    m = V.do(lambda e, i=i, t=t, tile=tile: normalise(e, r_xn[i][:, :], tile, r_stats, t))
                    Y.wait(m)
                    kept = store_tokens[i].start(Y, tokens[tile * P:(tile + 1) * P, :], r_xn[i][:, :])
                    if tile == NT - 1:
                        kept = store_tokens[i].start(Y, tokens[NT * P:(NT + 1) * P, :], r_xn[i][:, :])
                    yield
                    S.wait(m, r_free["junk"])
                    jm = S.do(lambda e, i=i, t=t: e.activation(junk[:, :], r_xn[i][:, :], ACT.Square, accum_out=mean_sqs[b % 2][:, 0, t:t + 1]))
                    r_free["junk"] = jm
                    while turn_ps.busy():
                        yield
                    n, ps = turn_ps.take(T)
                    T.wait(m)
                    for k in range(KD):
                        f = lambda e, k=k, i=i, ps=ps: e.transpose(ps[:, k * P:(k + 1) * P], r_xn[i][:, k * P:(k + 1) * P], ident[:, :])
                        T.run(f) if k < KD - 1 else None
                    m = T.do(f)
                    r_free["xn"][i] = (m, jm, kept)
                    yield
                    S.wait(m, r_free["xnT"])
                    xm = S.do(lambda e, ps=ps: e.activation(r_xnT[:, :, :], ps[:, :].rearrange("p (k j) -> p k j", k=KD), ACT.Copy))
                    turn_ps.release(n, xm)
                    yield
                    while turn_ps.busy():
                        yield
                    n, ps = turn_ps.take(T)
                    T.wait(xm, wr_mark)
                    for k in range(KD):
                        f = lambda e, k=k, ps=ps: e.matmul(ps[:, 0:NE], r_xnT[:, k, :], w_router[:, k, :], start=(k == 0), stop=(k == KD - 1))
                        T.run(f) if k < KD - 1 else None
                    m = T.do(f)
                    r_free["xnT"] = m
                    yield
                    V.wait(m)
                    m = V.do(lambda e, tile=tile, ps=ps: e.tensor_copy(logit[:, tile, :], ps[:, 0:NE]))
                    turn_ps.release(n, m)
                    yield
                made["router products", b] = (m, jm)

            def choose(b):
                step = lambda f: V.wait(V.do(f))
                ts = slice(b * TPB, (b + 1) * TPB)
                mean_sq = mean_sqs[b % 2]
                V.wait(*made["router products", b])
                m = V.do(lambda e: e.tensor_scalar(mean_sq[:, 0, :], mean_sq[:, 0, :], 1.0 / DIM, ROUTER_EPS, ALU.mult, ALU.add))
                for m in rsqrt(mean_sq[:, 0, :], mean_sq[:, 1, :], mean_sq[:, 2, :], m):
                    yield
                V.wait(m)
                step(lambda e: e.tensor_scalar(mean_sq[:, 1, :], mean_sq[:, 1, :], float(np.float32(DIM) ** np.float32(-0.5)), None, ALU.mult))
                over_e = lambda a: a.rearrange("p (t o) -> p t o", o=1).to_broadcast([P, TPB, NE])
                step(lambda e: e.tensor_tensor(logit[:, ts, :], logit[:, ts, :], over_e(mean_sq[:, 1, :]), ALU.mult))
                step(lambda e: e.reduce_max(mean_sq[:, 3, :], logit[:, ts, :], AX.X))
                m = V.do(lambda e: e.tensor_tensor(weight[:, ts, :], logit[:, ts, :], over_e(mean_sq[:, 3, :]), ALU.subtract))
                S.wait(m)
                em = S.do(lambda e: e.activation(weight[:, ts, :], weight[:, ts, :], ACT.Exp))
                yield
                la = logit[:, ts, :].rearrange("p t (e o) -> p t e o", o=1).to_broadcast([P, TPB, NE, NE])
                lb = logit[:, ts, :].rearrange("p t (o e) -> p t o e", o=1).to_broadcast([P, TPB, NE, NE])
                low = lower[:, :, :].rearrange("p (o a) b -> p o a b", o=1).to_broadcast([P, TPB, NE, NE])
                V.do(lambda e: e.tensor_tensor(larger[:, :, :, :], lb, la, ALU.is_gt))
                step(lambda e: e.tensor_tensor(equal[:, :, :, :], lb, la, ALU.is_equal))
                step(lambda e: e.tensor_tensor(equal[:, :, :, :], equal[:, :, :, :], low, ALU.mult))
                step(lambda e: e.tensor_tensor(larger[:, :, :, :], larger[:, :, :, :], equal[:, :, :, :], ALU.add))
                step(lambda e: e.reduce_sum(rank[:, :, :], larger[:, :, :, :], AX.X))
                V.do(lambda e: e.tensor_scalar(sel[0][:, ts, :], rank[:, :, :], 0.0, None, ALU.is_equal))
                V.do(lambda e: e.tensor_scalar(sel[1][:, ts, :], rank[:, :, :], 1.0, None, ALU.is_equal))
                step(lambda e: e.tensor_scalar(sel[2][:, ts, :], rank[:, :, :], 2.0, None, ALU.is_lt))
                yield
                V.wait(em)
                step(lambda e: e.tensor_tensor(weight[:, ts, :], weight[:, ts, :], sel[2][:, ts, :], ALU.mult))
                step(lambda e: e.reduce_sum(mean_sq[:, 3, :], weight[:, ts, :], AX.X))
                step(lambda e: e.reciprocal(mean_sq[:, 3, :], mean_sq[:, 3, :]))
                step(lambda e: e.tensor_tensor(weight[:, ts, :], weight[:, ts, :], over_e(mean_sq[:, 3, :]), ALU.mult))
                step(lambda e: e.tensor_tensor(weight[:, ts, :], weight[:, ts, :], e_scale[:, :].rearrange("p (o e) -> p o e", o=1).to_broadcast([P, TPB, NE]), ALU.mult))
                for c in range(2):
                    step(lambda e, c=c: e.tensor_tensor(rank[:, :, :], sel[c][:, ts, :], weight[:, ts, :], ALU.mult))
                    step(lambda e, c=c: e.reduce_sum(value[:, 1, c, ts], rank[:, :, :], AX.X))
                yield

            alternate((attention(), 32 * NB), (heads(), 40 * NB), (routes(), 12 * NB))
            barrier()

        with ExitStack() as st:
            cross_attention(st)

        def experts(st):
            bank = lambda name, shape=[P, 512], dt=F32: st.enter_context(nc.psum_tensor(name, shape, dt))
            gate_ps = Ring([bank("gate_ps0"), bank("gate_ps1")])
            up_ps = Ring([bank("up_ps0"), bank("up_ps1")])
            turn_ps = Ring([bank("mturn_ps0"), bank("mturn_ps1")])
            down_ps = Ring([bank("down_ps0"), bank("down_ps1")])
            total = sb(st, "total", [P, NT, NE])
            upto = sb(st, "upto", [P, NT, NE])
            counts = sb(st, "counts", [P, 4, NE])
            counts_i = sb(st, "counts_i", [P, 2, NE], mybir.dt.int32)
            slot_f = sb(st, "slot_f", [P, 2, NT])
            slot_i = sb(st, "slot_i", [P, 2, 2, NT], mybir.dt.int32)
            tile_of = sb(st, "tile_of", [P, 2, NT])
            place_of = sb(st, "place_of", [P, 2, NT])
            own = sb(st, "own", [P, NT, MT])
            own_values = [sb(st, f"own_value{i}", [P, NT, 2, MT]) for i in range(2)]
            places = Ring([sb(st, f"place{i}", [P, P]) for i in range(12)])
            owner_f = sb(st, "owner_f", [P, 3, MT])
            owner = sb(st, "owner", [P, 3, MT], mybir.dt.int32)
            owned = sb(st, "owned", [P, MT, NE])
            ids = sb(st, "ids", [P, MT], mybir.dt.uint32)
            row_w = sb(st, "row_w", [P, MT])
            xg = Ring([sb(st, f"xg{i}", [P, DIM]) for i in range(3)])
            xgT = [sb(st, f"xgT{i}", [P, KD, P]) for i in range(2)]
            gelu = [sb(st, f"gelu{i}", [P, EH]) for i in range(2)]
            act = [sb(st, f"act{i}", [P, EH]) for i in range(2)]
            actT = [sb(st, f"actT{i}", [P, KD, P]) for i in range(2)]
            y_out = Ring([sb(st, f"y_out{i}", [P, DIM]) for i in range(3)])
            out_init = Load(semaphore("out_init"))
            gather = [Load(semaphore(f"gather{i}")) for i in range(3)]
            scatter = Load(semaphore("scatter"))

            for t in range(NT):
                Y.wait(x_ready[t])
                out_init.start(Y, out[t * P:(t + 1) * P, :], x_sb[:, t, :])
            residual_out = out_init.start(Y, out[NT * P:(NT + 1) * P, :], x_sb[:, 0, :])

            for e in (V, G, T):
                e.wait(expert_loads["constants"])
            weights_ready = [expert_loads["weights 0"]]
            m = V.do(lambda e: e.memset(ones[:, :], 1.0))

            def step(f):
                m = V.do(f)
                V.wait(m)
                return m

            over_t = lambda a: a.rearrange("p (o e) -> p o e", o=1).to_broadcast([P, NT, NE])
            n1, ps1 = gate_ps.take(T)
            n2, ps2 = up_ps.take(T)
            T.wait(m)
            both = sel[2][:, :, :].rearrange("p t e -> p (t e)")
            T.run(lambda e: e.matmul(ps2[:, 0:NT * NE], ones[:, :], both, start=True, stop=True))
            pm = T.do(lambda e: e.matmul(ps1[:, 0:NT * NE], before[:, :], both, start=True, stop=True))
            V.wait(pm)
            step(lambda e: e.tensor_copy(total[:, :, :].rearrange("p t e -> p (t e)"), ps2[:, 0:NT * NE]))
            for x in range(NE):
                m = V.do(lambda e, x=x: e.tensor_tensor_scan(upto[:, :, x], ones[:, 0:NT], total[:, :, x], 0.0, ALU.mult, ALU.add))
            V.wait(m)
            step(lambda e: e.tensor_scalar(counts[:, 3, :], upto[:, NT - 1, :], float(P - 1), None, ALU.add))
            step(lambda e: e.tensor_copy(counts_i[:, 0, :], counts[:, 3, :]))
            step(lambda e: e.tensor_scalar(counts_i[:, 1, :], counts_i[:, 0, :], P.bit_length() - 1, None, ALU.arith_shift_right))
            step(lambda e: e.tensor_copy(counts[:, 3, :], counts_i[:, 1, :]))
            step(lambda e: e.tensor_scalar(counts[:, 0, :], counts[:, 3, :], 1.0, None, ALU.max))
            step(lambda e: e.tensor_tensor_scan(counts[:, 1, :], ones[:, 0:NE], counts[:, 0, :], 0.0, ALU.mult, ALU.add))
            step(lambda e: e.tensor_tensor(counts[:, 2, :], counts[:, 1, :], counts[:, 0, :], ALU.subtract))
            bases = counts[:, 2, :].rearrange("p (o e) -> p o e", o=1).to_broadcast([P, MT, NE])
            tiles = tile_id[:, :].rearrange("p (i o) -> p i o", o=1).to_broadcast([P, MT, NE])
            step(lambda e: e.tensor_tensor(owned[:, :, :], bases, tiles, ALU.is_le))
            step(lambda e: e.reduce_sum(owner_f[:, 2, :], owned[:, :, :], AX.X))
            step(lambda e: e.tensor_scalar(owner_f[:, 0, :], owner_f[:, 2, :], 1.0, None, ALU.subtract))
            step(lambda e: e.tensor_scalar(owner_f[:, 1, :], owner_f[:, 0, :], float(WR), float(-WR), ALU.is_ge, ALU.mult))
            step(lambda e: e.tensor_tensor(owner_f[:, 1, :], owner_f[:, 1, :], owner_f[:, 0, :], ALU.add))
            step(lambda e: e.tensor_scalar(owner_f[:, 2, :], owner_f[:, 0, :], float(2 * WR), float(-WR), ALU.is_ge, ALU.mult))
            step(lambda e: e.tensor_tensor(owner_f[:, 1, :], owner_f[:, 1, :], owner_f[:, 2, :], ALU.add))
            step(lambda e: e.tensor_tensor(owner_f[:, 2, 1:MT], owner_f[:, 0, 1:MT], owner_f[:, 0, 0:MT - 1], ALU.subtract))
            owner_mark = V.do(lambda e: e.tensor_copy(owner[:, :, :], owner_f[:, :, :]))
            step(lambda e: e.tensor_tensor(upto[:, :, :], upto[:, :, :], total[:, :, :], ALU.subtract))
            step(lambda e: e.tensor_tensor(upto[:, :, :].rearrange("p t e -> p (t e)"), upto[:, :, :].rearrange("p t e -> p (t e)"), ps1[:, 0:NT * NE], ALU.add))
            step(lambda e: e.tensor_scalar(counts[:, 3, :], counts[:, 2, :], float(P), None, ALU.mult))
            step(lambda e: e.tensor_tensor(upto[:, :, :], upto[:, :, :], over_t(counts[:, 3, :]), ALU.add))
            for c in range(2):
                step(lambda e, c=c: e.tensor_tensor(total[:, :, :], sel[c][:, :, :], upto[:, :, :], ALU.mult))
                step(lambda e, c=c: e.reduce_sum(slot_f[:, c, :], total[:, :, :], AX.X))
            step(lambda e: e.tensor_copy(slot_i[:, 0, :, :], slot_f[:, :, :]))
            step(lambda e: e.tensor_scalar(slot_i[:, 1, :, :], slot_i[:, 0, :, :], P.bit_length() - 1, None, ALU.arith_shift_right))
            step(lambda e: e.tensor_copy(tile_of[:, :, :], slot_i[:, 1, :, :]))
            step(lambda e: e.scalar_tensor_tensor(place_of[:, :, :], tile_of[:, :, :], -float(P), slot_f[:, :, :], ALU.mult, ALU.add))
            placed = step(lambda e: e.scalar_tensor_tensor(
                value[:, 0, :, :], place_of[:, :, :], -1.0, token_id[:, :].rearrange("p (o t) -> p o t", o=1).to_broadcast([P, 2, NT]), ALU.mult, ALU.add))
            step(lambda e: e.tensor_scalar(value[:, 0, :, :], value[:, 0, :, :], float(NT * P), None, ALU.subtract))
            pn, pps = turn_ps.take(T)
            wide_t = lambda a: a.rearrange("p (t i) -> p t i", i=1).to_broadcast([P, NT, MT])
            for c in range(2):
                own_value = own_values[c]
                step(lambda e, c=c: e.tensor_tensor(own[:, :, :], tile_id[:, :].rearrange("p (o i) -> p o i", o=1).to_broadcast([P, NT, MT]), wide_t(tile_of[:, c, :]), ALU.is_equal))
                for kind in range(2):
                    m = V.do(lambda e, c=c, kind=kind, o=own_value: e.tensor_tensor(o[:, :, kind, :], own[:, :, :], wide_t(value[:, kind, c, :]), ALU.mult))
                for t in range(NT):
                    E_ = G if t % 3 == 2 else V
                    n, at_place = places.take(E_)
                    E_.wait(placed)
                    pm = E_.do(lambda e, c=c, t=t, o=at_place: e.tensor_scalar(o[:, :], row_id[:, :], place_of[:, c, t:t + 1], None, ALU.is_equal))
                    T.wait(pm, m)
                    f = lambda e, c=c, t=t, w=at_place, v=own_value: e.matmul(pps[:, 0:2 * MT], w[:, :], v[:, t, :, :], start=(c == 0 and t == 0), stop=(c == 1 and t == NT - 1))
                    used = T.do(f)
                    places.release(n, used)
            V.wait(used)
            ids_mark = V.do(lambda e: e.tensor_scalar(ids[:, :], pps[:, 0:MT], token_id[:, 0:1], float(NT * P), ALU.add, ALU.add))
            row_w_mark = V.do(lambda e: e.tensor_copy(row_w[:, :], pps[:, MT:2 * MT]))
            V.wait(row_w_mark)
            turn_ps.release(pn, row_w_mark)
            gate_ps.release(n1, row_w_mark)
            up_ps.release(n2, row_w_mark)

            fr = dict(xgT=[None, None], gelu=[None, None], act=[None, None], actT=[None, None])
            gathered, place, done_tile, act_mark = [], {}, [], {}

            def fetch(i):
                n, buf = xg.take(G)
                G.wait(ids_mark, *[(x.sem, x.count) for x in store_tokens])
                s = gather[n]
                s.count += 16
                G.run(lambda e: e.indirect_dma_start(out=buf[:, :], out_offset=None, in_=tokens,
                                                     in_offset=bass.IndirectOffsetOnAxis(ap=ids[:, i:i + 1], axis=0)).then_inc(s.sem, 16))
                gathered.append((n, buf, (s.sem, s.count)))

            def load_weights(i):
                s = load_e[i % 4]
                Y.wait(owner_mark, done_tile[i - WR] if i >= WR else None)

                def go(e):
                    expert = e.value_load(owner[0:1, 0, i:i + 1], min_val=0, max_val=NE - 1)
                    at = e.value_load(owner[0:1, 1, i:i + 1], min_val=0, max_val=WR - 1)
                    new = e.value_load(owner[0:1, 2, i:i + 1], min_val=0, max_val=1)
                    e.dma_start(w_gu[:, bass.ds(at, 1), :, :], gu_dram[:, bass.ds(expert, 1), :, :], cond=new).then_inc(s.sem, 16)
                    e.dma_start(w_dn[:, bass.ds(at, 1), :, :], dn_dram[:, bass.ds(expert, 1), :, :], cond=new).then_inc(s.sem, 16)
                Y.run(go)
                s.count += 32
                weights_ready.append((s.sem, s.count))

            turned = {}

            def turn(i, buf, outs, mark, free, source_free):
                n, ps = turn_ps.take(T)
                T.wait(mark)
                for k in range(KD):
                    f = lambda e, k=k: e.transpose(ps[:, k * P:(k + 1) * P], buf[:, k * P:(k + 1) * P], ident[:, :])
                    T.run(f) if k < KD - 1 else None
                m = T.do(f)
                source_free(m)
                S.wait(m, free)
                m = S.do(lambda e: e.activation(outs[:, :, :], ps[:, :].rearrange("p (k j) -> p k j", k=KD), ACT.Copy))
                turn_ps.release(n, m)
                return m

            def turn_tokens(i):
                gn, buf, mark = gathered[i]
                turned["x", i] = turn(i, buf, xgT[i % 2], mark, fr["xgT"][i % 2], lambda m: xg.release(gn, m))

            def turn_act(i):
                j = i % 2
                turned["act", i] = turn(i, act[j], actT[j], act_mark[i], fr["actT"][j], lambda m: fr["act"].__setitem__(j, m))

            def up(i):
                j = i % 2
                n1, gps = gate_ps.take(T)
                n2, ups = up_ps.take(T)
                T.wait(turned["x", i], weights_ready[i], owner_mark)
                T.run(lambda e: place.__setitem__(i, e.value_load(owner[0:1, 1, i:i + 1], min_val=0, max_val=WR - 1)))
                for ps_, off in ((gps, 0), (ups, EH)):
                    for k in range(KD):
                        f = lambda e, k=k, ps_=ps_, off=off: e.matmul(ps_[:, :], xgT[j][:, k, :], w_gu[:, bass.ds(place[i], 1), k, off:off + EH].rearrange("p o n -> p (o n)"), start=(k == 0), stop=(k == KD - 1))
                        T.run(f) if k < KD - 1 else None
                    m = T.do(f)
                    if off == 0:
                        S.wait(m, fr["gelu"][j])
                        gm = S.do(lambda e: e.activation(gelu[j][:, :], gps[:, :], ACT.Gelu_apprx_tanh))
                        gate_ps.release(n1, gm)
                fr["xgT"][j] = m
                V.wait(m, gm, fr["act"][j])
                m = V.do(lambda e: e.tensor_tensor(act[j][:, :], gelu[j][:, :], ups[:, :], ALU.mult))
                up_ps.release(n2, m)
                fr["gelu"][j] = m
                act_mark[i] = m

            def down(i):
                j = i % 2
                dn, dps = down_ps.take(T)
                T.wait(turned["act", i])
                for k in range(KD):
                    f = lambda e, k=k: e.matmul(dps[:, :], actT[j][:, k, :], w_dn[:, bass.ds(place[i], 1), k, :].rearrange("p o n -> p (o n)"), start=(k == 0), stop=(k == KD - 1))
                    T.run(f) if k < KD - 1 else None
                m = T.do(f)
                fr["actT"][j] = m
                done_tile.append(m)
                yn, ybuf = y_out.take(V)
                V.wait(m)
                vm = V.do(lambda e: e.tensor_scalar(ybuf[:, :], dps[:, :], row_w[:, i:i + 1], None, ALU.mult))
                down_ps.release(dn, vm)
                G.wait(vm, residual_out, (scatter.sem, scatter.count) if scatter.count else None)
                scatter.count += 16
                G.run(lambda e: e.indirect_dma_start(
                    out=out, out_offset=bass.IndirectOffsetOnAxis(ap=ids[:, i:i + 1], axis=0),
                    in_=ybuf[:, :], in_offset=None, compute_op=ALU.add).then_inc(scatter.sem, 16))
                y_out.release(yn, (scatter.sem, scatter.count))

            fetch(0)
            fetch(1)
            for i in range(1, WR):
                load_weights(i)
            turn_tokens(0)
            for i in range(MT):
                if i + 2 < MT:
                    fetch(i + 2)
                up(i)
                if i + 1 < MT:
                    turn_tokens(i + 1)
                if i > 0:
                    down(i - 1)
                    if i - 1 + WR < MT:
                        load_weights(i - 1 + WR)
                turn_act(i)
            down(MT - 1)
            Y.wait((scatter.sem, scatter.count))

        with ExitStack() as st:
            experts(st)

        with nc.Block() as b:

            @b.tensor
            def _(e):
                for f in T.queue:
                    f(e)

            @b.vector
            def _(e):
                for f in V.queue:
                    f(e)

            @b.scalar
            def _(e):
                for f in S.queue:
                    f(e)

            @b.gpsimd
            def _(e):
                for f in G.queue:
                    f(e)

            @b.sync
            def _(e):
                for f in Y.queue:
                    f(e)


def shape_constants():
    j = np.arange(P)
    select = np.zeros((64, NG, P), np.float32)
    for part in range(3):
        for g in range(NG):
            select[part * NG + g, g, :] = 1.0
    sign = np.zeros((64, HG, P), np.float32)
    for part in range(3):
        for h in range(HG):
            sign[3 * NG + part * HG + h, h, :] = -1.0
    expand = np.zeros((NH, HID // 2), np.float32)
    for h in range(NH):
        expand[h, h % (NH // 2) * HP:(h % (NH // 2) + 1) * HP] = 1.0
    lower = (np.arange(NE)[None, :] < np.arange(NE)[:, None]).astype(np.float32).reshape(1, NE * NE)
    return {
        "c_ident": np.eye(P, dtype=np.float32),
        "c_causal": (j[:, None] <= j[None, :]).astype(np.float32),
        "c_select": select.reshape(64, NG * P),
        "c_head_sign": sign.reshape(64, HG * P),
        "c_expand": expand,
        "c_before": (j[:, None] < j[None, :]).astype(np.float32),
        "c_token_id": (np.arange(NT)[None, :] * P + j[:, None]).astype(np.float32),
        "c_tile_id": np.broadcast_to(np.arange(MT, dtype=np.float32), (P, MT)).copy(),
        "c_row_id": np.broadcast_to(j.astype(np.float32), (P, P)).copy(),
        "c_lower": np.broadcast_to(lower, (P, NE * NE)).copy(),
    }


def kernel(**inputs):
    import concourse.bacc as bacc
    from concourse.bass_utils import run_bass_kernel_spmd

    a = {k: np.asarray(v) for k, v in inputs.items()}
    arrays = {k: np.ascontiguousarray(a[k]) for k in (
        "x", "ctx_512", "L0_attn_conv_w", "L0_attn_dt_bias", "L0_attn_A_log",
        "L0_ffn_router_logits", "L0_ffn_linear", "L0_ffn_per_expert_scale")}
    columns = lambda v: np.ascontiguousarray(v.reshape(-1, P).T)
    arrays["c_norm_w"] = columns(a["L0_attn_norm_w"])
    arrays["c_router_scale"] = columns(a["L0_ffn_router_scale"])
    arrays["c_w_inT"] = np.ascontiguousarray(a["L0_attn_W_in"].T)
    arrays["c_w_outT"] = np.ascontiguousarray(a["L0_attn_W_out"].T)
    arrays["c_gatingT"] = np.ascontiguousarray(a["L0_ffn_gating_einsum"].transpose(0, 3, 1, 2).reshape(NE, DIM, 2 * EH))
    arrays["c_D_channels"] = columns(np.repeat(a["L0_attn_D"], HP))
    arrays.update(shape_constants())

    nc = bacc.Bacc("TRN2", target_bir_lowering=False, num_devices=1)
    feeds, aps = {}, {}
    for name, value in arrays.items():
        feeds[name + "_dram"] = value
        aps[name] = nc.dram_tensor(name + "_dram", value.shape, mybir.dt.from_np(value.dtype), kind="ExternalInput").ap()
    out = nc.dram_tensor("out_dram", ((NT + 1) * P, DIM), F32, kind="ExternalOutput").ap()
    layer_kernel(nc, aps, out)
    result = run_bass_kernel_spmd(nc, [feeds], core_ids=[0])
    return result.results[0]["out_dram"][:NT * P].reshape(NB, L, DIM)
```
